# Optimizing a Trainium2 kernel written in Bass

```python
import numpy as np
import jax
import jax.numpy as jnp

def _softmax(x, axis=-1):
    return jax.nn.softmax(x, axis=axis)

def _gelu(x):
    return jax.nn.gelu(x, approximate=True)

def _silu(x):
    return jax.nn.silu(x)

def _sigmoid(x):
    return jax.nn.sigmoid(x)

def _layernorm(x, axis=-1, eps=1e-05):
    m = jnp.mean(x, axis=axis, keepdims=True)
    v = jnp.var(x, axis=axis, keepdims=True)
    return (x - m) / jnp.sqrt(v + eps)

def _scatter_add(tgt, idx, src, axis=0):
    return tgt.at[idx].add(src)

def _segment_sum(src, seg, n):
    return jax.ops.segment_sum(src, seg, n)
kernel_name = 'mk_flamingo_gated_d2_seqx_r8_927d6c'

def setup_inputs(seed: int=0):
    np.random.seed(seed)
    _w = jnp.asarray

    def _rec_inputs():
        import jax
        import jax.numpy as jnp
        _rk = jax.random.key(seed)
        x = 7.22e-05 + 1 * jax.random.normal(jax.random.fold_in(_rk, 1), (2, 512, 128), jnp.float32)
        _lenS = 512 - jax.random.randint(jax.random.fold_in(_rk, 7), (2,), 0, max(1, 512 // 4) + 1, jnp.int32)
        _lenS2 = 154 - jax.random.randint(jax.random.fold_in(_rk, 8), (2,), 0, max(1, 154 // 4) + 1, jnp.int32)
        _ctx_1024P = jax.random.normal(jax.random.fold_in(_rk, 11), (2, 16, 128), jnp.float32)
        _ctx_1024c = jax.random.dirichlet(jax.random.fold_in(_rk, 511), 0.3 * jnp.ones((16,), jnp.float32), (2, 154))
        _ctx_1024t = jnp.einsum('bsk,bkd->bsd', _ctx_1024c, _ctx_1024P)
        _ctx_1024t = _ctx_1024t * jax.lax.rsqrt(jnp.mean(jnp.square(_ctx_1024t)) + 1e-12) * 0.953939
        ctx_1024 = -0.000514642 + 1.00011 * (_ctx_1024t + 0.3 * jax.random.normal(jax.random.fold_in(_rk, 611), (2, 154, 128), jnp.float32))
        _g = jax.random.normal(jax.random.fold_in(_rk, 9001), (2, 2), jnp.float32)
        _g = jnp.sign(_g) * jnp.maximum(jnp.abs(_g), 1.0) + (_g == 0) * 1.0
        g_xattn = _g[0]
        g_ffn = _g[1]
        return (x, ctx_1024, g_xattn, g_ffn)
    x, ctx_1024, g_xattn, g_ffn = _rec_inputs()

    def _L0_xattn_setup():
        import jax, jax.numpy as jnp
        import numpy as np
        H, NH, HD = (128, 16, 64)
        INNER = NH * HD
        EPS = 1e-05

        def layernorm(x, g, b):
            mu = jnp.mean(x, axis=-1, keepdims=True)
            var = jnp.var(x, axis=-1, keepdims=True)
            return (x - mu) * jax.lax.rsqrt(var + EPS) * g + b
        key = jax.random.key(seed)
        ks = jax.random.split(key, 10)
        B, N, M = (2, 512, 128)
        s = 1.0 / np.sqrt(H)
        return {'hidden_states': jax.random.normal(ks[0], (B, N, H), jnp.float32), 'encoder_hidden_states': jax.random.normal(ks[1], (B, M, H), jnp.float32), 'Wq': jax.random.normal(ks[2], (H, INNER), jnp.float32) * s, 'Wk': jax.random.normal(ks[3], (H, INNER), jnp.float32) * s, 'Wv': jax.random.normal(ks[4], (H, INNER), jnp.float32) * s, 'Wo': jax.random.normal(ks[5], (INNER, H), jnp.float32) * (1.0 / np.sqrt(INNER)), 'bo': jnp.zeros((H,), jnp.float32), 'q_gamma': jnp.ones((HD,), jnp.float32), 'q_beta': jnp.zeros((HD,), jnp.float32), 'k_gamma': jnp.ones((HD,), jnp.float32), 'k_beta': jnp.zeros((HD,), jnp.float32)}
    _L0_xattn_all = _L0_xattn_setup()
    _L0_xattn_in = {k: v for k, v in _L0_xattn_all.items() if k in ('Wq', 'Wk', 'Wv', 'Wo', 'bo', 'q_gamma', 'q_beta', 'k_gamma', 'k_beta')}
    del _L0_xattn_all

    def _L0_ffn_setup():
        import math
        import jax, jax.numpy as jnp
        import numpy as np
        D_MODEL = 128
        D_HIDDEN = 256
        N_EXPERTS = 8
        TOP_K = 2
        CAPACITY_FACTOR = 1.25

        def _moe_forward(x, w_router, w_gate, w_down):
            B, T, D = x.shape
            N = B * T
            xf = x.reshape(N, D)
            logits = xf.astype(jnp.float32) @ w_router.T
            gates = jax.nn.softmax(logits, axis=-1)
            topk_gates, topk_idx = jax.lax.top_k(gates, TOP_K)
            expert_mask = jax.nn.one_hot(topk_idx, N_EXPERTS, dtype=jnp.int32).sum(axis=1)
            capacity = math.ceil(N / N_EXPERTS * CAPACITY_FACTOR)
            position_in_expert = jnp.cumsum(expert_mask, axis=0) - 1
            expert_mask = expert_mask * (position_in_expert < capacity)
            keep = jnp.take_along_axis(expert_mask, topk_idx, axis=1) > 0
            topk_gates = topk_gates * keep
            topk_gates = topk_gates / (topk_gates.sum(axis=-1, keepdims=True) + 1e-06)
            hidden = jax.nn.silu(xf @ w_gate.T)
            combine = (topk_gates[:, :, None] * jax.nn.one_hot(topk_idx, N_EXPERTS, dtype=topk_gates.dtype)).sum(axis=1)
            y = jnp.zeros((N, D), dtype=x.dtype)
            for e in range(N_EXPERTS):
                y = y + combine[:, e:e + 1] * (hidden @ w_down[e].T)
            return y.reshape(B, T, D)
        key = jax.random.key(seed)
        k0, k1, k2, k3 = jax.random.split(key, 4)
        B, T = (2, 256)
        x = jax.random.normal(k0, (B, T, D_MODEL), dtype=jnp.float32)
        w_router = jax.random.normal(k1, (N_EXPERTS, D_MODEL), dtype=jnp.float32) * 0.02
        w_gate = jax.random.normal(k2, (D_HIDDEN, D_MODEL), dtype=jnp.float32) * 0.02
        w_down = jax.random.normal(k3, (N_EXPERTS, D_MODEL, D_HIDDEN), dtype=jnp.float32) * 0.02
        return {'x': x, 'w_router': w_router, 'w_gate': w_gate, 'w_down': w_down}
    _L0_ffn_all = _L0_ffn_setup()
    _L0_ffn_in = {k: v for k, v in _L0_ffn_all.items() if k in ('w_router', 'w_gate', 'w_down')}
    del _L0_ffn_all

    def _L1_xattn_setup():
        import jax, jax.numpy as jnp
        import numpy as np
        EMBED = 128
        HEADS = 16
        HEAD_DIM = EMBED // HEADS
        EXP_DIM = 2 * HEAD_DIM

        def _feature_map(x, fm_w, fm_b):
            z = jnp.einsum('nshd,ed->nshe', x, fm_w) + fm_b
            return jnp.concatenate([jnp.exp(z), jnp.exp(-z)], axis=-1)
        key = jax.random.key(seed)
        ks = jax.random.split(key, 7)
        N, S = (4, 256)
        values = jax.random.normal(ks[0], (N, S, EMBED), dtype=jnp.float32)
        keys_ = jax.random.normal(ks[1], (N, S, EMBED), dtype=jnp.float32)
        query = jax.random.normal(ks[2], (N, S, EMBED), dtype=jnp.float32)
        fm_w = jnp.eye(HEAD_DIM, dtype=jnp.float32) + 0.02 * jax.random.normal(ks[3], (HEAD_DIM, HEAD_DIM), dtype=jnp.float32)
        fm_b = 0.02 * jax.random.normal(ks[4], (HEAD_DIM,), dtype=jnp.float32)
        fc_w = jax.random.normal(ks[5], (EMBED, HEADS * EXP_DIM), dtype=jnp.float32) * (1.0 / np.sqrt(HEADS * EXP_DIM))
        fc_b = jnp.zeros((EMBED,), dtype=jnp.float32)
        return {'values': values, 'keys': keys_, 'query': query, 'fm_w': fm_w, 'fm_b': fm_b, 'fc_w': fc_w, 'fc_b': fc_b}
    _L1_xattn_all = _L1_xattn_setup()
    _L1_xattn_in = {k: v for k, v in _L1_xattn_all.items() if k in ('fm_w', 'fm_b', 'fc_w', 'fc_b')}
    del _L1_xattn_all

    def _L1_ffn_setup():
        import jax, jax.numpy as jnp
        import numpy as np
        B, S, D, E, H = (4, 256, 128, 8, 512)
        key = jax.random.key(seed)
        ks = jax.random.split(key, 7)
        scale_d = 1.0 / np.sqrt(D)
        scale_h = 1.0 / np.sqrt(H)
        return {'x': jax.random.normal(ks[0], (B, S, D), dtype=jnp.float32), 'Wr': jax.random.uniform(ks[1], (D, E), jnp.float32, -scale_d, scale_d), 'br': jnp.zeros((E,), jnp.float32), 'W1': jax.random.uniform(ks[2], (E, D, H), jnp.float32, -scale_d, scale_d), 'b1': jax.random.uniform(ks[3], (E, H), jnp.float32, -scale_d, scale_d), 'W2': jax.random.uniform(ks[4], (E, H, D), jnp.float32, -scale_h, scale_h), 'b2': jax.random.uniform(ks[5], (E, D), jnp.float32, -scale_h, scale_h)}
    _L1_ffn_all = _L1_ffn_setup()
    _L1_ffn_in = {k: v for k, v in _L1_ffn_all.items() if k in ('Wr', 'br', 'W1', 'b1', 'W2', 'b2')}
    del _L1_ffn_all
    return {'x': x, 'ctx_1024': ctx_1024, 'g_xattn': g_xattn, 'g_ffn': g_ffn, 'L0_xattn_Wq': _L0_xattn_in['Wq'], 'L0_xattn_Wk': _L0_xattn_in['Wk'], 'L0_xattn_Wv': _L0_xattn_in['Wv'], 'L0_xattn_Wo': _L0_xattn_in['Wo'], 'L0_xattn_bo': _L0_xattn_in['bo'], 'L0_xattn_q_gamma': _L0_xattn_in['q_gamma'], 'L0_xattn_q_beta': _L0_xattn_in['q_beta'], 'L0_xattn_k_gamma': _L0_xattn_in['k_gamma'], 'L0_xattn_k_beta': _L0_xattn_in['k_beta'], 'L0_ffn_w_router': _L0_ffn_in['w_router'], 'L0_ffn_w_gate': _L0_ffn_in['w_gate'], 'L0_ffn_w_down': _L0_ffn_in['w_down'], 'L1_xattn_fm_w': _L1_xattn_in['fm_w'], 'L1_xattn_fm_b': _L1_xattn_in['fm_b'], 'L1_xattn_fc_w': _L1_xattn_in['fc_w'], 'L1_xattn_fc_b': _L1_xattn_in['fc_b'], 'L1_ffn_Wr': _L1_ffn_in['Wr'], 'L1_ffn_br': _L1_ffn_in['br'], 'L1_ffn_W1': _L1_ffn_in['W1'], 'L1_ffn_b1': _L1_ffn_in['b1'], 'L1_ffn_W2': _L1_ffn_in['W2'], 'L1_ffn_b2': _L1_ffn_in['b2']}

def reference(x, ctx_1024, g_xattn, g_ffn, L0_xattn_Wq, L0_xattn_Wk, L0_xattn_Wv, L0_xattn_Wo, L0_xattn_bo, L0_xattn_q_gamma, L0_xattn_q_beta, L0_xattn_k_gamma, L0_xattn_k_beta, L0_ffn_w_router, L0_ffn_w_gate, L0_ffn_w_down, L1_xattn_fm_w, L1_xattn_fm_b, L1_xattn_fc_w, L1_xattn_fc_b, L1_ffn_Wr, L1_ffn_br, L1_ffn_W1, L1_ffn_b1, L1_ffn_W2, L1_ffn_b2):
    import jax
    import jax.numpy as jnp

    def _L0_xattn_ref(hidden_states, encoder_hidden_states, Wq, Wk, Wv, Wo, bo, q_gamma, q_beta, k_gamma, k_beta):
        import jax, jax.numpy as jnp
        import numpy as np
        H, NH, HD = (128, 16, 64)
        INNER = NH * HD
        EPS = 1e-05

        def layernorm(x, g, b):
            mu = jnp.mean(x, axis=-1, keepdims=True)
            var = jnp.var(x, axis=-1, keepdims=True)
            return (x - mu) * jax.lax.rsqrt(var + EPS) * g + b
        B, N, D = hidden_states.shape
        M = encoder_hidden_states.shape[1]
        q = (hidden_states @ Wq).reshape(B, N, NH, HD).transpose(0, 2, 1, 3)
        k = (encoder_hidden_states @ Wk).reshape(B, M, NH, HD).transpose(0, 2, 1, 3)
        v = (encoder_hidden_states @ Wv).reshape(B, M, NH, HD).transpose(0, 2, 1, 3)
        q = layernorm(q, q_gamma, q_beta)
        k = layernorm(k, k_gamma, k_beta)
        scale = HD ** (-0.5)
        scores = jnp.einsum('bhnd,bhmd->bhnm', q, k) * scale
        attn = jax.nn.softmax(scores, axis=-1)
        out = jnp.einsum('bhnm,bhmd->bhnd', attn, v)
        out = out.transpose(0, 2, 1, 3).reshape(B, N, INNER)
        return out @ Wo + bo

    def _L0_ffn_ref(x, w_router, w_gate, w_down):
        import math
        import jax, jax.numpy as jnp
        import numpy as np
        D_MODEL = 128
        D_HIDDEN = 256
        N_EXPERTS = 8
        TOP_K = 2
        CAPACITY_FACTOR = 1.25

        def _moe_forward(x, w_router, w_gate, w_down):
            B, T, D = x.shape
            N = B * T
            xf = x.reshape(N, D)
            logits = xf.astype(jnp.float32) @ w_router.T
            gates = jax.nn.softmax(logits, axis=-1)
            topk_gates, topk_idx = jax.lax.top_k(gates, TOP_K)
            expert_mask = jax.nn.one_hot(topk_idx, N_EXPERTS, dtype=jnp.int32).sum(axis=1)
            capacity = math.ceil(N / N_EXPERTS * CAPACITY_FACTOR)
            position_in_expert = jnp.cumsum(expert_mask, axis=0) - 1
            expert_mask = expert_mask * (position_in_expert < capacity)
            keep = jnp.take_along_axis(expert_mask, topk_idx, axis=1) > 0
            topk_gates = topk_gates * keep
            topk_gates = topk_gates / (topk_gates.sum(axis=-1, keepdims=True) + 1e-06)
            hidden = jax.nn.silu(xf @ w_gate.T)
            combine = (topk_gates[:, :, None] * jax.nn.one_hot(topk_idx, N_EXPERTS, dtype=topk_gates.dtype)).sum(axis=1)
            y = jnp.zeros((N, D), dtype=x.dtype)
            for e in range(N_EXPERTS):
                y = y + combine[:, e:e + 1] * (hidden @ w_down[e].T)
            return y.reshape(B, T, D)
        return _moe_forward(x, w_router, w_gate, w_down)

    def _L1_xattn_ref(values, keys, query, fm_w, fm_b, fc_w, fc_b):
        import jax, jax.numpy as jnp
        import numpy as np
        EMBED = 128
        HEADS = 16
        HEAD_DIM = EMBED // HEADS
        EXP_DIM = 2 * HEAD_DIM

        def _feature_map(x, fm_w, fm_b):
            z = jnp.einsum('nshd,ed->nshe', x, fm_w) + fm_b
            return jnp.concatenate([jnp.exp(z), jnp.exp(-z)], axis=-1)
        N, S, _ = query.shape
        v = values.reshape(N, -1, HEADS, HEAD_DIM)
        k = keys.reshape(N, -1, HEADS, HEAD_DIM)
        q = query.reshape(N, -1, HEADS, HEAD_DIM)
        v, k, q = (_feature_map(x, fm_w, fm_b) for x in (v, k, q))
        scores = jnp.einsum('nqhd,nkhd->nhqk', q, k) / jnp.sqrt(jnp.float32(EMBED))
        attn = jax.nn.softmax(scores, axis=-1)
        out = jnp.einsum('nhql,nlhd->nqhd', attn, v)
        out = out.reshape(N, S, HEADS * EXP_DIM)
        return out @ fc_w.T + fc_b

    def _L1_ffn_ref(x, Wr, br, W1, b1, W2, b2):
        import jax, jax.numpy as jnp
        import numpy as np
        B, S, D, E, H = (4, 256, 128, 8, 512)
        route_logits = jnp.einsum('bsd,de->bse', x, Wr) + br
        routing_weights = jax.nn.softmax(route_logits, axis=-1)
        selected_expert = jnp.argmax(routing_weights, axis=-1)
        num_experts = W1.shape[0]
        out = jnp.zeros_like(x)
        for e in range(num_experts):
            h = jax.nn.gelu(jnp.einsum('bsd,dh->bsh', x, W1[e]) + b1[e], approximate=False)
            y = jnp.einsum('bsh,hd->bsd', h, W2[e]) + b2[e]
            out = jnp.where((selected_expert == e)[..., None], y, out)
        return out
    x = x + jnp.tanh(g_xattn[0]) * _L0_xattn_ref(_layernorm(x, axis=-1), ctx_1024, L0_xattn_Wq, L0_xattn_Wk, L0_xattn_Wv, L0_xattn_Wo, L0_xattn_bo, L0_xattn_q_gamma, L0_xattn_q_beta, L0_xattn_k_gamma, L0_xattn_k_beta)
    x = x + jnp.tanh(g_ffn[0]) * _L0_ffn_ref(_layernorm(x, axis=-1), L0_ffn_w_router, L0_ffn_w_gate, L0_ffn_w_down)
    x = x + jnp.tanh(g_xattn[1]) * _L1_xattn_ref(ctx_1024, ctx_1024, _layernorm(x, axis=-1), L1_xattn_fm_w, L1_xattn_fm_b, L1_xattn_fc_w, L1_xattn_fc_b)
    x = x + jnp.tanh(g_ffn[1]) * _L1_ffn_ref(_layernorm(x, axis=-1), L1_ffn_Wr, L1_ffn_br, L1_ffn_W1, L1_ffn_b1, L1_ffn_W2, L1_ffn_b2)
    return x

_drawn_inputs = setup_inputs


def setup_inputs(seed=0):
    import zlib

    import numpy as np

    out = dict(_drawn_inputs(seed))
    spreads = {'g_ffn': (-1.0, 0.6),
     'L0_xattn_bo': (0.0, 0.1),
     'L0_xattn_q_gamma': (1.0, 0.2),
     'L0_xattn_q_beta': (0.0, 0.501),
     'L0_xattn_k_gamma': (1.0, 0.2),
     'L0_xattn_k_beta': (0.0, 2.0),
     'L1_xattn_fc_b': (0.0, 0.8),
     'L1_ffn_br': (0.0, 0.8)}
    factors = {'L1_ffn_Wr': 5.153,
     'L1_ffn_W1': 5.328,
     'L1_ffn_b1': 8.0,
     'L1_ffn_W2': 5.012,
     'L1_ffn_b2': 35.44}
    for name, (base, spread) in spreads.items():
        noise = np.random.default_rng([zlib.crc32(name.encode()), seed]).standard_normal(out[name].shape)
        drawn = base * np.exp(spread * noise) if base else spread * noise
        out[name] = jnp.asarray(drawn.astype(out[name].dtype))
    for name, factor in factors.items():
        out[name] = (out[name] * factor).astype(out[name].dtype)
    return out
```

```python
from contextlib import ExitStack

import numpy as np

import concourse.bass as bass
from concourse import mybir

ALU = mybir.AluOpType
ACT = mybir.ActivationFunctionType
AX = mybir.AxisListType
F32 = mybir.dt.float32
F16 = mybir.dt.float16
BF16 = mybir.dt.bfloat16
U32 = mybir.dt.uint32

P = 128
B, N, D = 2, 512, 128
M = 154
KA, KC, KCP = 128, 26, 32
KW = KA + KCP
TB = N // P
T = B * TB
NH, HD = 16, 64
G = 4
NG = NH // G
GT = B * NG
EPS = 1e-5
E0, F0, CAP = 8, 256, 160
E1, F1 = 8, 512
HC1 = F1 // P
FD = 16
WS = 64.0

ROW = {}
_at = 0
for _n, _w in (("bo", D), ("gq", HD), ("bq", HD), ("gk", HD), ("bk", HD), ("gx", 2), ("gf", 2),
               ("fmb", D), ("fcb", D), ("br", E1), ("iota", 8)):
    ROW[_n] = (_at, _at + _w)
    _at += _w
ROWS = _at


def build(nc, x_d, out_d, rows_d, ident_d, tri_d, sel_d, ctx_d, wq_d, wk_d, wv_d, wo_d, fm_d,
          wgate_d, wdown_d, wrouter_d, fcw_d, wr_d, w1_d, b1_d, w2_d, b2_d):
    with ExitStack() as ctx:
        def sb(name, shape, dt=F32):
            return ctx.enter_context(nc.sbuf_tensor(name, shape, dt))

        def sem(name):
            return ctx.enter_context(nc.semaphore(name))

        x = sb("x", [P, T, D])
        rows = sb("rows", [P, ROWS])
        ident = sb("ident", [P, P])
        e32 = sb("e32", [P, G + 1, N])
        eh = sb("eh", [P, 2, G + 1, N], F16)
        el = sb("el", [P, 2, G + 1, N], F16)
        e_flat = e32[:].rearrange("p a b -> p (a b)")
        eh_flat = eh[:].rearrange("p z a b -> p (z a b)").bitcast(F32)
        xn = e_flat[:, 0:T * D].rearrange("p (t d) -> p t d", t=T)
        xnT = e_flat[:, T * D:2 * T * D]
        xh = el[:].rearrange("p z a b -> p (z a b)")[:, 0:2 * T * P].rearrange("p (z n) -> p z n", z=2)
        ctxT = eh_flat[:, 0:2 * B * P].rearrange("p (c k) -> p c k", k=P)
        tri = eh_flat[:, 1024:1152]
        sel = eh_flat[0:2 * G, 512:512 + G * P].rearrange("p (j k) -> p j k", j=G)
        stage = sb("stage", [P, 5120])
        wq, wk, wv, wo = (stage[:, 1024 * i:1024 * i + 1024] for i in range(4))
        wkm = stage[:, 4096:5120]
        fm = sb("fm", [P, D])

        def row(name):
            a, b = ROW[name]
            return rows[:, a:b]

        ident16 = sb("ident16", [P, P], F16)
        identb = sb("identb", [P, P], BF16)
        selb = sb("selb", [2 * G, G, P], BF16)
        wsp = sb("wsp", [P, 5, 2, 1024], F16)
        c16 = sb("c16", [P, 2, 2 * B * P], F16)
        th = sb("th", [P, 4])
        hmean = sb("hmean", [P, 2, NH])
        co = sb("co", [P, 5, HD])
        coc = sb("coc", [P, 1])
        st = sb("st", [P, T, 6])
        mv = sb("mv", [P, T, 2])
        lnv = sb("lnv", [P, 3, T])
        work = sb("work", [P, T * NH * (HD + 1)])
        sq = work[:, 4096:6144].rearrange("p (z n) -> p z n", z=2)
        ssk = sb("ssk", [P, 3, 2 * B, NH])
        ssq = eh_flat[:, 1152:1152 + 3 * T * NH].rearrange("p (i t h) -> p i t h", i=3, t=T)
        km = work[:, 0:4096].rearrange("p (c h a d) -> p c h a d", c=2, h=NH, a=2)
        kT = sb("kT", [P, 2, B, NH, KW], F16)
        qn = work[:, 6144:8192].rearrange("p (z h d) -> p z h d", z=2, h=NH)
        qs = sb("qs", [P, T, NH, 2, HD], F16)
        qT = sb("qT", [P, 3, G, N], F16)
        va = sb("va", [P, 2, B, NH, HD + 1], F16)
        vc = sb("vc", [P, 2, B, NH, HD + 1], F16)
        mx = sb("mx", [P, 2, TB, G])
        m12 = sb("m12", [P, 2, TB, 2, G], BF16)
        mT = sb("mT", [2 * G, 2, N], BF16)
        kf = e_flat[:, 0:2 * G * KW].rearrange("p (z h k) -> p z h k", z=2, h=G)
        osum = work[:].rearrange("p (t h d) -> p t h d", t=T, h=NH)
        rsum = sb("rsum", [P, T, NH])
        obo = sb("obo", [P, 2, D])
        wrt = sb("wrt", [P, 2, 8])
        b1c = sb("b1c", [P, E1, HC1])
        b2s = sb("b2s", [E1, D])
        trib = sb("trib", [P, P], BF16)
        onesb = sb("onesb", [P, P], BF16)
        wgs = sb("wgs", [P, 2, F0], F16)
        fcs = sb("fcs", [P, 2, 2 * D], F16)
        gt = sb("gt", [P, 8, T, 8])
        g1 = sb("g1", [P, 4, T])
        g8 = sb("g8", [P, 2, T, 8])
        gi = sb("gi", [P, T, 8], U32)
        maskb = sb("maskb", [P, T, 8], BF16)
        maskT = work[0:E1, 5120:6144]
        qs_flat = qs[:].rearrange("p t h a d -> p (t h a d)")
        wdf, wgf, fcf = stage[:, 0:2048], stage[:, 2048:2304], stage[:, 2304:2560]
        wds = qs_flat[:, 4096:8192].rearrange("p (v c n) -> p v c n", v=2, c=2)
        hs = work[:, 0:2048].rearrange("p (c n) -> p c n", c=2)
        hh0 = work[:, 2048:4096].bitcast(F16).rearrange("p (c v n) -> p c v n", c=2, v=2)
        yw = work[:, 4096:6144].rearrange("p (z e d) -> p z e d", z=2, e=E0)
        fk = stage[:, 4096:5120].rearrange("p (c h d) -> p c h d", c=2 * B, h=NH)
        rk = work[:, 6144:7168].rearrange("p (c h d) -> p c h d", c=2 * B, h=NH)
        zk = work[:, 7168:7680].rearrange("p (c h d) -> p c h d", c=2 * B, h=NH)
        ks = qT[:].bitcast(BF16).rearrange("p z j n -> p (z j n)")\
            .rearrange("p (c h a d) -> p c h a d", c=2 * B, h=NH, a=6)
        fq = stage[:, 0:2048].rearrange("p (t h d) -> p t h d", t=T, h=NH)
        rq = stage[:, 2048:4096].rearrange("p (t h d) -> p t h d", t=T, h=NH)
        zq = stage[:, 4096:5120].rearrange("p (t h d) -> p t h d", t=T, h=NH)
        qs1 = qs_flat[:, 0:T * NH * 6 * FD].bitcast(BF16).rearrange("p (t h a d) -> p t h a d", t=T, h=NH, a=6)
        V1 = FD + 1
        va1, vc1 = (v[:].rearrange("p v b h d -> p (v b h d)")[:, 0:B * NH * 3 * V1].bitcast(BF16)
                    .rearrange("p (b h a d) -> p b h a d", b=B, h=NH, a=3) for v in (va, vc))
        fms = sb("fms", [P, 2, D], F16)
        osum1 = work[:, 0:T * NH * 3 * V1].rearrange("p (t h d) -> p t h d", t=T, h=NH)
        os1 = stage[:, 0:T * NH * V1].rearrange("p (t h d) -> p t h d", t=T, h=NH)
        w1f = stage[:, 3072:5120].rearrange("p (z v n) -> p z v n", z=2, v=2)
        w1s = wsp[:].rearrange("p i v n -> p (i v n)")[:, 0:8192].rearrange("p (z v n) -> p z v n", z=4, v=2)
        h32 = work[:, 0:2048].rearrange("p (z n) -> p z n", z=2)
        hh1 = qs_flat.rearrange("p (z c v n) -> p z c v n", z=2, c=HC1, v=2)
        yt = work[:, 2048:4096].rearrange("p (z t d) -> p z t d", z=2, t=T)
        acc = work[:, 4096:5120].rearrange("p (t d) -> p t d", t=T)

        ps = ctx.enter_context(nc.psum_tensor("ps", [P, 8, 512], F32))

        dma = {n: sem("ld_" + n) for n in ("x", "rows", "ident", "tri", "sel", "ctx", "wq", "wk", "wv",
                                           "wo", "fm", "wdown", "wgate", "fcw", "wr", "wr2", "b1", "b2")}
        dma_e = [sem(f"ld_expert{r}") for r in range(2)]
        s_fms = sem("feature_weights_split")
        s_wg = sem("ffn0_weights_split")
        s_xf = sem("ln_f32")
        s_rt = [sem("router_logits0"), sem("router_logits1")]
        s_gm = [sem("gate_shifted0"), sem("gate_shifted1")]
        s_ge = [sem("gate_exps0"), sem("gate_exps1")]
        s_mk = [sem("masks0"), sem("masks1")]
        s_cum = sem("mask_cumulated")
        s_hp = sem("hidden0_in_psum")
        s_hs = sem("hidden0_silu")
        s_h0 = sem("hidden0_hi")
        s_l0 = sem("hidden0_lo")
        s_y0 = sem("experts0_in_psum")
        s_yw = sem("experts0_weighted")
        s_x0 = sem("ffn0_added")
        s_zk = sem("key_features_in_psum")
        s_zb = sem("key_features_biased")
        s_fk = sem("key_features")
        s_ka = sem("key_parts_act")
        s_kd = sem("key_parts_dve")
        s_v1 = sem("value_ones")
        s_k1 = sem("key_stacks_transposed")
        s_k1e = sem("key_stacks_out")
        s_zq = sem("query_features_in_psum")
        s_zqb = sem("query_features_biased")
        s_fq = sem("query_features")
        s_qa = sem("query_parts_act")
        s_qp = sem("query_parts_pool")
        s_qd = sem("query_parts_dve")
        s_os = sem("parts_summed")
        s_mT = sem("mask_transposed")
        s_mTe = sem("mask_rows")
        s_b2 = sem("selected_b2")
        s_ac = sem("expert_accumulated")
        s_wh = sem("expert_weights_hi")
        s_wl = sem("expert_weights_lo")
        s_h1p = sem("hidden1_in_psum")
        s_h1 = sem("hidden1_gelu")
        s_h1h = sem("hidden1_hi")
        s_h1l = sem("hidden1_lo")
        s_y1 = sem("experts1_in_psum")
        s_y1m = sem("experts1_masked")
        s_dve = sem("dve_chain")
        s_act = sem("act_chain")
        s_pool = sem("pool_chain")
        s_cst = sem("constants_cast")
        s_tanh = sem("gates_ready")
        s_wc = sem("weights_centred")
        s_wkm = sem("wk_mapped")
        s_whi = sem("weights_hi")
        s_wlo = sem("weights_lo")
        s_chi = sem("ctx_hi")
        s_clo = sem("ctx_lo")
        s_beta = sem("beta_row")
        s_betaT = sem("beta_transposed")
        s_coc = sem("beta_column")
        s_lv = sem("ln_var")
        s_ly = sem("ln_rsqrt")
        s_xn = sem("ln_out")
        s_xt = sem("ln_transposed")
        s_xhi = sem("ln_hi")
        s_xlo = sem("ln_lo")
        s_proj = sem("projection_in_psum")
        s_sqr = sem("squares")
        s_ss = sem("square_sums")
        s_ry = sem("head_rsqrt")
        s_km = sem("keys_normalised")
        s_km2 = sem("keys_doubled")
        s_vh = sem("values_hi")
        s_vl = sem("values_lo")
        s_kt = sem("keys_transposed")
        s_kf = sem("keys_f32")
        s_kh = sem("keys_hi")
        s_kl = sem("keys_lo")
        s_qn = sem("queries_normalised")
        s_qh = sem("queries_hi")
        s_ql = sem("queries_lo")
        s_ones = sem("constant_columns")
        s_fin = sem("out_stored")

        def per_layer(name):
            return [sem(f"{name}{k}") for k in range(2)]

        s_qt = per_layer("queries_transposed")
        s_qea = per_layer("queries_out_act")
        s_qed = per_layer("queries_out_dve")
        s_s1 = per_layer("scores_for_max")
        s_mx = per_layer("maxima")
        s_ms = per_layer("maxima_split")
        s_mt = per_layer("maxima_transposed")
        s_me = per_layer("maxima_out")
        s_s2 = per_layer("scores_a")
        s_s2c = per_layer("scores_c")
        s_e = per_layer("exps_a")
        s_ec = per_layer("exps_c")
        s_eha = per_layer("exps_hi_act")
        s_ehp = per_layer("exps_hi_pool")
        s_el = per_layer("exps_lo")
        s_pv = per_layer("weighted_values")
        s_pve = per_layer("weighted_values_out")
        s_rs = per_layer("reciprocal_sums")
        s_on = per_layer("heads_normalised")
        s_ot = per_layer("heads_transposed")
        s_oh = per_layer("heads_hi")
        s_ol = per_layer("heads_lo")
        s_wo = per_layer("attention_projected")
        s_bo = sem("bias_added")
        s_x = sem("residual_updated")

        PROJ = 3 * 2 * B + T

        def pair(n):
            b = 2 * (n % 3)
            return ps[:, b:b + 2, :]

        kT1 = kT[:].bitcast(BF16)
        q_stack = (qs[:].rearrange("p t h a d -> p t h (a d)"), qs1.rearrange("p t h a d -> p t h (a d)"))
        q_T = (qT[:], qT[:].bitcast(BF16))
        ident_q = (ident16, identb)
        QK = (P, 6 * FD)
        SCALE = (1.0, D ** -0.5)
        KPARTS = (((kT[:, 0], P), (kT[:, 1], HD)), ((kT1[:, 0], 6 * FD),))
        VW = (HD + 1, 3 * (FD + 1))
        osums = (osum, osum1)

        def pv_parts(k, b, h, c):
            if k == 0:
                v = vc if c else va
                return ((0, v[:, 0, b, h, :]), (0, v[:, 1, b, h, :]), (1, v[:, 0, b, h, :]))
            v = (vc1 if c else va1)[:, b, h].rearrange("p a d -> p (a d)")
            return ((0, v), (1, v[:, 0:2 * V1]))

        def groups():
            return range(-2, GT + 1)

        def attention_pe(pe, k):
            qTk = q_T[k]
            for it in groups():
                for j in range(G):
                    g = it + 1
                    if 0 <= g < GT:
                        i, b, h = G * g + j, g // NG, G * (g % NG) + j
                        if j == 0:
                            pe.wait_ge(s_qea[k], g + 1)
                        if j == 2:
                            pe.wait_ge(s_qed[k], g + 1)
                        for half in range(2):
                            if i:
                                pe.wait_ge(s_mx[k], 2 * (i - 1) + half + 1)
                            for u in range(2):
                                t = 2 * half + u
                                last = pe.matmul(ps[:, half, u * M:u * M + M],
                                                 qTk[0:QK[k], g % 3, j, t * P:t * P + P],
                                                 KPARTS[k][0][0][0:QK[k], b, h, 0:M], start=True, stop=True)
                            last.then_inc(s_s1[k], 1)
                    g = it
                    if 0 <= g < GT:
                        i, b, h = G * g + j, g // NG, G * (g % NG) + j
                        if j == 0:
                            pe.wait_ge(s_me[k], g + 1)
                        if i >= 2:
                            pe.wait_ge(s_e[k], i - 1)
                        out = ps[:, 2 + i % 2, :]
                        for n, (kk, rws) in enumerate(KPARTS[k]):
                            pe.matmul(out, kk[0:rws, b, h, 0:KA], qTk[0:rws, g % 3, j, :], start=(n == 0), stop=False)
                        pe.matmul(out, selb[:, j, :], mT[:, g % 2, :], start=False, stop=True).then_inc(s_s2[k], 1)
                        if j == 0 and g:
                            pe.wait_ge(s_ec[k], g)
                        out = ps[KCP * j:KCP * j + KCP, 4, :]
                        for n, (kk, rws) in enumerate(KPARTS[k]):
                            pe.matmul(out, kk[0:rws, b, h, KA:KW], qTk[0:rws, g % 3, j, :], start=(n == 0), stop=False,
                                      tile_position=(0, KCP * j))
                        last = pe.matmul(out, selb[:, j, 0:KCP], mT[:, g % 2, :], start=False, stop=True,
                                         tile_position=(0, KCP * j))
                        if j == G - 1:
                            last.then_inc(s_s2c[k], 1)
                    g = it + 2
                    if g < GT and j % 2 == 1:
                        if j == 1 and g >= 2:
                            pe.wait_ge(s_me[k], g - 1)
                        elif j == 1 and g == 1:
                            pe.wait_ge(s_qed[k], 1)
                        elif j == 3:
                            pe.wait_ge(s_qea[k], g + 1)
                        o = ps[:, 5, :].bitcast(BF16 if k else F16)
                        for u in range(2):
                            h = G * (g % NG) + j - 1 + u
                            for t in range(TB):
                                last = pe.transpose(o[0:QK[k], u * N + t * P:u * N + t * P + P],
                                                    q_stack[k][:, TB * (g // NG) + t, h, :], ident_q[k][:])
                        last.then_inc(s_qt[k], 1)
                for j in range(G):
                    g = it - 1
                    if 0 <= g < GT:
                        i, b, h = G * g + j, g // NG, G * (g % NG) + j
                        if j == 0:
                            pe.wait_ge(s_el[k], (G + 1) * (g + 1))
                        if i >= 2:
                            pe.wait_ge(s_pve[k], i - 1)
                        for t in range(TB):
                            out = ps[:, 6 + i % 2, t * VW[k]:(t + 1) * VW[k]]
                            prods = []
                            for c, (slot, lo, hi) in enumerate(((j, 0, KA), (G, KCP * j, KCP * j + KC))):
                                for part, v in pv_parts(k, b, h, c):
                                    prods.append(((eh, el)[part][lo:hi, g % 2, slot, t * P:t * P + P], v[lo:hi]))
                            for n, (w, v) in enumerate(prods):
                                last = pe.matmul(out[:, 0:v.shape[1]], w, v, start=(n == 0), stop=(n == len(prods) - 1))
                        last.then_inc(s_pv[k], 1)
                    g = it + 1
                    if j == 1 and 0 <= g < GT:
                        pe.wait_ge(s_ms[k], g + 1)
                        if g + 1 < GT:
                            pe.wait_ge(s_qed[k], g + 2)
                        else:
                            pe.wait_ge(s_me[k], g)
                        o = ps[:, 5, :].bitcast(BF16)
                        for t in range(TB):
                            last = pe.transpose(o[0:2 * G, t * P:t * P + P],
                                                m12[:, g % 2, t].rearrange("p a j -> p (a j)"), identb[:])
                        last.then_inc(s_mt[k], 1)

        def queries_out(eng, k, g, half):
            o = ps[:, 5, :].bitcast(BF16 if k else F16)[0:QK[k], :].rearrange("p (u n) -> p u n", u=2)
            dst = q_T[k][0:QK[k], g % 3, 2 * half:2 * half + 2, :]
            eng.wait_ge(s_qt[k], 2 * g + half + 1)
            if half == 0:
                eng.activation(dst, o, ACT.Copy).then_inc(s_qea[k], 1)
            else:
                eng.tensor_copy(dst, o).then_inc(s_qed[k], 1)

        def attention_act(act, k):
            for it in groups():
                for j in range(G):
                    g = it
                    if 0 <= g < GT:
                        i = G * g + j
                        act.wait_ge(s_s2[k], i + 1)
                        if g:
                            act.wait_ge(s_el[k], (G + 1) * (g - 1) + j + 1)
                        act.activation(e32[:, j, :], ps[:, 2 + i % 2, :], ACT.Exp, scale=SCALE[k]).then_inc(s_e[k], 1)
                        if j % 2 == 0:
                            act.wait_ge(s_e[k], i + 1)
                            if g >= 2:
                                act.wait_ge(s_pv[k], G * (g - 1))
                            act.activation(eh[:, g % 2, j, :], e32[:, j, :], ACT.Copy).then_inc(s_eha[k], 1)
                    if j == 1 and it + 2 < GT:
                        queries_out(act, k, it + 2, 0)
                g = it
                if 0 <= g < GT:
                    act.wait_ge(s_s2c[k], g + 1)
                    if g:
                        act.wait_ge(s_el[k], (G + 1) * g)
                    act.activation(e32[:, G, :], ps[:, 4, :], ACT.Exp, scale=SCALE[k]).then_inc(s_ec[k], 1)
                    act.wait_ge(s_ec[k], g + 1)
                    act.activation(eh[:, g % 2, G, :], e32[:, G, :], ACT.Copy).then_inc(s_eha[k], 1)
                for j in range(G):
                    g = it - 1
                    if 0 <= g < GT:
                        i, b, h = G * g + j, g // NG, G * (g % NG) + j
                        act.wait_ge(s_pv[k], i + 1)
                        act.activation(osums[k][:, TB * b:TB * b + TB, h, :],
                                       ps[:, 6 + i % 2, 0:TB * VW[k]].rearrange("p (t d) -> p t d", t=TB),
                                       ACT.Copy).then_inc(s_pve[k], 1)
                    g = it + 1
                    if j == 1 and 0 <= g < GT:
                        act.wait_ge(s_mt[k], g + 1)
                        act.activation(mT[:, g % 2, :], ps[0:2 * G, 5, :].bitcast(BF16)[:, 0:N], ACT.Copy)\
                           .then_inc(s_me[k], 1)

        def exp_hi_ready(eng, k, g, j):
            if j % 2 == 0:
                eng.wait_ge(s_eha[k], 3 * g + j // 2 + 1)
            else:
                eng.wait_ge(s_ehp[k], 2 * g + j // 2 + 1)

        def attention_pool(pool, k):
            for g in range(GT):
                for j in (1, 3):
                    pool.wait_ge(s_e[k], G * g + j + 1)
                    if g >= 2:
                        pool.wait_ge(s_pv[k], G * (g - 1))
                    pool.tensor_scalar(eh[:, g % 2, j, :], e32[:, j, :], 1.0, 0.0, ALU.mult, ALU.add)\
                        .then_inc(s_ehp[k], 1)

        def attention_dve(dve, k, link):
            def lo(g, j):
                exp_hi_ready(dve, k, g, j)
                if g >= 2 and j == 0:
                    dve.wait_ge(s_pv[k], G * (g - 1))
                dve.tensor_tensor(el[:, g % 2, j, :], e32[:, j, :], eh[:, g % 2, j, :], ALU.subtract)\
                   .then_inc(s_el[k], 1)

            for it in groups():
                for j in range(G):
                    g = it + 1
                    if 0 <= g < GT:
                        i = G * g + j
                        for half in range(2):
                            dve.wait_ge(s_s1[k], 2 * i + half + 1)
                            dve.tensor_reduce(mx[:, g % 2, 2 * half:2 * half + 2, j],
                                              ps[:, half, 0:2 * M].rearrange("p (u m) -> p u m", u=2),
                                              AX.X, ALU.max).then_inc(s_mx[k], 1)
                    if 0 <= it < GT:
                        lo(it, j)
                    if j == 3 and it + 2 < GT:
                        queries_out(dve, k, it + 2, 1)
                g = it + 1
                if 0 <= g < GT:
                    dve.wait_ge(s_mx[k], 2 * G * (g + 1))
                    if g >= 2:
                        dve.wait_ge(s_mt[k], g - 1)
                    link(dve.tensor_copy(m12[:, g % 2, :, 0, :], mx[:, g % 2]))
                    dve.tensor_tensor(m12[:, g % 2, :, 1, :], mx[:, g % 2], m12[:, g % 2, :, 0, :],
                                      ALU.subtract).then_inc(s_ms[k], 1)
                if 0 <= it < GT:
                    lo(it, G)

        on = qs[:].rearrange("p t h a d -> p (t h a d)")[:, 8192:12288].bitcast(F32)\
            .rearrange("p (z n) -> p z n", z=2)
        HCH = (NH * HD // P, NH * FD // P)
        oT = qs[:].rearrange("p t h a d -> p (t h a d)")[:, 0:4096].rearrange("p (z l n) -> p z l n", z=2, l=2)

        def project_out_pe(pe, k, weights):
            C = HCH[k]
            for t in range(T + 1):
                if t < T:
                    pe.wait_ge(s_on[k], t + 1)
                    if t >= 2:
                        pe.wait_ge(s_ol[k], t - 1)
                    for c in range(C):
                        last = pe.transpose(ps[:, 2 * (t % 2) + c // 4, (c % 4) * P:(c % 4 + 1) * P],
                                            on[:, t % 2, c * P:(c + 1) * P], ident[:])
                    last.then_inc(s_ot[k], 1)
                if t:
                    u = t - 1
                    pe.wait_ge(s_ol[k], u + 1)
                    n = 0
                    for c in range(C):
                        for a, w in ((0, 0), (0, 1), (1, 0)):
                            last = pe.matmul(ps[:, 4 + u // 4, (u % 4) * P:(u % 4 + 1) * P],
                                             oT[:, u % 2, a, c * P:(c + 1) * P], weights(w, c),
                                             start=(n == 0), stop=(n == 3 * C - 1))
                            n += 1
                    last.then_inc(s_wo[k], 1)

        def project_out_act(act, k):
            C = HCH[k]
            for t in range(T):
                act.wait_ge(s_ot[k], t + 1)
                if t >= 2:
                    act.wait_ge(s_wo[k], t - 1)
                act.activation(oT[:, t % 2, 0, 0:C * P], ps[:, 2 * (t % 2):2 * (t % 2) + 2, :]
                               .rearrange("p a b -> p (a b)")[:, 0:C * P], ACT.Copy).then_inc(s_oh[k], 1)

        def project_out_dve(dve, k, o, r):
            C, W = HCH[k], o.shape[3]
            for t in range(T + 1):
                if t < T:
                    if t >= 2:
                        dve.wait_ge(s_ot[k], t - 1)
                    dve.tensor_tensor(on[:, t % 2, 0:C * P].rearrange("p (h d) -> p h d", d=W), o[:, t],
                                      r[:, t, :].unsqueeze(2).to_broadcast([P, NH, W]), ALU.mult).then_inc(s_on[k], 1)
                if t == 0:
                    continue
                t -= 1
                dve.wait_ge(s_oh[k], t + 1)
                dve.tensor_tensor(oT[:, t % 2, 1, 0:C * P], ps[:, 2 * (t % 2):2 * (t % 2) + 2, :]
                                  .rearrange("p a b -> p (a b)")[:, 0:C * P], oT[:, t % 2, 0, 0:C * P],
                                  ALU.subtract).then_inc(s_ol[k], 1)

        x_ps = ps[:, 6:8, :].rearrange("p a b -> p (a b)")

        def ln_pe(pe, k):
            for t in range(T):
                pe.wait_ge(s_xn, T * k + t + 1)
                pe.transpose(ps[:, 6 + t // 4, (t % 4) * P:(t % 4 + 1) * P], xn[:, t, :], ident[:]).then_inc(s_xt, 1)

        def ln_act(act, k):
            act.wait_ge(s_xt, T * k + T)
            if k in (1, 3):
                act.activation(xnT, x_ps, ACT.Copy).then_inc(s_xf, 1)
            act.activation(xh[:, 0, :], x_ps, ACT.Copy).then_inc(s_xhi, 1)

        def ln_dve(dve, k):
            dve.wait_ge(s_xhi, k + 1)
            dve.tensor_tensor(xh[:, 1, :], x_ps, xh[:, 0, :], ALU.subtract).then_inc(s_xlo, 1)

        def router_pe(pe, k):
            pe.wait_ge(s_xf, k + 1)
            pe.wait_ge(dma["wr"], 16)
            for t in range(T):
                last = pe.matmul(ps[:, 5, t * 8:t * 8 + 8], xnT[:, t * P:t * P + P], wrt[:, k, :], start=True, stop=True)
            last.then_inc(s_rt[k], 1)

        LG, EX, GA, MA, MB, KM, CO, TM = range(8)

        def wide(ap):
            return ap.unsqueeze(2).to_broadcast([P, T, 8])

        def iota():
            return rows[:, ROW["iota"][0]:ROW["iota"][1]].unsqueeze(1).to_broadcast([P, T, 8])

        def gates_dve(dve, k, link):
            dve.wait_ge(s_rt[k], 1)
            lp = ps[:, 5, 0:T * 8].rearrange("p (t e) -> p t e", t=T)
            if k:
                br = rows[:, ROW["br"][0]:ROW["br"][1]].unsqueeze(1).to_broadcast([P, T, 8])
                link(dve.tensor_tensor(gt[:, LG], lp, br, ALU.add))
                lp = gt[:, LG]
            link(dve.tensor_reduce(g1[:, 0, :], lp, AX.X, ALU.max))
            dve.tensor_tensor(gt[:, LG], lp, wide(g1[:, 0, :]), ALU.subtract).then_inc(s_gm[k], 1)
            dve.wait_ge(s_ge[k], 1)
            link(dve.tensor_reduce(g1[:, 1, :], gt[:, EX], AX.X, ALU.add))
            link(dve.reciprocal(g1[:, 2, :], g1[:, 1, :]))
            link(dve.tensor_tensor(gt[:, GA], gt[:, EX], wide(g1[:, 2, :]), ALU.mult))
            for t in range(T):
                last = dve.max(g8[:, 0, t, :], gt[:, GA, t, :])
            link(last)
            for t in range(T):
                last = dve.max_index(gi[:, t, :], g8[:, 0, t, :], gt[:, GA, t, :])
            link(last)
            link(dve.tensor_copy(g8[:, 1], gi[:]))
            first = dve.tensor_tensor(gt[:, MA], iota(), wide(g8[:, 1, :, 0]), ALU.is_equal)
            if k:
                first.then_inc(s_mk[1], 1)
            else:
                link(first)
                link(dve.tensor_tensor(gt[:, MB], iota(), wide(g8[:, 1, :, 1]), ALU.is_equal))
                link(dve.tensor_tensor(gt[:, MA], gt[:, MA], gt[:, MB], ALU.add))
                dve.tensor_copy(maskb[:], gt[:, MA]).then_inc(s_mk[0], 1)

        def gates_act(act, k):
            act.wait_ge(s_gm[k], 1)
            act.activation(gt[:, EX], gt[:, LG], ACT.Exp).then_inc(s_ge[k], 1)

        block = ctx.enter_context(nc.Block())

        @block.sync
        def _(sp):
            for name, dst, src in (
                ("x", x[:], x_d.rearrange("(t p) d -> p t d", p=P)),
                ("wk", wk, wk_d), ("rows", rows[:], rows_d.partition_broadcast(P)), ("ctx", ctxT, ctx_d),
                ("ident", ident[:], ident_d), ("wq", wq, wq_d), ("wv", wv, wv_d), ("sel", sel, sel_d),
                ("tri", tri, tri_d), ("fm", fm[:], fm_d),
                ("wo", wo.rearrange("p (c d) -> p c d", d=D), wo_d.rearrange("(c p) d -> p c d", p=P)),
            ):
                sp.dma_start(dst, src).then_inc(dma[name], 16)
            sp.dma_start(wrt[:, 0, :], wrouter_d).then_inc(dma["wr"], 16)
            sp.dma_start(wrt[:, 1, :], wr_d).then_inc(dma["wr2"], 16)
            sp.dma_start(b1c[:], b1_d).then_inc(dma["b1"], 16)
            sp.dma_start(b2s[:], b2_d).then_inc(dma["b2"], 16)
            sp.wait_ge(s_clo, 4)
            sp.wait_ge(s_wlo, 2)
            sp.dma_start(wdf, wdown_d.rearrange("p c n -> p (c n)")).then_inc(dma["wdown"], 16)
            sp.dma_start(wgf, wgate_d).then_inc(dma["wgate"], 16)
            sp.dma_start(fcf.rearrange("p (c d) -> p c d", d=D), fcw_d).then_inc(dma["fcw"], 16)
            sp.wait_ge(s_zqb, 1)
            sp.wait_ge(s_fq, 4)
            sp.wait_ge(s_qd, 6)
            sp.wait_ge(s_qa, 4)
            for e in range(E1):
                if e >= 2:
                    sp.wait_ge(s_wl, 2 * (e - 1))
                sp.dma_start(w1f[:, e % 2, 0, :], w1_d[e]).then_inc(dma_e[e % 2], 16)
                sp.dma_start(w1f[:, e % 2, 1, :].rearrange("p (c d) -> p c d", c=HC1), w2_d[e]).then_inc(dma_e[e % 2], 16)
            sp.wait_ge(s_x, 5)
            sp.dma_start(out_d.rearrange("(t p) d -> p t d", p=P), x[:]).then_inc(s_fin, 16)
            sp.wait_ge(s_fin, 16)

        def heads(ap):
            return ap.rearrange("p (h d) -> p h d", d=HD)

        def bc(ap, shape, axis):
            return ap.unsqueeze(axis).to_broadcast(shape)

        @block.vector
        def _(dve):
            links = [0]

            def link(ins):
                links[0] += 1
                ins.then_inc(s_dve, 1)
                dve.wait_ge(s_dve, links[0])

            def rsqrt_newton(y, v, t):
                link(dve.tensor_tensor(t, y, y, ALU.mult))
                link(dve.scalar_tensor_tensor(out=t, in0=t, scalar=-0.5, in1=v, op0=ALU.mult, op1=ALU.mult))
                return dve.scalar_tensor_tensor(out=y, in0=t, scalar=1.5, in1=y, op0=ALU.add, op1=ALU.mult)

            def layernorm(k):
                for t in range(T):
                    i = dve.bn_stats(st[:, t, :], x[:, t, :])
                link(i)
                for t in range(T):
                    i = dve.bn_aggr(mv[:, t, :], st[:, t, :])
                link(i)
                dve.tensor_scalar(lnv[:, 0, :], mv[:, :, 1], 1.0, EPS, ALU.mult, ALU.add).then_inc(s_lv, 1)
                dve.wait_ge(s_ly, k + 1)
                link(rsqrt_newton(lnv[:, 1, :], lnv[:, 0, :], lnv[:, 2, :]))
                for t in range(T):
                    dve.tensor_scalar(xn[:, t, :], x[:, t, :], mv[:, t, 0:1], lnv[:, 1, t:t + 1],
                                      ALU.subtract, ALU.mult).then_inc(s_xn, 1)

            def centre(w, i):
                link(dve.tensor_reduce(hmean[:, i, :], heads(w), AX.X, ALU.add, negate=True))
                link(dve.tensor_scalar(hmean[:, i, :], hmean[:, i, :], 1.0 / HD, None, ALU.mult))
                ins = dve.tensor_tensor(heads(w), heads(w), bc(hmean[:, i, :], [P, NH, HD], 2), ALU.add)
                ins.then_inc(s_wc, 1)

            dve.wait_ge(dma["x"], 16)
            layernorm(0)
            dve.wait_ge(dma["wk"], 16)
            centre(wk, 0)
            dve.wait_ge(dma["rows"], 16)
            s = HD ** -0.5
            a, c, tmp, beta, beta2 = (co[:, i, :] for i in range(5))
            L = HD - 1
            link(dve.scalar_tensor_tensor(out=a, in0=row("gk"), scalar=s, in1=row("gq"), op0=ALU.mult, op1=ALU.mult))
            link(dve.scalar_tensor_tensor(out=c, in0=row("gk"), scalar=s, in1=row("bq"), op0=ALU.mult, op1=ALU.mult))
            link(dve.scalar_tensor_tensor(out=beta, in0=row("bk"), scalar=s, in1=row("gq"), op0=ALU.mult, op1=ALU.mult))
            link(dve.scalar_tensor_tensor(out=tmp, in0=row("bk"), scalar=s, in1=row("bq"), op0=ALU.mult, op1=ALU.mult))
            link(dve.tensor_scalar(beta[:, 0:L], beta[:, 0:L], beta[:, L:HD], None, ALU.subtract))
            link(dve.tensor_reduce(beta[:, L:HD], tmp, AX.X, ALU.add))
            dve.tensor_copy(beta2, beta).then_inc(s_beta, 1)
            dve.wait_ge(s_wc, 1)
            wkm3 = heads(wkm)
            link(dve.tensor_tensor(wkm3, heads(wk), bc(c, [P, NH, HD], 1), ALU.mult))
            link(dve.tensor_reduce(hmean[:, 0, :], wkm3, AX.X, ALU.add))
            link(dve.tensor_tensor(wkm3, heads(wk), bc(a, [P, NH, HD], 1), ALU.mult))
            link(dve.tensor_tensor(wkm3[:, :, 0:L], wkm3[:, :, 0:L],
                                   wkm3[:, :, L:HD].to_broadcast([P, NH, L]), ALU.subtract))
            dve.tensor_copy(wkm3[:, :, L], hmean[:, 0, :]).then_inc(s_wkm, 1)
            dve.wait_ge(dma["wq"], 16)
            centre(wq, 1)
            for i, (w, k) in enumerate(((wk, 1), (wkm, 2))):
                dve.wait_ge(s_whi, i + 1)
                if i:
                    dve.wait_ge(s_wkm, 1)
                dve.tensor_tensor(wsp[:, k, 1, :], w, wsp[:, k, 0, :], ALU.subtract).then_inc(s_wlo, 1)
            dve.wait_ge(s_xhi, 1)
            dve.tensor_tensor(xh[:, 1, :], ps[:, 6:8, :].rearrange("p a b -> p (a b)"), xh[:, 0, :],
                              ALU.subtract).then_inc(s_xlo, 1)
            dve.wait_ge(s_betaT, 1)
            dve.tensor_copy(coc[:], ps[:, 0, 0:1]).then_inc(s_coc, 1)

            def head_sums(dst, i):
                dve.wait_ge(s_sqr, i + 1)
                link(dve.tensor_reduce(dst, heads(sq[:, i % 2, :]), AX.X, ALU.add))
                dve.tensor_scalar(dst, dst, 1.0 / HD, EPS, ALU.mult, ALU.add).then_inc(s_ss, 1)

            def keys(c):
                n0 = 3 * c
                head_sums(ssk[:, 0, c, :], c)
                dve.wait_ge(s_vh, c + 1)
                v = vc if c % 2 else va
                pv = pair(n0 + 2).rearrange("p a (h d) -> p (a h) d", d=HD)
                dve.tensor_tensor(v[:, 1, c // 2, :, 0:HD], pv, v[:, 0, c // 2, :, 0:HD],
                                  ALU.subtract).then_inc(s_vl, 1)
                dve.wait_ge(s_ry, c + 1)
                link(rsqrt_newton(ssk[:, 1, c, :], ssk[:, 0, c, :], ssk[:, 2, c, :]))
                dve.wait_ge(s_proj, n0 + 2)
                if c == 2:
                    dve.wait_ge(s_kt, NG)
                pk = pair(n0 + 1).rearrange("p a (h d) -> p (a h) d", d=HD)
                dve.tensor_tensor(km[:, c % 2, :, 0, :], pk, bc(ssk[:, 1, c, :], [P, NH, HD], 2),
                                  ALU.mult).then_inc(s_km, 1)

            def queries(t):
                n0 = 3 * 2 * B + t
                head_sums(ssq[:, 0, t, :], 2 * B + t)
                dve.wait_ge(s_ry, 2 * B + t + 1)
                link(rsqrt_newton(ssq[:, 1, t, :], ssq[:, 0, t, :], ssq[:, 2, t, :]))
                if t >= 2:
                    dve.wait_ge(s_qh, t - 1)
                    dve.wait_ge(s_ql, t - 1)
                pq = pair(n0).rearrange("p a (h d) -> p (a h) d", d=HD)
                dve.tensor_tensor(qn[:, t % 2, :, :], pq, bc(ssq[:, 1, t, :], [P, NH, HD], 2),
                                  ALU.mult).then_inc(s_qn, 1)

            for c in range(2 * B):
                keys(c)
                if c % 2:
                    for g in range(NG * (c // 2), NG * (c // 2 + 1)):
                        dve.wait_ge(s_kh, g + 1)
                        b, h = g // NG, G * (g % NG)
                        dve.tensor_tensor(kT[:, 1, b, h:h + G, :], kf[:, g % 2, :, :], kT[:, 0, b, h:h + G, :],
                                          ALU.subtract).then_inc(s_kl, 1)
            for t in range(T):
                queries(t)
            attention_dve(dve, 0, link)
            dve.wait_ge(s_pve[0], B * NH)
            link(dve.reciprocal(rsum[:], osum[:, :, :, HD]))
            project_out_dve(dve, 0, osum[:, :, :, 0:HD], rsum)
            for u in range(2):
                dve.wait_ge(s_wo[0], TB * (u + 1))
                dve.wait_ge(s_bo, 2)
                xs = x[:, TB * u:TB * u + TB, :]
                dve.scalar_tensor_tensor(out=xs, in0=ps[:, 4 + u, :].rearrange("p (t d) -> p t d", t=TB),
                                         scalar=th[:, 0:1], in1=xs, op0=ALU.mult, op1=ALU.add).then_inc(s_x, 1)

            dve.wait_ge(s_x, 2)
            layernorm(1)
            ln_dve(dve, 1)
            gates_dve(dve, 0, link)
            dve.wait_ge(s_cum, 1)
            cum = ps[:, 4, 0:T * 8].rearrange("p (t e) -> p t e", t=T)
            link(dve.scalar_tensor_tensor(out=gt[:, KM], in0=cum, scalar=float(CAP), in1=gt[:, MA],
                                          op0=ALU.is_le, op1=ALU.mult))
            link(dve.tensor_tensor(gt[:, KM], gt[:, KM], gt[:, GA], ALU.mult))
            link(dve.tensor_reduce(g1[:, 0, :], gt[:, KM], AX.X, ALU.add))
            link(dve.tensor_scalar(g1[:, 0, :], g1[:, 0, :], 1.0, 1e-6, ALU.mult, ALU.add))
            link(dve.reciprocal(g1[:, 1, :], g1[:, 0, :]))
            link(dve.tensor_scalar(g1[:, 1, :], g1[:, 1, :], th[:, 2:3], 1.0 / WS, ALU.mult, ALU.mult))
            link(dve.tensor_tensor(gt[:, CO], gt[:, KM], wide(g1[:, 1, :]), ALU.mult))
            for c in range(2):
                dve.wait_ge(s_h0, c + 1)
                dve.tensor_tensor(hh0[:, c, 1, :], hs[:, c, :], hh0[:, c, 0, :], ALU.subtract).then_inc(s_l0, 1)
            for t in range(T):
                dve.wait_ge(s_y0, t + 1)
                if t >= 2:
                    dve.wait_ge(s_x0, t - 1)
                dve.tensor_tensor(yw[:, t % 2], ps[:, 2 * (t % 2):2 * (t % 2) + 2, :].rearrange("p a (e d) -> p (a e) d", d=D),
                                  bc(gt[:, CO, t, :], [P, E0, D], 2), ALU.mult).then_inc(s_yw, 1)
                if t == 0:
                    dve.wait_ge(s_zk, 1)
                    fmb = row("fmb").unsqueeze(1).to_broadcast([P, 2 * B, D])
                    dve.tensor_tensor(zk.rearrange("p c h d -> p c (h d)"), ps[:, 5, :].rearrange("p (c n) -> p c n", n=D),
                                      fmb, ALU.add).then_inc(s_zb, 1)
                if t == 2:
                    dve.wait_ge(s_ka, 1)
                    dve.tensor_tensor(rk, fk, ks[:, :, :, 0, :], ALU.subtract).then_inc(s_kd, 1)
                if t == 3:
                    dve.wait_ge(s_ka, 5)
                    link(dve.tensor_tensor(ks[:, :, :, 4, :], rk, ks[:, :, :, 1, :], ALU.subtract))
                    dve.wait_ge(s_v1, 4)
                    for c in range(2 * B):
                        v = (vc1 if c % 2 else va1)[:, c // 2]
                        for part, slot in enumerate((0, 1, 4)):
                            last = dve.tensor_copy(v[:, :, part, 0:FD], ks[:, c, :, slot, :])
                    last.then_inc(s_kd, 1)

            dve.wait_ge(s_x0, T)
            layernorm(2)
            ln_dve(dve, 2)
            dve.wait_ge(s_zq, 1)
            fmb = row("fmb").unsqueeze(1).to_broadcast([P, T, D])
            dve.tensor_tensor(zq.rearrange("p t h d -> p t (h d)"), ps[:, 0:2, :].rearrange("p a (t n) -> p (a t) n", n=D),
                              fmb, ALU.add).then_inc(s_zqb, 1)
            for b in range(B):
                ts = slice(TB * b, TB * b + TB)
                dve.wait_ge(s_qa, 2 * b + 1)
                link(dve.tensor_tensor(rq[:, ts], fq[:, ts], qs1[:, ts, :, 0, :], ALU.subtract))
                dve.tensor_copy(qs1[:, ts, :, 2, :], rq[:, ts]).then_inc(s_qd, 1)
                dve.wait_ge(s_qd, 3 * b + 1)
                dve.tensor_tensor(qs1[:, ts, :, 5, :], rq[:, ts], qs1[:, ts, :, 2, :], ALU.subtract).then_inc(s_qd, 1)
                dve.tensor_copy(qs1[:, ts, :, 3, :], qs1[:, ts, :, 2, :]).then_inc(s_qd, 1)
            attention_dve(dve, 1, link)
            for b in range(B):
                ts = slice(TB * b, TB * b + TB)
                dve.wait_ge(s_pve[1], NH * (b + 1))
                link(dve.tensor_reduce(os1[:, ts].rearrange("p t h d -> p (t h) d"),
                                       osum1[:, ts].rearrange("p t h (a d) -> p (t h) d a", a=3), AX.X, ALU.add))
            link(dve.reciprocal(rsum[:], os1[:, :, :, FD]))
            project_out_dve(dve, 1, os1[:, :, :, 0:FD], rsum)
            for u in range(2):
                dve.wait_ge(s_wo[1], TB * (u + 1))
                dve.wait_ge(s_bo, 4)
                xs = x[:, TB * u:TB * u + TB, :]
                dve.scalar_tensor_tensor(out=xs, in0=ps[:, 4 + u, :].rearrange("p (t d) -> p t d", t=TB),
                                         scalar=th[:, 1:2], in1=xs, op0=ALU.mult, op1=ALU.add).then_inc(s_x, 1)

            dve.wait_ge(s_x, 4)
            layernorm(3)
            ln_dve(dve, 3)
            gates_dve(dve, 1, link)
            for u in range(2):
                dve.wait_ge(s_mT, T)
                dve.tensor_copy(maskT[:, u * 512:u * 512 + 512], ps[0:E1, 6 + u, :]).then_inc(s_mTe, 1)
            dve.wait_ge(s_b2, 1)
            dve.tensor_copy(acc, ps[:, 4:6, :].rearrange("p a (t d) -> p (a t) d", d=D)).then_inc(s_ac, 1)

            def weights_lo(e):
                dve.wait_ge(s_wh, 2 * (e + 1))
                for w in range(2):
                    dve.tensor_tensor(w1s[:, e % 4, 1, 512 * w:512 * w + 512], w1f[:, e % 2, w, :],
                                      w1s[:, e % 4, 0, 512 * w:512 * w + 512], ALU.subtract).then_inc(s_wl, 1)

            weights_lo(0)
            weights_lo(1)
            for n in range(HC1 * (E1 + 1)):
                e, c = n // HC1, n % HC1
                if e < E1:
                    dve.wait_ge(s_h1h, n + 1)
                    if e >= 2 and c == 0:
                        dve.wait_ge(s_y1, e - 1)
                    dve.tensor_tensor(hh1[:, e % 2, c, 1, :], h32[:, n % 2, :], hh1[:, e % 2, c, 0, :],
                                      ALU.subtract).then_inc(s_h1l, 1)
                if c == 3 and e + 2 < E1:
                    weights_lo(e + 2)
                if c == 2 and e >= 1:
                    f = e - 1
                    dve.wait_ge(s_y1, f + 1)
                    link(dve.tensor_tensor(yt[:, f % 2], ps[:, 4 + 2 * (f % 2):6 + 2 * (f % 2), :]
                                           .rearrange("p a (t d) -> p (a t) d", d=D),
                                           bc(gt[:, MA, :, f], [P, T, D], 2), ALU.mult))
                    dve.tensor_tensor(acc, acc, yt[:, f % 2], ALU.add).then_inc(s_ac, 1)
                    dve.wait_ge(s_ac, f + 2)
            dve.scalar_tensor_tensor(out=x[:], in0=acc, scalar=th[:, 3:4], in1=x[:], op0=ALU.mult,
                                     op1=ALU.add).then_inc(s_x, 1)

        @block.gpsimd
        def _(pool):
            pool.memset(qs[:, :, :, 0, HD - 1:HD], 1.0).then_inc(s_ones, 1)
            pool.memset(qs[:, :, :, 1, HD - 1:HD], 0.0).then_inc(s_ones, 1)
            for v in (va, vc):
                pool.memset(v[:, 0, :, :, HD:HD + 1], 1.0).then_inc(s_ones, 1)
                pool.memset(v[:, 1, :, :, HD:HD + 1], 0.0).then_inc(s_ones, 1)

            def cast(dst, src):
                return pool.tensor_scalar(dst, src, 1.0, 0.0, ALU.mult, ALU.add)

            pool.wait_ge(dma["ident"], 16)
            cast(ident16[:], ident[:]).then_inc(s_cst, 1)
            cast(identb[:], ident[:]).then_inc(s_cst, 1)
            pool.wait_ge(dma["sel"], 16)
            cast(selb[:], sel).then_inc(s_cst, 1)
            pool.wait_ge(dma["tri"], 16)
            cast(trib[:], tri).then_inc(s_cst, 1)
            pool.memset(onesb[:], 1.0).then_inc(s_cst, 1)
            pool.wait_ge(s_chi, 1)
            pool.tensor_tensor(c16[:, 1, :], ctxT.rearrange("p a b -> p (a b)"), c16[:, 0, :],
                               ALU.subtract).then_inc(s_clo, 1)
            pool.wait_ge(s_whi, 3)
            pool.tensor_tensor(wsp[:, 3, 1, :], wv, wsp[:, 3, 0, :], ALU.subtract).then_inc(s_clo, 1)
            pool.wait_ge(s_whi, 4)
            pool.tensor_tensor(wsp[:, 0, 1, :], wq, wsp[:, 0, 0, :], ALU.subtract).then_inc(s_clo, 1)
            pool.wait_ge(s_whi, 5)
            pool.tensor_tensor(wsp[:, 4, 1, :], wo, wsp[:, 4, 0, :], ALU.subtract).then_inc(s_clo, 1)
            for g in range(GT):
                if g % NG == 0:
                    for c in (2 * g // NG, 2 * g // NG + 1):
                        pool.wait_ge(s_km, c + 1)
                        if c == 2:
                            pool.wait_ge(s_kt, NG)
                        cast(km[:, c % 2, :, 1, :], km[:, c % 2, :, 0, :]).then_inc(s_km2, 1)
                pool.wait_ge(s_kf, g + 1)
                b, h = g // NG, G * (g % NG)
                cast(kT[:, 0, b, h:h + G, :], kf[:, g % 2, :, :]).then_inc(s_kh, 1)
            for t in range(T):
                pool.wait_ge(s_qh, t + 1)
                pool.tensor_tensor(qs[:, t, :, 1, 0:HD - 1], qn[:, t % 2, :, 0:HD - 1],
                                   qs[:, t, :, 0, 0:HD - 1], ALU.subtract).then_inc(s_ql, 1)
            pool.wait_ge(s_tanh, 1)
            pool.wait_ge(s_xn, T)
            pool.tensor_scalar(obo[:, 0, :], row("bo"), th[:, 0:1], 0.0, ALU.mult, ALU.add).then_inc(s_bo, 1)
            pool.wait_ge(s_bo, 1)
            pool.tensor_tensor(x[:], x[:], obo[:, 0, :].unsqueeze(1).to_broadcast([P, T, D]), ALU.add).then_inc(s_bo, 1)
            attention_pool(pool, 0)

            links = [0]

            def link(ins):
                links[0] += 1
                ins.then_inc(s_pool, 1)
                pool.wait_ge(s_pool, links[0])

            pool.wait_ge(dma["wgate"], 16)
            pool.wait_ge(dma["wdown"], 16)
            pool.wait_ge(s_qt[0], 2 * GT)
            wd_hi, wd_lo = (wds[:, w].rearrange("p c n -> p (c n)") for w in range(2))
            for w, hi, lo in ((wgf, wgs[:, 0, :], wgs[:, 1, :]), (wdf, wd_hi, wd_lo)):
                pool.tensor_scalar(hi, w, WS, 0.0, ALU.mult, ALU.add)
                link(pool.tensor_scalar(w, w, WS, 0.0, ALU.mult, ALU.add))
                pool.tensor_tensor(lo, w, hi, ALU.subtract).then_inc(s_wg, 1)
            pool.wait_ge(dma["fcw"], 16)
            pool.wait_ge(dma["fm"], 16)
            cast(fms[:, 0, :], fm[:])
            link(cast(fcs[:, 0, :], fcf))
            pool.tensor_tensor(fms[:, 1, :], fm[:], fms[:, 0, :], ALU.subtract).then_inc(s_fms, 1)
            pool.tensor_tensor(fcs[:, 1, :], fcf, fcs[:, 0, :], ALU.subtract).then_inc(s_fms, 1)
            pool.wait_ge(s_pv[0], B * NH)
            for v in (va1, vc1):
                pool.memset(v[:, :, :, 0, FD:V1], 1.0).then_inc(s_v1, 1)
                pool.memset(v[:, :, :, 1:3, FD:V1], 0.0).then_inc(s_v1, 1)
            for t in range(T):
                pool.wait_ge(s_yw, t + 1)
                for half in (4, 2, 1):
                    link(pool.tensor_tensor(yw[:, t % 2, 0:half, :], yw[:, t % 2, 0:half, :],
                                            yw[:, t % 2, half:2 * half, :], ALU.add))
                pool.tensor_tensor(x[:, t, :], x[:, t, :], yw[:, t % 2, 0, :], ALU.add).then_inc(s_x0, 1)
            pool.wait_ge(s_xn, 2 * T + T)
            pool.tensor_scalar(obo[:, 1, :], row("fcb"), th[:, 1:2], 0.0, ALU.mult, ALU.add).then_inc(s_bo, 1)
            pool.wait_ge(s_bo, 3)
            pool.tensor_tensor(x[:], x[:], obo[:, 1, :].unsqueeze(1).to_broadcast([P, T, D]), ALU.add).then_inc(s_bo, 1)
            for b in range(B):
                ts = slice(TB * b, TB * b + TB)
                pool.wait_ge(s_fq, 2 * b + 2)
                cast(qs1[:, ts, :, 1, :], fq[:, ts]).then_inc(s_qp, 1)
            attention_pool(pool, 1)
            for n in range(HC1 * E1):
                e, c = n // HC1, n % HC1
                pool.wait_ge(s_h1, n + 1)
                if e >= 2 and c == 0:
                    pool.wait_ge(s_y1, e - 1)
                cast(hh1[:, e % 2, c, 0, :], h32[:, n % 2, :]).then_inc(s_h1h, 1)

        @block.scalar
        def _(act):
            links = [0]

            def link(ins):
                links[0] += 1
                ins.then_inc(s_act, 1)
                act.wait_ge(s_act, links[0])

            def rsqrt_first(y, v):
                link(act.activation(y, v, ACT.Ln))
                return act.activation(y, y, ACT.Exp, scale=-0.5)

            act.wait_ge(dma["rows"], 16)
            act.activation(th[:], rows[:, ROW["gx"][0]:ROW["gf"][1]], ACT.Tanh).then_inc(s_tanh, 1)
            act.wait_ge(s_lv, 1)
            rsqrt_first(lnv[:, 1, :], lnv[:, 0, :]).then_inc(s_ly, 1)
            act.wait_ge(dma["ctx"], 16)
            act.activation(c16[:, 0, :], ctxT.rearrange("p a b -> p (a b)"), ACT.Copy).then_inc(s_chi, 1)
            act.wait_ge(s_wc, 1)
            act.activation(wsp[:, 1, 0, :], wk, ACT.Copy).then_inc(s_whi, 1)
            act.wait_ge(s_wkm, 1)
            act.activation(wsp[:, 2, 0, :], wkm, ACT.Copy).then_inc(s_whi, 1)
            act.wait_ge(dma["wv"], 16)
            act.activation(wsp[:, 3, 0, :], wv, ACT.Copy).then_inc(s_whi, 1)
            act.wait_ge(s_wc, 2)
            act.activation(wsp[:, 0, 0, :], wq, ACT.Copy).then_inc(s_whi, 1)
            act.wait_ge(dma["wo"], 16)
            act.activation(wsp[:, 4, 0, :], wo, ACT.Copy).then_inc(s_whi, 1)
            act.wait_ge(s_xt, T)
            act.activation(xh[:, 0, :], ps[:, 6:8, :].rearrange("p a b -> p (a b)"), ACT.Copy).then_inc(s_xhi, 1)

            def squares(n0, i):
                act.wait_ge(s_proj, n0 + 1)
                if i >= 2:
                    act.wait_ge(s_ss, i - 1)
                act.activation(sq[:, i % 2, :], pair(n0).rearrange("p a b -> p (a b)"), ACT.Square).then_inc(s_sqr, 1)

            for c in range(2 * B):
                squares(3 * c, c)
                act.wait_ge(s_proj, 3 * c + 3)
                v = vc if c % 2 else va
                pv = pair(3 * c + 2).rearrange("p a (h d) -> p (a h) d", d=HD)
                act.activation(v[:, 0, c // 2, :, 0:HD], pv, ACT.Copy).then_inc(s_vh, 1)
                act.wait_ge(s_ss, c + 1)
                rsqrt_first(ssk[:, 1, c, :], ssk[:, 0, c, :]).then_inc(s_ry, 1)
                for g in range(NG * (c // 2), NG * (c // 2 + 1)) if c % 2 else ():
                    act.wait_ge(s_coc, 1)
                    act.wait_ge(s_kt, g + 1)
                    if g >= 2:
                        act.wait_ge(s_kl, g - 1)
                    act.activation(kf[:, g % 2, :, :].rearrange("p (a h) k -> p a (h k)", a=2),
                                   ps[:, 6:8, 0:2 * KW], ACT.Identity, bias=coc[:]).then_inc(s_kf, 1)

            def q_hi(t):
                act.wait_ge(s_qn, t + 1)
                act.activation(qs[:, t, :, 0, 0:HD - 1], qn[:, t % 2, :, 0:HD - 1], ACT.Copy).then_inc(s_qh, 1)

            for t in range(T):
                squares(3 * 2 * B + t, 2 * B + t)
                act.wait_ge(s_ss, 2 * B + t + 1)
                rsqrt_first(ssq[:, 1, t, :], ssq[:, 0, t, :]).then_inc(s_ry, 1)
                if t >= 1:
                    q_hi(t - 1)
            q_hi(T - 1)
            attention_act(act, 0)
            project_out_act(act, 0)

            def layernorm(k):
                act.wait_ge(s_lv, k + 1)
                rsqrt_first(lnv[:, 1, :], lnv[:, 0, :]).then_inc(s_ly, 1)
                ln_act(act, k)

            layernorm(1)
            gates_act(act, 0)
            for c in range(2):
                act.wait_ge(s_hp, c + 1)
                act.activation(hs[:, c, :], ps[:, 2 * c:2 * c + 2, :].rearrange("p a b -> p (a b)"), ACT.Silu,
                               scale=1.0 / WS).then_inc(s_hs, 1)
                act.wait_ge(s_hs, c + 1)
                act.activation(hh0[:, c, 0, :], hs[:, c, :], ACT.Copy).then_inc(s_h0, 1)
            act.wait_ge(s_zb, 1)
            act.activation(fk[:, :, :, 0:8], zk, ACT.Exp).then_inc(s_fk, 1)
            act.activation(fk[:, :, :, 8:16], zk, ACT.Exp, scale=-1.0).then_inc(s_fk, 1)
            act.wait_ge(s_fk, 2)
            for slot in (0, 2, 5):
                act.activation(ks[:, :, :, slot, :], fk, ACT.Copy).then_inc(s_ka, 1)
            act.wait_ge(s_kd, 1)
            for slot in (1, 3):
                act.activation(ks[:, :, :, slot, :], rk, ACT.Copy).then_inc(s_ka, 1)
            for g in range(GT):
                act.wait_ge(s_k1, g + 1)
                b, h = g // NG, G * (g % NG)
                act.activation(kT1[0:6 * FD, 0, b, h:h + G, :],
                               ps[:, 6 + g % 2, :].bitcast(BF16)[0:6 * FD, 0:G * KW].rearrange("p (h k) -> p h k", h=G),
                               ACT.Copy).then_inc(s_k1e, 1)
            layernorm(2)
            act.wait_ge(s_zqb, 1)
            for b in range(B):
                ts = slice(TB * b, TB * b + TB)
                act.activation(fq[:, ts, :, 0:8], zq[:, ts], ACT.Exp).then_inc(s_fq, 1)
                act.activation(fq[:, ts, :, 8:16], zq[:, ts], ACT.Exp, scale=-1.0).then_inc(s_fq, 1)
                act.wait_ge(s_fq, 2 * b + 2)
                act.activation(qs1[:, ts, :, 0, :], fq[:, ts], ACT.Copy).then_inc(s_qa, 1)
                act.activation(qs1[:, ts, :, 4, :], fq[:, ts], ACT.Copy).then_inc(s_qa, 1)
            attention_act(act, 1)
            project_out_act(act, 1)
            layernorm(3)
            gates_act(act, 1)

            def weights_hi(e):
                act.wait_ge(dma_e[e % 2], 32 * (e // 2 + 1))
                if e >= 4:
                    act.wait_ge(s_y1, e - 3)
                for w in range(2):
                    act.activation(w1s[:, e % 4, 0, 512 * w:512 * w + 512], w1f[:, e % 2, w, :], ACT.Copy).then_inc(s_wh, 1)

            weights_hi(0)
            weights_hi(1)
            for n in range(HC1 * E1):
                e, c = n // HC1, n % HC1
                act.wait_ge(s_h1p, n + 1)
                if n >= 2:
                    act.wait_ge(s_h1l, n - 1)
                act.activation(h32[:, n % 2, :], ps[:, 2 * (n % 2):2 * (n % 2) + 2, :].rearrange("p a b -> p (a b)"),
                               ACT.Gelu, bias=b1c[:, e, c:c + 1]).then_inc(s_h1, 1)
                if c == 2 and e + 2 < E1:
                    weights_hi(e + 2)

        @block.tensor
        def _(pe):
            pe.wait_ge(dma["ident"], 16)
            for t in range(T):
                pe.wait_ge(s_xn, t + 1)
                pe.transpose(ps[:, 6 + t // 4, (t % 4) * P:(t % 4 + 1) * P], xn[:, t, :], ident[:]).then_inc(s_xt, 1)
            pe.wait_ge(s_beta, 1)
            pe.transpose(ps[:, 0, 0:P], co[:, 3:5, :].rearrange("p a d -> p (a d)"), ident[:]).then_inc(s_betaT, 1)

            def project(n, xs, k):
                for half in range(2):
                    for i, (a, w) in enumerate(((0, 0), (0, 1), (1, 0))):
                        last = pe.matmul(pair(n)[:, half, :], xs[a], wsp[:, k, w, half * 512:half * 512 + 512],
                                         start=(i == 0), stop=(i == 2))
                last.then_inc(s_proj, 1)

            def keys_transposed(b):
                for g in range(NG * b, NG * b + NG):
                    h0 = G * (g % NG)
                    pe.wait_ge(s_km2, 2 * b + 2)
                    if g:
                        pe.wait_ge(s_kf, g)
                    else:
                        pe.wait_ge(s_xlo, 1)
                    for j in range(G):
                        for c, (w, at) in enumerate(((KA, 0), (KCP, KA))):
                            o = (j % 2) * KW + at
                            last = pe.transpose(ps[:, 6 + j // 2, o:o + w],
                                                km[0:w, c, h0 + j].rearrange("p a d -> p (a d)"), ident[0:w, 0:w])
                    last.then_inc(s_kt, 1)

            pe.wait_ge(s_coc, 1)
            pe.wait_ge(s_chi, 1)
            for c in range(2 * B):
                xs = [c16[:, i, c * P:c * P + P] for i in range(2)]
                if c == 0:
                    pe.wait_ge(s_wlo, 1)
                    pe.wait_ge(s_clo, 1)
                else:
                    pe.wait_ge(s_sqr, c)
                project(3 * c, xs, 1)
                if c == 0:
                    pe.wait_ge(s_wlo, 2)
                else:
                    pe.wait_ge(s_km, c)
                project(3 * c + 1, xs, 2)
                if c == 0:
                    pe.wait_ge(s_clo, 2)
                else:
                    pe.wait_ge(s_vl, c)
                project(3 * c + 2, xs, 3)
                if c % 2:
                    keys_transposed(c // 2)
            pe.wait_ge(s_xlo, 1)
            pe.wait_ge(s_clo, 3)
            for t in range(T):
                if t == 0:
                    pe.wait_ge(s_km, 2 * B)
                    pe.wait_ge(s_vl, 2 * B)
                elif t >= 3:
                    pe.wait_ge(s_qn, t - 2)
                project(3 * 2 * B + t, [xh[:, i, t * P:t * P + P] for i in range(2)], 0)
            pe.wait_ge(s_qn, T)
            pe.wait_ge(s_ql, T)
            pe.wait_ge(s_kl, GT)
            pe.wait_ge(s_kf, GT)
            pe.wait_ge(s_ones, 6)
            pe.wait_ge(s_cst, 3)
            attention_pe(pe, 0)
            project_out_pe(pe, 0, lambda w, c: wsp[:, 4, w, c * P:(c + 1) * P])

            HILO = ((0, 0), (0, 1), (1, 0))

            ln_pe(pe, 1)
            router_pe(pe, 0)
            pe.wait_ge(s_xlo, 2)
            pe.wait_ge(s_wg, 1)
            for c in range(2):
                for u in range(2):
                    for i, (w, a) in enumerate(HILO):
                        last = pe.matmul(ps[:, 2 * c + u, :], wgs[:, w, c * P:(c + 1) * P],
                                         xh[:, a, u * 512:u * 512 + 512], start=(i == 0), stop=(i == 2))
                last.then_inc(s_hp, 1)
            pe.wait_ge(s_mk[0], 1)
            for t in range(T):
                for u in range(t + 1):
                    last = pe.matmul(ps[:, 4, t * 8:t * 8 + 8], trib[:] if u == t else onesb[:], maskb[:, u, :],
                                     start=(u == 0), stop=(u == t))
            last.then_inc(s_cum, 1)
            pe.wait_ge(s_fms, 1)
            for c in range(2 * B):
                for i, (a, w) in enumerate(HILO):
                    last = pe.matmul(ps[:, 5, c * P:(c + 1) * P], c16[:, a, c * P:(c + 1) * P], fms[:, w, :],
                                     start=(i == 0), stop=(i == 2))
            last.then_inc(s_zk, 1)
            pe.wait_ge(s_l0, 2)
            pe.wait_ge(s_wg, 2)
            for t in range(T):
                if t >= 2:
                    pe.wait_ge(s_yw, t - 1)
                for u in range(2):
                    n = 0
                    for c in range(2):
                        for a, w in HILO:
                            last = pe.matmul(ps[:, 2 * (t % 2) + u, :], hh0[:, c, a, t * P:(t + 1) * P],
                                             wds[:, w, c, u * 512:u * 512 + 512], start=(n == 0), stop=(n == 5))
                            n += 1
                last.then_inc(s_y0, 1)
            for g in range(GT):
                if g == 0:
                    pe.wait_ge(s_ka, 5)
                    pe.wait_ge(s_kd, 2)
                if g >= 2:
                    pe.wait_ge(s_k1e, g - 1)
                o = ps[:, 6 + g % 2, :].bitcast(BF16)
                for j in range(G):
                    for c, (w, at) in enumerate(((KA, 0), (KCP, KA))):
                        last = pe.transpose(o[0:6 * FD, j * KW + at:j * KW + at + w],
                                            ks[0:w, 2 * (g // NG) + c, G * (g % NG) + j].rearrange("p a d -> p (a d)"),
                                            identb[0:w, 0:w])
                last.then_inc(s_k1, 1)
            pe.wait_ge(s_k1e, GT)
            ln_pe(pe, 2)
            pe.wait_ge(s_xlo, 3)
            for t in range(T):
                for i, (a, w) in enumerate(HILO):
                    last = pe.matmul(ps[:, t // 4, (t % 4) * P:(t % 4 + 1) * P], xh[:, a, t * P:(t + 1) * P], fms[:, w, :],
                                     start=(i == 0), stop=(i == 2))
            last.then_inc(s_zq, 1)
            pe.wait_ge(s_qd, 6)
            pe.wait_ge(s_qa, 4)
            pe.wait_ge(s_qp, 2)
            attention_pe(pe, 1)
            project_out_pe(pe, 1, lambda w, c: fcs[:, w, c * P:(c + 1) * P])
            ln_pe(pe, 3)
            pe.wait_ge(dma["wr2"], 16)
            router_pe(pe, 1)
            pe.wait_ge(s_xlo, 4)
            pe.wait_ge(s_mk[1], 1)
            for t in range(T):
                pe.transpose(ps[0:E1, 6 + t // 4, (t % 4) * P:(t % 4 + 1) * P], gt[:, MA, t, :], ident[:]).then_inc(s_mT, 1)
            pe.wait_ge(s_mTe, 2)
            pe.wait_ge(dma["b2"], 16)
            for t in range(T):
                last = pe.matmul(ps[:, 4 + t // 4, (t % 4) * P:(t % 4 + 1) * P], maskT[:, t * P:(t + 1) * P], b2s[:],
                                 start=True, stop=True)
            last.then_inc(s_b2, 1)
            pe.wait_ge(dma["b1"], 16)
            for n in range(HC1 * (E1 + 1)):
                e, c = n // HC1, n % HC1
                if e < E1:
                    if c == 0:
                        pe.wait_ge(s_wl, 2 * (e + 1))
                    if n >= 2:
                        pe.wait_ge(s_h1, n - 1)
                    for u in range(2):
                        for i, (w, a) in enumerate(HILO):
                            last = pe.matmul(ps[:, 2 * (n % 2) + u, :], w1s[:, e % 4, w, c * P:(c + 1) * P],
                                             xh[:, a, u * 512:u * 512 + 512], start=(i == 0), stop=(i == 2))
                    last.then_inc(s_h1p, 1)
                if e >= 1:
                    f = e - 1
                    if c == 0:
                        pe.wait_ge(s_h1l, HC1 * e)
                        pe.wait_ge(s_ac, max(1, f))
                    for t in (2 * c, 2 * c + 1):
                        m = 0
                        for q in range(HC1):
                            for a, w in HILO:
                                last = pe.matmul(ps[:, 4 + 2 * (f % 2) + t // 4, (t % 4) * P:(t % 4 + 1) * P],
                                                 hh1[:, f % 2, q, a, t * P:(t + 1) * P],
                                                 w1s[:, f % 4, w, 512 + q * P:512 + (q + 1) * P],
                                                 start=(m == 0), stop=(m == 3 * HC1 - 1))
                                m += 1
                    if c == HC1 - 1:
                        last.then_inc(s_y1, 1)


NAMES = ("rows", "ident", "tri", "sel", "ctx", "wq", "wk", "wv", "wo", "fm", "wgate", "wdown", "wrouter",
         "fcw", "wr", "w1", "b1", "w2", "b2")


def laid_out(i):
    f = {k: np.asarray(v) for k, v in i.items()}
    row = np.zeros((1, ROWS), np.float32)
    for name, v in (("bo", f["L0_xattn_bo"]), ("gq", f["L0_xattn_q_gamma"]), ("bq", f["L0_xattn_q_beta"]),
                    ("gk", f["L0_xattn_k_gamma"]), ("bk", f["L0_xattn_k_beta"]), ("gx", f["g_xattn"]),
                    ("gf", f["g_ffn"]), ("fmb", np.tile(f["L1_xattn_fm_b"], NH)), ("fcb", f["L1_xattn_fc_b"]),
                    ("br", f["L1_ffn_br"]), ("iota", np.arange(8, dtype=np.float32))):
        row[0, ROW[name][0]:ROW[name][1]] = v
    sel = np.zeros((2, G, G, P), np.float32)
    for j in range(G):
        sel[:, j, j, :] = -1.0
    c = f["ctx_1024"]
    tiles = []
    for b in range(B):
        tiles.append(c[b, :KA])
        tiles += [np.concatenate([c[b, KA:M], c[b, :KCP - KC]])] * G
    fm = np.zeros((NH, 8, NH, 8), np.float32)
    for h in range(NH):
        fm[h, :, h, :] = f["L1_xattn_fm_w"].T
    return {
        "x": f["x"].reshape(B * N, D), "rows": row, "ident": np.eye(P, dtype=np.float32),
        "tri": np.triu(np.ones((P, P), np.float32)), "sel": sel.reshape(2 * G, G, P),
        "ctx": np.concatenate(tiles).T.reshape(D, 2 * B, P),
        "wq": f["L0_xattn_Wq"], "wk": f["L0_xattn_Wk"], "wv": f["L0_xattn_Wv"], "wo": f["L0_xattn_Wo"],
        "fm": fm.reshape(P, P), "wgate": f["L0_ffn_w_gate"].T,
        "wdown": f["L0_ffn_w_down"].transpose(2, 0, 1).reshape(2, P, E0 * D).transpose(1, 0, 2),
        "wrouter": f["L0_ffn_w_router"].T, "fcw": f["L1_xattn_fc_w"].T.reshape(2, P, D).transpose(1, 0, 2),
        "wr": f["L1_ffn_Wr"], "w1": f["L1_ffn_W1"], "b1": f["L1_ffn_b1"].reshape(E1, HC1, P).transpose(2, 0, 1),
        "w2": f["L1_ffn_W2"].reshape(E1, HC1, P, D).transpose(0, 2, 1, 3), "b2": f["L1_ffn_b2"],
    }


def kernel(**inputs):
    from concourse import bacc
    from concourse.bass_utils import run_bass_kernel_spmd

    nc = bacc.Bacc("TRN2", target_bir_lowering=False, num_devices=1)
    arrays = {k: np.ascontiguousarray(v) for k, v in laid_out(inputs).items()}
    aps = {k: nc.dram_tensor(k + "_in", v.shape, mybir.dt.from_np(v.dtype), kind="ExternalInput").ap()
           for k, v in arrays.items()}
    out = nc.dram_tensor("out", (B * N, D), F32, kind="ExternalOutput").ap()
    build(nc, aps["x"], out, *[aps[k] for k in NAMES])
    r = run_bass_kernel_spmd(nc, [{k + "_in": v for k, v in arrays.items()}], core_ids=[0])
    return r.results[0]["out"].reshape(B, N, D)
```

```python
from contextlib import ExitStack

import numpy as np

import concourse.bass as bass
from concourse import mybir

ALU = mybir.AluOpType
ACT = mybir.ActivationFunctionType
AX = mybir.AxisListType
F32 = mybir.dt.float32
F16 = mybir.dt.float16
BF16 = mybir.dt.bfloat16
U32 = mybir.dt.uint32

P = 128
B, N, D = 2, 512, 128
M = 154
KA, KC, KCP = 128, 26, 32
KW = KA + KCP
TB = N // P
T = B * TB
NH, HD = 16, 64
G = 4
NG = NH // G
GT = B * NG
EPS = 1e-5
E0, F0, CAP = 8, 256, 160
E1, F1 = 8, 512
HC1 = F1 // P
FD = 16
WS = 64.0

ROW = {}
_at = 0
for _n, _w in (("bo", D), ("gq", HD), ("bq", HD), ("gk", HD), ("bk", HD), ("gx", 2), ("gf", 2),
               ("fmb", D), ("fcb", D), ("br", E1), ("iota", 8)):
    ROW[_n] = (_at, _at + _w)
    _at += _w
ROWS = _at


def build(nc, x_d, out_d, rows_d, ident_d, tri_d, ctx_d, wq_d, wk_d, wv_d, wo_d, fm_d,
          wgate_d, wdown_d, wrouter_d, fcw_d, wr_d, w1_d, b1_d, w2_d, b2_d):
    with ExitStack() as ctx:
        def sb(name, shape, dt=F32):
            return ctx.enter_context(nc.sbuf_tensor(name, shape, dt))

        def sem(name):
            return ctx.enter_context(nc.semaphore(name))

        x = sb("x", [P, T, D])
        rows = sb("rows", [P, ROWS])
        ident = sb("ident", [P, P])
        e32 = sb("e32", [P, G + 1, N])
        eh = sb("eh", [P, 2, G + 1, N], F16)
        el = sb("el", [P, 2, G + 1, N], F16)
        e_flat = e32[:].rearrange("p a b -> p (a b)")
        eh_flat = eh[:].rearrange("p z a b -> p (z a b)").bitcast(F32)
        xn = e_flat[:, 0:T * D].rearrange("p (t d) -> p t d", t=T)
        xnT = e_flat[:, T * D:2 * T * D]
        xh = el[:].rearrange("p z a b -> p (z a b)")[:, 0:2 * T * P].rearrange("p (z n) -> p z n", z=2)
        ctxT = eh_flat[:, 0:2 * B * P].rearrange("p (c k) -> p c k", k=P)
        tri = eh_flat[:, 1024:1152]
        stage = sb("stage", [P, 5120])
        wq, wk, wv, wo = (stage[:, 1024 * i:1024 * i + 1024] for i in range(4))
        wkm = stage[:, 4096:5120]
        fm = sb("fm", [P, D])

        def row(name):
            a, b = ROW[name]
            return rows[:, a:b]

        ident16 = sb("ident16", [P, P], F16)
        identb = sb("identb", [P, P], BF16)
        wsp = sb("wsp", [P, 5, 2, 1024], F16)
        c16 = sb("c16", [P, 2, 2 * B * P], F16)
        th = sb("th", [P, 4])
        hmean = sb("hmean", [P, 2, NH])
        co = sb("co", [P, 5, HD])
        coc = sb("coc", [P, 1])
        st = sb("st", [P, T, 6])
        mv = sb("mv", [P, T, 2])
        lnv = sb("lnv", [P, 3, T])
        work = sb("work", [P, T * NH * (HD + 1)])
        sq = work[:, 4096:6144].rearrange("p (z n) -> p z n", z=2)
        ssk = sb("ssk", [P, 3, 2 * B, NH])
        ssq = eh_flat[:, 1152:1152 + 3 * T * NH].rearrange("p (i t h) -> p i t h", i=3, t=T)
        km = work[:, 0:4096].rearrange("p (c h a d) -> p c h a d", c=2, h=NH, a=2)
        kT = sb("kT", [P, 2, B, NH, KW], F16)
        qn = work[:, 6144:8192].rearrange("p (z h d) -> p z h d", z=2, h=NH)
        qs = sb("qs", [P, T, NH, 2, HD], F16)
        qT = sb("qT", [P, 3, G, N], F16)
        va = sb("va", [P, 2, B, NH, HD + 1], F16)
        vc = sb("vc", [P, 2, B, NH, HD + 1], F16)
        mx = sb("mx", [P, 2, TB, G])
        m12 = sb("m12", [P, 2, TB, 2, G], BF16)
        mT = sb("mT", [2 * G, 2, N], BF16)
        kf = e_flat[:, 0:2 * G * KW].rearrange("p (z h k) -> p z h k", z=2, h=G)
        osum = work[:].rearrange("p (t h d) -> p t h d", t=T, h=NH)
        rsum = sb("rsum", [P, T, NH])
        obo = sb("obo", [P, 2, D])
        wrt = sb("wrt", [P, 2, 8])
        b1c = sb("b1c", [P, E1, HC1])
        b2s = sb("b2s", [E1, D])
        trib = sb("trib", [P, P], BF16)
        onesb = sb("onesb", [P, P], BF16)
        wgs = sb("wgs", [P, 2, F0], F16)
        fcs = sb("fcs", [P, 2, 2 * D], F16)
        gt = sb("gt", [P, 8, T, 8])
        g1 = sb("g1", [P, 4, T])
        g8 = sb("g8", [P, 2, T, 8])
        gi = sb("gi", [P, T, 8], U32)
        maskb = sb("maskb", [P, T, 8], BF16)
        maskT = work[0:E1, 5120:6144]
        qs_flat = qs[:].rearrange("p t h a d -> p (t h a d)")
        wdf, wgf, fcf = stage[:, 0:2048], stage[:, 2048:2304], stage[:, 2304:2560]
        wds = qs_flat[:, 4096:8192].rearrange("p (v c n) -> p v c n", v=2, c=2)
        hs = work[:, 0:2048].rearrange("p (c n) -> p c n", c=2)
        hh0 = work[:, 2048:4096].bitcast(F16).rearrange("p (c v n) -> p c v n", c=2, v=2)
        yw = work[:, 4096:6144].rearrange("p (z e d) -> p z e d", z=2, e=E0)
        fk = stage[:, 4096:5120].rearrange("p (c h d) -> p c h d", c=2 * B, h=NH)
        rk = work[:, 6144:7168].rearrange("p (c h d) -> p c h d", c=2 * B, h=NH)
        zk = work[:, 7168:7680].rearrange("p (c h d) -> p c h d", c=2 * B, h=NH)
        ks = qT[:].bitcast(BF16).rearrange("p z j n -> p (z j n)")\
            .rearrange("p (c h a d) -> p c h a d", c=2 * B, h=NH, a=6)
        fq = stage[:, 0:2048].rearrange("p (t h d) -> p t h d", t=T, h=NH)
        rq = stage[:, 2048:4096].rearrange("p (t h d) -> p t h d", t=T, h=NH)
        zq = stage[:, 4096:5120].rearrange("p (t h d) -> p t h d", t=T, h=NH)
        qs1 = qs_flat[:, 0:T * NH * 6 * FD].bitcast(BF16).rearrange("p (t h a d) -> p t h a d", t=T, h=NH, a=6)
        V1 = FD + 1
        va1, vc1 = (v[:].rearrange("p v b h d -> p (v b h d)")[:, 0:B * NH * 3 * V1].bitcast(BF16)
                    .rearrange("p (b h a d) -> p b h a d", b=B, h=NH, a=3) for v in (va, vc))
        fms = sb("fms", [P, 2, D], F16)
        osum1 = work[:, 0:T * NH * 3 * V1].rearrange("p (t h d) -> p t h d", t=T, h=NH)
        os1 = stage[:, 0:T * NH * V1].rearrange("p (t h d) -> p t h d", t=T, h=NH)
        w1f = stage[:, 3072:5120].rearrange("p (z v n) -> p z v n", z=2, v=2)
        w1s = wsp[:].rearrange("p i v n -> p (i v n)")[:, 0:8192].rearrange("p (z v n) -> p z v n", z=4, v=2)
        h32 = work[:, 0:2048].rearrange("p (z n) -> p z n", z=2)
        hh1 = qs_flat.rearrange("p (z c v n) -> p z c v n", z=2, c=HC1, v=2)
        yt = work[:, 2048:4096].rearrange("p (z t d) -> p z t d", z=2, t=T)
        acc = work[:, 4096:5120].rearrange("p (t d) -> p t d", t=T)

        ps = ctx.enter_context(nc.psum_tensor("ps", [P, 8, 512], F32))

        dma = {n: sem("ld_" + n) for n in ("x", "rows", "ident", "tri", "ctx", "wq", "wk", "wv",
                                           "wo", "fm", "wdown", "wgate", "fcw", "wr", "wr2", "b1", "b2")}
        dma_e = [sem(f"ld_expert{r}") for r in range(2)]
        s_fms = sem("feature_weights_split")
        s_wg = sem("ffn0_weights_split")
        s_xf = sem("ln_f32")
        s_rt = [sem("router_logits0"), sem("router_logits1")]
        s_gm = [sem("gate_shifted0"), sem("gate_shifted1")]
        s_ge = [sem("gate_exps0"), sem("gate_exps1")]
        s_mk = [sem("masks0"), sem("masks1")]
        s_cum = sem("mask_cumulated")
        s_hp = sem("hidden0_in_psum")
        s_hs = sem("hidden0_silu")
        s_h0 = sem("hidden0_hi")
        s_l0 = sem("hidden0_lo")
        s_y0 = sem("experts0_in_psum")
        s_yw = sem("experts0_weighted")
        s_x0 = sem("ffn0_added")
        s_zk = sem("key_features_in_psum")
        s_zb = sem("key_features_biased")
        s_fk = sem("key_features")
        s_ka = sem("key_parts_act")
        s_kd = sem("key_parts_dve")
        s_v1 = sem("value_ones")
        s_m1 = sem("minus_ones")
        s_k1 = sem("key_stacks_transposed")
        s_k1e = sem("key_stacks_out")
        s_zq = sem("query_features_in_psum")
        s_zqb = sem("query_features_biased")
        s_fq = sem("query_features")
        s_qa = sem("query_parts_act")
        s_qp = sem("query_parts_pool")
        s_qd = sem("query_parts_dve")
        s_mT = sem("mask_transposed")
        s_mTe = sem("mask_rows")
        s_b2 = sem("selected_b2")
        s_ac = sem("expert_accumulated")
        s_wh = sem("expert_weights_hi")
        s_wl = sem("expert_weights_lo")
        s_h1p = sem("hidden1_in_psum")
        s_h1 = sem("hidden1_gelu")
        s_h1h = sem("hidden1_hi")
        s_h1l = sem("hidden1_lo")
        s_y1 = sem("experts1_in_psum")
        s_dve = sem("dve_chain")
        s_act = sem("act_chain")
        s_pool = sem("pool_chain")
        s_cst = sem("constants_cast")
        s_tanh = sem("gates_ready")
        s_wc = sem("weights_centred")
        s_wkm = sem("wk_mapped")
        s_whi = sem("weights_hi")
        s_wlo = sem("weights_lo")
        s_chi = sem("ctx_hi")
        s_clo = sem("ctx_lo")
        s_beta = sem("beta_row")
        s_betaT = sem("beta_transposed")
        s_coc = sem("beta_column")
        s_lv = sem("ln_var")
        s_ly = sem("ln_rsqrt")
        s_xn = sem("ln_out")
        s_xt = sem("ln_transposed")
        s_xhi = sem("ln_hi")
        s_xlo = sem("ln_lo")
        s_proj = sem("projection_in_psum")
        s_sqr = sem("squares")
        s_ss = sem("square_sums")
        s_ry = sem("head_rsqrt")
        s_km = sem("keys_normalised")
        s_km2 = sem("keys_doubled")
        s_vh = sem("values_hi")
        s_vl = sem("values_lo")
        s_kt = sem("keys_transposed")
        s_kf = sem("keys_f32")
        s_kh = sem("keys_hi")
        s_kl = sem("keys_lo")
        s_qn = sem("queries_normalised")
        s_qh = sem("queries_hi")
        s_ql = sem("queries_lo")
        s_ones = sem("constant_columns")
        s_fin = sem("out_stored")

        def per_layer(name):
            return [sem(f"{name}{k}") for k in range(2)]

        s_qt = per_layer("queries_transposed")
        s_qea = per_layer("queries_out_act")
        s_qed = per_layer("queries_out_dve")
        s_s1 = per_layer("scores_for_max")
        s_mx = per_layer("maxima")
        s_ms = per_layer("maxima_split")
        s_mt = per_layer("maxima_transposed")
        s_md = per_layer("maxima_in_stacks")
        s_me = per_layer("maxima_out")
        s_s2 = per_layer("scores_a")
        s_s2c = per_layer("scores_c")
        s_e = per_layer("exps_a")
        s_ec = per_layer("exps_c")
        s_eha = per_layer("exps_hi_act")
        s_ehp = per_layer("exps_hi_pool")
        s_el = per_layer("exps_lo")
        s_pv = per_layer("weighted_values")
        s_pve = per_layer("weighted_values_out")
        s_on = per_layer("heads_normalised")
        s_ot = per_layer("heads_transposed")
        s_oh = per_layer("heads_hi")
        s_ol = per_layer("heads_lo")
        s_wo = per_layer("attention_projected")
        s_bo = sem("bias_added")
        s_x = sem("residual_updated")

        JOBS = (("kv", 0), ("kv", 1), ("q", 0), ("q", 1), ("q", 2), ("q", 3), ("kv", 2), ("kv", 3),
                ("q", 4), ("q", 5), ("q", 6), ("q", 7))
        NJ = len(JOBS)
        KTJOB = (3, 4, 5, 6, 9, 10, 11, 12)
        PROJ = []
        for _n in range(NJ):
            kind, i = JOBS[_n]
            PROJ.append(("k" if kind == "kv" else "q", i))
            if _n and JOBS[_n - 1][0] == "kv":
                PROJ.append(("km", JOBS[_n - 1][1]))
            if kind == "kv":
                PROJ.append(("v", i))

        def job_of(what, i):
            return JOBS.index(("q" if what == "q" else "kv", i))

        def pair(n):
            b = 2 * (n % 3)
            return ps[:, b:b + 2, :]

        def pair_of(what, i):
            return pair(PROJ.index((what, i)))

        kT1 = kT[:].bitcast(BF16)
        q_stack = (qs[:].rearrange("p t h a d -> p t h (a d)"), qs1.rearrange("p t h a d -> p t h (a d)"))
        q_T = (qT[:], qT[:].bitcast(BF16))
        ident_q = (ident16, identb)
        QK = (P, 6 * FD)
        SCALE = (1.0, D ** -0.5)
        KPARTS = ((kT[:, 0], kT[:, 1]), (kT1[:, 0],))
        QM = (P - 1, 6 * FD)
        SK = (P, 6 * FD + 2)
        VW = (HD + 1, 3 * (FD + 1))
        osums = (osum, osum1)

        def pv_parts(k, b, h, c):
            if k == 0:
                v = vc if c else va
                return ((0, v[:, 0, b, h, :]), (0, v[:, 1, b, h, :]), (1, v[:, 0, b, h, :]))
            v = (vc1 if c else va1)[:, b, h].rearrange("p a d -> p (a d)")
            return ((0, v), (1, v[:, 0:2 * V1]))

        def groups():
            return range(-2, GT + 1)

        def where(g, j):
            return G * g + j, g // NG, G * (g % NG) + j

        MROWS = (1, 2)
        m_T = (mT[:].bitcast(F16), mT[:])
        m_1 = (m12[:].bitcast(F16), m12[:])

        def attention_pe(pe, k):
            qTk = q_T[k]

            def scores_for_max(g, j):
                i, b, h = where(g, j)
                if j == 0:
                    pe.wait_ge(s_qea[k], g + 1)
                if j == 2:
                    pe.wait_ge(s_qed[k], g + 1)
                for half in range(2):
                    if i:
                        pe.wait_ge(s_mx[k], 2 * (i - 1) + half + 1)
                    for u in range(2):
                        t = 2 * half + u
                        last = pe.matmul(ps[:, half, u * M:u * M + M], qTk[0:QK[k], g % 3, j, t * P:t * P + P],
                                         KPARTS[k][0][0:QK[k], b, h, 0:M], start=True, stop=True)
                    last.then_inc(s_s1[k], 1)

            def scores(g, j):
                i, b, h = where(g, j)
                if j == 0:
                    pe.wait_ge(s_md[k], 16 * MROWS[k] * (g + 1))
                if i >= 2:
                    pe.wait_ge(s_e[k], i - 1)
                n = len(KPARTS[k])
                for q, kk in enumerate(KPARTS[k]):
                    last = pe.matmul(ps[:, 2 + i % 2, :], kk[0:SK[k], b, h, 0:KA], qTk[0:SK[k], g % 3, j, :],
                                     start=(q == 0), stop=(q == n - 1))
                last.then_inc(s_s2[k], 1)

            def scores_c(g):
                if g:
                    pe.wait_ge(s_ec[k], g)
                n = len(KPARTS[k])
                for q, kk in enumerate(KPARTS[k]):
                    for j in range(G):
                        i, b, h = where(g, j)
                        last = pe.matmul(ps[KCP * j:KCP * j + KCP, 4, :], kk[0:SK[k], b, h, KA:KW],
                                         qTk[0:SK[k], g % 3, j, :], start=(q == 0), stop=(q == n - 1),
                                         tile_position=(0, KCP * j))
                last.then_inc(s_s2c[k], 1)

            def queries_in(g, half):
                if half:
                    if g:
                        pe.wait_ge(s_me[k], g)
                    else:
                        pe.wait_ge(s_qea[k], g + 1)
                elif g:
                    pe.wait_ge(s_qed[k], g)
                o = ps[:, 5, :].bitcast(BF16 if k else F16)
                for u in range(2):
                    h = G * (g % NG) + 2 * half + u
                    for t in range(TB):
                        last = pe.transpose(o[0:QK[k], u * N + t * P:u * N + t * P + P],
                                            q_stack[k][:, TB * (g // NG) + t, h, :], ident_q[k][:])
                last.then_inc(s_qt[k], 1)

            def times_values(g, j):
                i, b, h = where(g, j)
                if j == 0:
                    pe.wait_ge(s_el[k], (G + 1) * (g + 1))
                if i >= 2:
                    pe.wait_ge(s_pve[k], i - 1)
                for t in range(TB):
                    out = ps[:, 6 + i % 2, t * VW[k]:(t + 1) * VW[k]]
                    prods = []
                    for c, (slot, lo, hi) in enumerate(((j, 0, KA), (G, KCP * j, KCP * j + KC))):
                        for part, v in pv_parts(k, b, h, c):
                            prods.append(((eh, el)[part][lo:hi, g % 2, slot, t * P:t * P + P], v[lo:hi]))
                    for n, (w, v) in enumerate(prods):
                        last = pe.matmul(out[:, 0:v.shape[1]], w, v, start=(n == 0), stop=(n == len(prods) - 1))
                last.then_inc(s_pv[k], 1)

            def maxima_in(g):
                pe.wait_ge(s_ms[k], g + 1)
                if g + 1 < GT:
                    pe.wait_ge(s_qea[k], g + 2)
                o = ps[:, 5, :].bitcast(BF16 if k else F16)
                for t in range(TB):
                    last = pe.transpose(o[0:MROWS[k] * G, t * P:t * P + P],
                                        m_1[k][:, g % 2, t, 0:MROWS[k]].rearrange("p a j -> p (a j)"), ident_q[k][:])
                last.then_inc(s_mt[k], 1)

            for it in groups():
                ahead, now, behind = 0 <= it + 1 < GT, 0 <= it < GT, 0 <= it - 1 < GT
                if ahead:
                    scores_for_max(it + 1, 0)
                    scores_for_max(it + 1, 1)
                if now:
                    scores(it, 0)
                if ahead:
                    scores_for_max(it + 1, 2)
                if now:
                    scores(it, 1)
                if behind:
                    times_values(it - 1, 0)
                if ahead:
                    scores_for_max(it + 1, 3)
                if now:
                    scores(it, 2)
                    scores_c(it)
                if it + 2 < GT:
                    queries_in(it + 2, 0)
                if now:
                    scores(it, 3)
                if behind:
                    times_values(it - 1, 1)
                if ahead:
                    maxima_in(it + 1)
                if behind:
                    times_values(it - 1, 2)
                if it + 2 < GT:
                    queries_in(it + 2, 1)
                if behind:
                    times_values(it - 1, 3)

        def queries_out(eng, k, g, half):
            o = ps[:, 5, :].bitcast(BF16 if k else F16)[0:QK[k], :].rearrange("p (u n) -> p u n", u=2)
            dst = q_T[k][0:QK[k], g % 3, 2 * half:2 * half + 2, :]
            eng.wait_ge(s_qt[k], 2 * g + half + 1)
            if half == 0:
                eng.activation(dst, o, ACT.Copy).then_inc(s_qea[k], 1)
            else:
                eng.tensor_copy(dst, o).then_inc(s_qed[k], 1)

        def maxima_to_stacks(sp, k):
            for g in range(GT):
                sp.wait_ge(s_me[k], g + 1)
                for a in range(MROWS[k]):
                    sp.dma_start(q_T[k][QM[k] + a:QM[k] + a + 1, g % 3, :, :],
                                 m_T[k][G * a:G * a + G, g % 2, :]).then_inc(s_md[k], 16)

        ORDER = (0, 1, 2, G, 3)

        def e32_free(eng, k, g, j):
            if g:
                eng.wait_ge(s_el[k], (G + 1) * (g - 1) + ORDER.index(j) + 1)

        def attention_act(act, k):
            def exps(g, j):
                i = G * g + j
                act.wait_ge(s_s2[k], i + 1)
                e32_free(act, k, g, j)
                act.activation(e32[:, j, :], ps[:, 2 + i % 2, :], ACT.Exp, scale=SCALE[k]).then_inc(s_e[k], 1)

            def exps_c(g):
                act.wait_ge(s_s2c[k], g + 1)
                e32_free(act, k, g, G)
                act.activation(e32[:, G, :], ps[:, 4, :], ACT.Exp, scale=SCALE[k]).then_inc(s_ec[k], 1)

            def values_out(g, j):
                i, b, h = where(g, j)
                act.wait_ge(s_pv[k], i + 1)
                act.activation(osums[k][:, TB * b:TB * b + TB, h, :],
                               ps[:, 6 + i % 2, 0:TB * VW[k]].rearrange("p (t d) -> p t d", t=TB),
                               ACT.Copy).then_inc(s_pve[k], 1)

            for it in groups():
                ahead, now, behind = 0 <= it + 1 < GT, 0 <= it < GT, 0 <= it - 1 < GT
                if now:
                    exps(it, 0)
                    exps(it, 1)
                    act.wait_ge(s_e[k], G * it + 1)
                    if it >= 2:
                        act.wait_ge(s_pv[k], G * (it - 1))
                    act.activation(eh[:, it % 2, 0, :], e32[:, 0, :], ACT.Copy).then_inc(s_eha[k], 1)
                if behind:
                    values_out(it - 1, 0)
                if now:
                    exps(it, 2)
                    exps_c(it)
                if it + 2 < GT:
                    queries_out(act, k, it + 2, 0)
                if now:
                    exps(it, 3)
                if behind:
                    values_out(it - 1, 1)
                if ahead:
                    act.wait_ge(s_mt[k], it + 2)
                    if it >= 1:
                        act.wait_ge(s_md[k], 16 * MROWS[k] * it)
                    act.activation(m_T[k][0:MROWS[k] * G, (it + 1) % 2, :],
                                   ps[0:MROWS[k] * G, 5, :].bitcast(BF16 if k else F16)[:, 0:N],
                                   ACT.Copy).then_inc(s_me[k], 1)
                if behind:
                    values_out(it - 1, 2)
                    values_out(it - 1, 3)

        def attention_pool(pool, k):
            for g in range(GT):
                for j in ORDER[1:]:
                    if j == G:
                        pool.wait_ge(s_ec[k], g + 1)
                    else:
                        pool.wait_ge(s_e[k], G * g + j + 1)
                    if g >= 2:
                        pool.wait_ge(s_pv[k], G * (g - 1))
                    pool.tensor_scalar(eh[:, g % 2, j, :], e32[:, j, :], 1.0, 0.0, ALU.mult, ALU.add)\
                        .then_inc(s_ehp[k], 1)

        def attention_dve(dve, k, link):
            def lo(g):
                for n, j in enumerate(ORDER):
                    if n == 0:
                        dve.wait_ge(s_eha[k], g + 1)
                        if g >= 2:
                            dve.wait_ge(s_pv[k], G * (g - 1))
                    else:
                        dve.wait_ge(s_ehp[k], G * g + n)
                    dve.tensor_tensor(el[:, g % 2, j, :], e32[:, j, :], eh[:, g % 2, j, :], ALU.subtract)\
                       .then_inc(s_el[k], 1)

            def maxima(g):
                for j in range(G):
                    i = G * g + j
                    for half in range(2):
                        dve.wait_ge(s_s1[k], 2 * i + half + 1)
                        dve.tensor_reduce(mx[:, g % 2, 2 * half:2 * half + 2, j],
                                          ps[:, half, 0:2 * M].rearrange("p (u m) -> p u m", u=2),
                                          AX.X, ALU.max).then_inc(s_mx[k], 1)
                dve.wait_ge(s_mx[k], 2 * G * (g + 1))
                if g >= 2:
                    dve.wait_ge(s_mt[k], g - 1)
                hi = m_1[k][:, g % 2, :, 0, :]
                if k == 0:
                    dve.tensor_copy(hi, mx[:, g % 2]).then_inc(s_ms[k], 1)
                else:
                    link(dve.tensor_copy(hi, mx[:, g % 2]))
                    dve.tensor_tensor(m_1[k][:, g % 2, :, 1, :], mx[:, g % 2], hi, ALU.subtract).then_inc(s_ms[k], 1)

            for it in groups():
                if 0 <= it + 1 < GT:
                    maxima(it + 1)
                if 0 <= it < GT:
                    lo(it)
                if it + 2 < GT:
                    queries_out(dve, k, it + 2, 1)

        on = qs[:].rearrange("p t h a d -> p (t h a d)")[:, 8192:12288].bitcast(F32)\
            .rearrange("p (z n) -> p z n", z=2)
        HCH = (NH * HD // P, NH * FD // P)
        oT = qs[:].rearrange("p t h a d -> p (t h a d)")[:, 0:4096].rearrange("p (z l n) -> p z l n", z=2, l=2)

        def project_out_pe(pe, k, weights):
            C = HCH[k]
            for t in range(T + 1):
                if t < T:
                    pe.wait_ge(s_on[k], t + 1)
                    if t >= 2:
                        pe.wait_ge(s_ol[k], t - 1)
                    for c in range(C):
                        last = pe.transpose(ps[:, 2 * (t % 2) + c // 4, (c % 4) * P:(c % 4 + 1) * P],
                                            on[:, t % 2, c * P:(c + 1) * P], ident[:])
                    last.then_inc(s_ot[k], 1)
                if t:
                    u = t - 1
                    pe.wait_ge(s_ol[k], u + 1)
                    n = 0
                    for c in range(C):
                        for a, w in ((0, 0), (0, 1), (1, 0)):
                            last = pe.matmul(ps[:, 4 + u // 4, (u % 4) * P:(u % 4 + 1) * P],
                                             oT[:, u % 2, a, c * P:(c + 1) * P], weights(w, c),
                                             start=(n == 0), stop=(n == 3 * C - 1))
                            n += 1
                    last.then_inc(s_wo[k], 1)

        def project_out_act(act, k):
            C = HCH[k]
            for t in range(T):
                act.wait_ge(s_ot[k], t + 1)
                if t >= 2:
                    act.wait_ge(s_wo[k], t - 1)
                act.activation(oT[:, t % 2, 0, 0:C * P], ps[:, 2 * (t % 2):2 * (t % 2) + 2, :]
                               .rearrange("p a b -> p (a b)")[:, 0:C * P], ACT.Copy).then_inc(s_oh[k], 1)

        def project_out_dve(dve, k, o, r):
            C, W = HCH[k], o.shape[3]
            for t in range(T + 1):
                if t < T:
                    if t >= 2:
                        dve.wait_ge(s_ot[k], t - 1)
                    dve.tensor_tensor(on[:, t % 2, 0:C * P].rearrange("p (h d) -> p h d", d=W), o[:, t],
                                      r[:, t, :].unsqueeze(2).to_broadcast([P, NH, W]), ALU.mult).then_inc(s_on[k], 1)
                if t == 0:
                    continue
                t -= 1
                dve.wait_ge(s_oh[k], t + 1)
                dve.tensor_tensor(oT[:, t % 2, 1, 0:C * P], ps[:, 2 * (t % 2):2 * (t % 2) + 2, :]
                                  .rearrange("p a b -> p (a b)")[:, 0:C * P], oT[:, t % 2, 0, 0:C * P],
                                  ALU.subtract).then_inc(s_ol[k], 1)

        x_ps = ps[:, 6:8, :].rearrange("p a b -> p (a b)")

        def ln_pe(pe, k):
            for t in range(T):
                pe.wait_ge(s_xn, T * k + t + 1)
                pe.transpose(ps[:, 6 + t // 4, (t % 4) * P:(t % 4 + 1) * P], xn[:, t, :], ident[:]).then_inc(s_xt, 1)

        def ln_act(act, k):
            act.wait_ge(s_xt, T * k + T)
            if k in (1, 3):
                act.activation(xnT, x_ps, ACT.Copy).then_inc(s_xf, 1)
            act.activation(xh[:, 0, :], x_ps, ACT.Copy).then_inc(s_xhi, 1)

        def ln_dve(dve, k):
            dve.wait_ge(s_xhi, k + 1)
            dve.tensor_tensor(xh[:, 1, :], x_ps, xh[:, 0, :], ALU.subtract).then_inc(s_xlo, 1)

        def router_pe(pe, k):
            pe.wait_ge(s_xf, k + 1)
            pe.wait_ge(dma["wr"], 16)
            for t in range(T):
                last = pe.matmul(ps[:, 5, t * 8:t * 8 + 8], xnT[:, t * P:t * P + P], wrt[:, k, :], start=True, stop=True)
            last.then_inc(s_rt[k], 1)

        LG, EX, GA, MA, MB, KM, CO, TM = range(8)

        def wide(ap):
            return ap.unsqueeze(2).to_broadcast([P, T, 8])

        def iota():
            return rows[:, ROW["iota"][0]:ROW["iota"][1]].unsqueeze(1).to_broadcast([P, T, 8])

        def gates_dve(dve, k, link):
            dve.wait_ge(s_rt[k], 1)
            lp = ps[:, 5, 0:T * 8].rearrange("p (t e) -> p t e", t=T)
            if k:
                br = rows[:, ROW["br"][0]:ROW["br"][1]].unsqueeze(1).to_broadcast([P, T, 8])
                link(dve.tensor_tensor(gt[:, LG], lp, br, ALU.add))
                lp = gt[:, LG]
            link(dve.tensor_reduce(g1[:, 0, :], lp, AX.X, ALU.max))
            dve.tensor_tensor(gt[:, LG], lp, wide(g1[:, 0, :]), ALU.subtract).then_inc(s_gm[k], 1)
            dve.wait_ge(s_ge[k], 1)
            link(dve.tensor_reduce(g1[:, 1, :], gt[:, EX], AX.X, ALU.add))
            link(dve.reciprocal(g1[:, 2, :], g1[:, 1, :]))
            link(dve.tensor_tensor(gt[:, GA], gt[:, EX], wide(g1[:, 2, :]), ALU.mult))
            for t in range(T):
                last = dve.max(g8[:, 0, t, :], gt[:, GA, t, :])
            link(last)
            for t in range(T):
                last = dve.max_index(gi[:, t, :], g8[:, 0, t, :], gt[:, GA, t, :])
            link(last)
            link(dve.tensor_copy(g8[:, 1], gi[:]))
            first = dve.tensor_tensor(gt[:, MA], iota(), wide(g8[:, 1, :, 0]), ALU.is_equal)
            if k:
                first.then_inc(s_mk[1], 1)
            else:
                link(first)
                link(dve.tensor_tensor(gt[:, MB], iota(), wide(g8[:, 1, :, 1]), ALU.is_equal))
                link(dve.tensor_tensor(gt[:, MA], gt[:, MA], gt[:, MB], ALU.add))
                dve.tensor_copy(maskb[:], gt[:, MA]).then_inc(s_mk[0], 1)

        def gates_act(act, k):
            act.wait_ge(s_gm[k], 1)
            act.activation(gt[:, EX], gt[:, LG], ACT.Exp).then_inc(s_ge[k], 1)

        block = ctx.enter_context(nc.Block())

        @block.sync
        def _(sp):
            for name, dst, src in (
                ("wk", wk, wk_d), ("rows", rows[:], rows_d.partition_broadcast(P)), ("ctx", ctxT, ctx_d),
                ("ident", ident[:], ident_d), ("x", x[:], x_d.rearrange("(t p) d -> p t d", p=P)), ("wv", wv, wv_d), ("wq", wq, wq_d),
                ("tri", tri, tri_d), ("fm", fm[:], fm_d),
                ("wo", wo.rearrange("p (c d) -> p c d", d=D), wo_d.rearrange("(c p) d -> p c d", p=P)),
            ):
                sp.dma_start(dst, src).then_inc(dma[name], 16)
            sp.dma_start(wrt[:, 0, :], wrouter_d).then_inc(dma["wr"], 16)
            sp.dma_start(wrt[:, 1, :], wr_d).then_inc(dma["wr2"], 16)
            sp.dma_start(b1c[:], b1_d).then_inc(dma["b1"], 16)
            sp.dma_start(b2s[:], b2_d).then_inc(dma["b2"], 16)
            sp.wait_ge(s_clo, 3)
            sp.wait_ge(s_wlo, 2)
            sp.dma_start(wdf, wdown_d.rearrange("p c n -> p (c n)")).then_inc(dma["wdown"], 16)
            sp.dma_start(wgf, wgate_d).then_inc(dma["wgate"], 16)
            sp.dma_start(fcf.rearrange("p (c d) -> p c d", d=D), fcw_d).then_inc(dma["fcw"], 16)
            maxima_to_stacks(sp, 0)
            sp.wait_ge(s_zqb, 1)
            sp.wait_ge(s_fq, 4)
            sp.wait_ge(s_qd, 6)
            sp.wait_ge(s_qa, 4)
            for e in range(E1):
                if e == 2:
                    maxima_to_stacks(sp, 1)
                if e >= 2:
                    sp.wait_ge(s_wl, 2 * (e - 1))
                sp.dma_start(w1f[:, e % 2, 0, :], w1_d[e]).then_inc(dma_e[e % 2], 16)
                sp.dma_start(w1f[:, e % 2, 1, :].rearrange("p (c d) -> p c d", c=HC1), w2_d[e]).then_inc(dma_e[e % 2], 16)
            sp.wait_ge(s_x, 5)
            sp.dma_start(out_d.rearrange("(t p) d -> p t d", p=P), x[:]).then_inc(s_fin, 16)
            sp.wait_ge(s_fin, 16)

        def heads(ap):
            return ap.rearrange("p (h d) -> p h d", d=HD)

        def bc(ap, shape, axis):
            return ap.unsqueeze(axis).to_broadcast(shape)

        @block.vector
        def _(dve):
            links = [0]

            def link(ins):
                links[0] += 1
                ins.then_inc(s_dve, 1)
                dve.wait_ge(s_dve, links[0])

            def rsqrt_newton(y, v, t):
                link(dve.tensor_tensor(t, y, y, ALU.mult))
                link(dve.scalar_tensor_tensor(out=t, in0=t, scalar=-0.5, in1=v, op0=ALU.mult, op1=ALU.mult))
                return dve.scalar_tensor_tensor(out=y, in0=t, scalar=1.5, in1=y, op0=ALU.add, op1=ALU.mult)

            def layernorm(k):
                for t in range(T):
                    i = dve.bn_stats(st[:, t, :], x[:, t, :])
                link(i)
                for t in range(T):
                    i = dve.bn_aggr(mv[:, t, :], st[:, t, :])
                link(i)
                dve.tensor_scalar(lnv[:, 0, :], mv[:, :, 1], 1.0, EPS, ALU.mult, ALU.add).then_inc(s_lv, 1)
                dve.wait_ge(s_ly, k + 1)
                link(rsqrt_newton(lnv[:, 1, :], lnv[:, 0, :], lnv[:, 2, :]))
                for t in range(T):
                    dve.tensor_scalar(xn[:, t, :], x[:, t, :], mv[:, t, 0:1], lnv[:, 1, t:t + 1],
                                      ALU.subtract, ALU.mult).then_inc(s_xn, 1)

            def centre(w, i):
                link(dve.tensor_reduce(hmean[:, i, :], heads(w), AX.X, ALU.add, negate=True))
                link(dve.tensor_scalar(hmean[:, i, :], hmean[:, i, :], 1.0 / HD, None, ALU.mult))
                ins = dve.tensor_tensor(heads(w), heads(w), bc(hmean[:, i, :], [P, NH, HD], 2), ALU.add)
                ins.then_inc(s_wc, 1)

            def split_lo(w, k):
                dve.tensor_tensor(wsp[:, k, 1, :], w, wsp[:, k, 0, :], ALU.subtract).then_inc(s_wlo, 1)

            dve.wait_ge(dma["wk"], 16)
            centre(wk, 0)
            dve.wait_ge(dma["rows"], 16)
            s = HD ** -0.5
            a, c, tmp, beta, beta2 = (co[:, i, :] for i in range(5))
            L = HD - 1
            dve.scalar_tensor_tensor(out=a, in0=row("gk"), scalar=s, in1=row("gq"), op0=ALU.mult, op1=ALU.mult)
            dve.scalar_tensor_tensor(out=c, in0=row("gk"), scalar=s, in1=row("bq"), op0=ALU.mult, op1=ALU.mult)
            dve.scalar_tensor_tensor(out=beta, in0=row("bk"), scalar=s, in1=row("gq"), op0=ALU.mult, op1=ALU.mult)
            link(dve.scalar_tensor_tensor(out=tmp, in0=row("bk"), scalar=s, in1=row("bq"), op0=ALU.mult, op1=ALU.mult))
            link(dve.tensor_scalar(beta[:, 0:L], beta[:, 0:L], beta[:, L:HD], None, ALU.subtract))
            link(dve.tensor_reduce(beta[:, L:HD], tmp, AX.X, ALU.add))
            dve.tensor_copy(beta2[:, 0:L], beta[:, 0:L])
            dve.memset(beta2[:, L:HD], -1.0).then_inc(s_beta, 1)
            dve.wait_ge(s_wc, 1)
            wkm3 = heads(wkm)
            link(dve.tensor_tensor(wkm3, heads(wk), bc(c, [P, NH, HD], 1), ALU.mult))
            link(dve.tensor_reduce(hmean[:, 0, :], wkm3, AX.X, ALU.add))
            dve.wait_ge(s_whi, 1)
            split_lo(wk, 1)
            link(dve.tensor_tensor(wkm3, heads(wk), bc(a, [P, NH, HD], 1), ALU.mult))
            link(dve.tensor_tensor(wkm3[:, :, 0:L], wkm3[:, :, 0:L],
                                   wkm3[:, :, L:HD].to_broadcast([P, NH, L]), ALU.subtract))
            dve.tensor_copy(wkm3[:, :, L], hmean[:, 0, :]).then_inc(s_wkm, 1)
            dve.wait_ge(s_betaT, 1)
            dve.tensor_copy(coc[:], ps[:, 6, 0:1]).then_inc(s_coc, 1)
            dve.wait_ge(s_wkm, 1)
            dve.wait_ge(s_whi, 3)
            split_lo(wkm, 2)

            def statistics(n):
                kind, i = JOBS[n]
                dst = ssk[:, 0, i, :] if kind == "kv" else ssq[:, 0, i, :]
                dve.wait_ge(s_sqr, n + 1)
                link(dve.tensor_reduce(dst, heads(sq[:, n % 2, :]), AX.X, ALU.add))
                dve.tensor_scalar(dst, dst, 1.0 / HD, EPS, ALU.mult, ALU.add).then_inc(s_ss, 1)

            def normalised(n):
                kind, i = JOBS[n]
                dve.wait_ge(s_ry, n + 1)
                if kind == "kv":
                    link(rsqrt_newton(ssk[:, 1, i, :], ssk[:, 0, i, :], ssk[:, 2, i, :]))
                    dve.wait_ge(s_proj, PROJ.index(("km", i)) + 1)
                    if i == 2:
                        dve.wait_ge(s_kt, NG)
                    pk = pair_of("km", i).rearrange("p a (h d) -> p (a h) d", d=HD)
                    dve.tensor_tensor(km[:, i % 2, :, 0, :], pk, bc(ssk[:, 1, i, :], [P, NH, HD], 2),
                                      ALU.mult).then_inc(s_km, 1)
                else:
                    link(rsqrt_newton(ssq[:, 1, i, :], ssq[:, 0, i, :], ssq[:, 2, i, :]))
                    if i >= 2:
                        dve.wait_ge(s_qh, i - 1)
                        dve.wait_ge(s_ql, i - 1)
                    pq = pair_of("q", i).rearrange("p a (h d) -> p (a h) d", d=HD)
                    dve.tensor_tensor(qn[:, i % 2, :, :], pq, bc(ssq[:, 1, i, :], [P, NH, HD], 2),
                                      ALU.mult).then_inc(s_qn, 1)

            for n in range(NJ + 2):
                if n < NJ:
                    statistics(n)
                if 0 <= n - 1 < NJ:
                    normalised(n - 1)
                if n < NJ and JOBS[n][0] == "kv":
                    c = JOBS[n][1]
                    dve.wait_ge(s_vh, c + 1)
                    v = vc if c % 2 else va
                    pv = pair_of("v", c).rearrange("p a (h d) -> p (a h) d", d=HD)
                    dve.tensor_tensor(v[:, 1, c // 2, :, 0:HD], pv, v[:, 0, c // 2, :, 0:HD],
                                      ALU.subtract).then_inc(s_vl, 1)
                if n == 0:
                    dve.wait_ge(dma["wq"], 16)
                    centre(wq, 1)
                    dve.wait_ge(dma["x"], 16)
                    layernorm(0)
                if n == 1:
                    dve.wait_ge(s_xhi, 1)
                    dve.tensor_tensor(xh[:, 1, :], x_ps, xh[:, 0, :], ALU.subtract).then_inc(s_xlo, 1)
            attention_dve(dve, 0, link)
            dve.wait_ge(s_pve[0], B * NH)
            link(dve.reciprocal(rsum[:], osum[:, :, :, HD]))
            project_out_dve(dve, 0, osum[:, :, :, 0:HD], rsum)
            for u in range(2):
                dve.wait_ge(s_wo[0], TB * (u + 1))
                dve.wait_ge(s_bo, 2)
                xs = x[:, TB * u:TB * u + TB, :]
                dve.scalar_tensor_tensor(out=xs, in0=ps[:, 4 + u, :].rearrange("p (t d) -> p t d", t=TB),
                                         scalar=th[:, 0:1], in1=xs, op0=ALU.mult, op1=ALU.add).then_inc(s_x, 1)

            dve.memset(kT1[QM[1]:QM[1] + 2, 0], -1.0).then_inc(s_m1, 1)

            dve.wait_ge(s_x, 2)
            layernorm(1)
            ln_dve(dve, 1)
            gates_dve(dve, 0, link)
            dve.wait_ge(s_cum, 1)
            cum = ps[:, 4, 0:T * 8].rearrange("p (t e) -> p t e", t=T)
            link(dve.scalar_tensor_tensor(out=gt[:, KM], in0=cum, scalar=float(CAP), in1=gt[:, MA],
                                          op0=ALU.is_le, op1=ALU.mult))
            link(dve.tensor_tensor(gt[:, KM], gt[:, KM], gt[:, GA], ALU.mult))
            link(dve.tensor_reduce(g1[:, 0, :], gt[:, KM], AX.X, ALU.add))
            link(dve.tensor_scalar(g1[:, 0, :], g1[:, 0, :], 1.0, 1e-6, ALU.mult, ALU.add))
            link(dve.reciprocal(g1[:, 1, :], g1[:, 0, :]))
            link(dve.tensor_scalar(g1[:, 1, :], g1[:, 1, :], th[:, 2:3], 1.0 / WS, ALU.mult, ALU.mult))
            link(dve.tensor_tensor(gt[:, CO], gt[:, KM], wide(g1[:, 1, :]), ALU.mult))
            for c in range(2):
                dve.wait_ge(s_h0, c + 1)
                dve.tensor_tensor(hh0[:, c, 1, :], hs[:, c, :], hh0[:, c, 0, :], ALU.subtract).then_inc(s_l0, 1)
            for t in range(T):
                dve.wait_ge(s_y0, t + 1)
                if t >= 2:
                    dve.wait_ge(s_x0, t - 1)
                dve.tensor_tensor(yw[:, t % 2], ps[:, 2 * (t % 2):2 * (t % 2) + 2, :].rearrange("p a (e d) -> p (a e) d", d=D),
                                  bc(gt[:, CO, t, :], [P, E0, D], 2), ALU.mult).then_inc(s_yw, 1)
                if t == 0:
                    dve.wait_ge(s_zk, 1)
                    fmb = row("fmb").unsqueeze(1).to_broadcast([P, 2 * B, D])
                    dve.tensor_tensor(zk.rearrange("p c h d -> p c (h d)"), ps[:, 5, :].rearrange("p (c n) -> p c n", n=D),
                                      fmb, ALU.add).then_inc(s_zb, 1)
                if t == 2:
                    dve.wait_ge(s_ka, 1)
                    dve.tensor_tensor(rk, fk, ks[:, :, :, 0, :], ALU.subtract).then_inc(s_kd, 1)
                if t == 3:
                    dve.wait_ge(s_ka, 5)
                    link(dve.tensor_tensor(ks[:, :, :, 4, :], rk, ks[:, :, :, 1, :], ALU.subtract))
                    dve.wait_ge(s_v1, 4)
                    for c in range(2 * B):
                        v = (vc1 if c % 2 else va1)[:, c // 2]
                        for part, slot in enumerate((0, 1, 4)):
                            last = dve.tensor_copy(v[:, :, part, 0:FD], ks[:, c, :, slot, :])
                    last.then_inc(s_kd, 1)

            dve.wait_ge(s_x0, T)
            layernorm(2)
            ln_dve(dve, 2)
            dve.wait_ge(s_zq, 1)
            fmb = row("fmb").unsqueeze(1).to_broadcast([P, T, D])
            dve.tensor_tensor(zq.rearrange("p t h d -> p t (h d)"), ps[:, 0:2, :].rearrange("p a (t n) -> p (a t) n", n=D),
                              fmb, ALU.add).then_inc(s_zqb, 1)
            for b in range(B):
                ts = slice(TB * b, TB * b + TB)
                dve.wait_ge(s_qa, 2 * b + 1)
                link(dve.tensor_tensor(rq[:, ts], fq[:, ts], qs1[:, ts, :, 0, :], ALU.subtract))
                dve.tensor_copy(qs1[:, ts, :, 2, :], rq[:, ts]).then_inc(s_qd, 1)
                dve.wait_ge(s_qd, 3 * b + 1)
                dve.tensor_tensor(qs1[:, ts, :, 5, :], rq[:, ts], qs1[:, ts, :, 2, :], ALU.subtract).then_inc(s_qd, 1)
                dve.tensor_copy(qs1[:, ts, :, 3, :], qs1[:, ts, :, 2, :]).then_inc(s_qd, 1)
            attention_dve(dve, 1, link)
            for b in range(B):
                ts = slice(TB * b, TB * b + TB)
                dve.wait_ge(s_pve[1], NH * (b + 1))
                link(dve.tensor_reduce(os1[:, ts].rearrange("p t h d -> p (t h) d"),
                                       osum1[:, ts].rearrange("p t h (a d) -> p (t h) d a", a=3), AX.X, ALU.add))
            link(dve.reciprocal(rsum[:], os1[:, :, :, FD]))
            project_out_dve(dve, 1, os1[:, :, :, 0:FD], rsum)
            for u in range(2):
                dve.wait_ge(s_wo[1], TB * (u + 1))
                dve.wait_ge(s_bo, 4)
                xs = x[:, TB * u:TB * u + TB, :]
                dve.scalar_tensor_tensor(out=xs, in0=ps[:, 4 + u, :].rearrange("p (t d) -> p t d", t=TB),
                                         scalar=th[:, 1:2], in1=xs, op0=ALU.mult, op1=ALU.add).then_inc(s_x, 1)

            dve.wait_ge(s_x, 4)
            layernorm(3)
            ln_dve(dve, 3)
            gates_dve(dve, 1, link)
            for u in range(2):
                dve.wait_ge(s_mT, T)
                dve.tensor_copy(maskT[:, u * 512:u * 512 + 512], ps[0:E1, 6 + u, :]).then_inc(s_mTe, 1)
            dve.wait_ge(s_b2, 1)
            dve.tensor_copy(acc, ps[:, 4:6, :].rearrange("p a (t d) -> p (a t) d", d=D)).then_inc(s_ac, 1)

            def weights_lo(e):
                dve.wait_ge(s_wh, 2 * (e + 1))
                for w in range(2):
                    dve.tensor_tensor(w1s[:, e % 4, 1, 512 * w:512 * w + 512], w1f[:, e % 2, w, :],
                                      w1s[:, e % 4, 0, 512 * w:512 * w + 512], ALU.subtract).then_inc(s_wl, 1)

            weights_lo(0)
            weights_lo(1)
            for n in range(HC1 * (E1 + 1)):
                e, c = n // HC1, n % HC1
                if e < E1:
                    dve.wait_ge(s_h1h, n + 1)
                    if e >= 2 and c == 0:
                        dve.wait_ge(s_y1, e - 1)
                    dve.tensor_tensor(hh1[:, e % 2, c, 1, :], h32[:, n % 2, :], hh1[:, e % 2, c, 0, :],
                                      ALU.subtract).then_inc(s_h1l, 1)
                if c == 3 and e + 2 < E1:
                    weights_lo(e + 2)
                if c == 2 and e >= 1:
                    f = e - 1
                    dve.wait_ge(s_y1, f + 1)
                    link(dve.tensor_tensor(yt[:, f % 2], ps[:, 4 + 2 * (f % 2):6 + 2 * (f % 2), :]
                                           .rearrange("p a (t d) -> p (a t) d", d=D),
                                           bc(gt[:, MA, :, f], [P, T, D], 2), ALU.mult))
                    dve.tensor_tensor(acc, acc, yt[:, f % 2], ALU.add).then_inc(s_ac, 1)
                    dve.wait_ge(s_ac, f + 2)
            dve.scalar_tensor_tensor(out=x[:], in0=acc, scalar=th[:, 3:4], in1=x[:], op0=ALU.mult,
                                     op1=ALU.add).then_inc(s_x, 1)

        @block.gpsimd
        def _(pool):
            pool.memset(qs[:, :, :, 0, HD - 1:HD], 1.0).then_inc(s_ones, 1)
            pool.memset(qs[:, :, :, 1, HD - 1:HD], 0.0).then_inc(s_ones, 1)
            for v in (va, vc):
                pool.memset(v[:, 0, :, :, HD:HD + 1], 1.0).then_inc(s_ones, 1)
                pool.memset(v[:, 1, :, :, HD:HD + 1], 0.0).then_inc(s_ones, 1)

            def cast(dst, src):
                return pool.tensor_scalar(dst, src, 1.0, 0.0, ALU.mult, ALU.add)

            pool.wait_ge(dma["ident"], 16)
            cast(ident16[:], ident[:]).then_inc(s_cst, 1)
            cast(identb[:], ident[:]).then_inc(s_cst, 1)
            pool.wait_ge(dma["tri"], 16)
            cast(trib[:], tri).then_inc(s_cst, 1)
            pool.memset(onesb[:], 1.0).then_inc(s_cst, 1)
            pool.wait_ge(s_chi, 1)
            pool.tensor_tensor(c16[:, 1, :], ctxT.rearrange("p a b -> p (a b)"), c16[:, 0, :],
                               ALU.subtract).then_inc(s_clo, 1)
            pool.wait_ge(s_whi, 2)
            pool.tensor_tensor(wsp[:, 3, 1, :], wv, wsp[:, 3, 0, :], ALU.subtract).then_inc(s_clo, 1)
            pool.wait_ge(s_whi, 4)
            pool.tensor_tensor(wsp[:, 0, 1, :], wq, wsp[:, 0, 0, :], ALU.subtract).then_inc(s_clo, 1)
            pool.memset(km[:, :, :, 1, HD - 1:HD], 0.0).then_inc(s_ones, 1)
            for n in range(NJ + 2):
                if 0 <= n - 1 < NJ and JOBS[n - 1][0] == "kv":
                    c = JOBS[n - 1][1]
                    pool.wait_ge(s_km, c + 1)
                    if c == 2:
                        pool.wait_ge(s_kt, NG)
                    cast(km[:, c % 2, :, 1, 0:HD - 1], km[:, c % 2, :, 0, 0:HD - 1]).then_inc(s_km2, 1)
                if n in KTJOB:
                    g = KTJOB.index(n)
                    pool.wait_ge(s_kf, g + 1)
                    b, h = g // NG, G * (g % NG)
                    pool.wait_ge(s_kh, g + 1)
                    pool.tensor_tensor(kT[:, 1, b, h:h + G, :], kf[:, g % 2, :, :], kT[:, 0, b, h:h + G, :],
                                       ALU.subtract).then_inc(s_kl, 1)
                if 0 <= n - 2 < NJ and JOBS[n - 2][0] == "q":
                    t = JOBS[n - 2][1]
                    pool.wait_ge(s_qh, t + 1)
                    pool.tensor_tensor(qs[:, t, :, 1, 0:HD - 1], qn[:, t % 2, :, 0:HD - 1],
                                       qs[:, t, :, 0, 0:HD - 1], ALU.subtract).then_inc(s_ql, 1)
            attention_pool(pool, 0)
            pool.wait_ge(s_whi, 5)
            pool.tensor_tensor(wsp[:, 4, 1, :], wo, wsp[:, 4, 0, :], ALU.subtract).then_inc(s_clo, 1)
            pool.wait_ge(s_tanh, 1)
            pool.wait_ge(s_xn, T)
            pool.tensor_scalar(obo[:, 0, :], row("bo"), th[:, 0:1], 0.0, ALU.mult, ALU.add).then_inc(s_bo, 1)
            pool.wait_ge(s_bo, 1)
            pool.tensor_tensor(x[:], x[:], obo[:, 0, :].unsqueeze(1).to_broadcast([P, T, D]), ALU.add).then_inc(s_bo, 1)


            links = [0]

            def link(ins):
                links[0] += 1
                ins.then_inc(s_pool, 1)
                pool.wait_ge(s_pool, links[0])

            pool.wait_ge(dma["wgate"], 16)
            pool.wait_ge(dma["wdown"], 16)
            pool.wait_ge(s_qt[0], 2 * GT)
            wd_hi, wd_lo = (wds[:, w].rearrange("p c n -> p (c n)") for w in range(2))
            for w, hi, lo in ((wgf, wgs[:, 0, :], wgs[:, 1, :]), (wdf, wd_hi, wd_lo)):
                pool.tensor_scalar(hi, w, WS, 0.0, ALU.mult, ALU.add)
                link(pool.tensor_scalar(w, w, WS, 0.0, ALU.mult, ALU.add))
                pool.tensor_tensor(lo, w, hi, ALU.subtract).then_inc(s_wg, 1)
            pool.wait_ge(dma["fcw"], 16)
            pool.wait_ge(dma["fm"], 16)
            cast(fms[:, 0, :], fm[:])
            link(cast(fcs[:, 0, :], fcf))
            pool.tensor_tensor(fms[:, 1, :], fm[:], fms[:, 0, :], ALU.subtract).then_inc(s_fms, 1)
            pool.tensor_tensor(fcs[:, 1, :], fcf, fcs[:, 0, :], ALU.subtract).then_inc(s_fms, 1)
            pool.wait_ge(s_pv[0], B * NH)
            for v in (va1, vc1):
                pool.memset(v[:, :, :, 0, FD:V1], 1.0).then_inc(s_v1, 1)
                pool.memset(v[:, :, :, 1:3, FD:V1], 0.0).then_inc(s_v1, 1)
            for t in range(T):
                pool.wait_ge(s_yw, t + 1)
                for half in (4, 2, 1):
                    link(pool.tensor_tensor(yw[:, t % 2, 0:half, :], yw[:, t % 2, 0:half, :],
                                            yw[:, t % 2, half:2 * half, :], ALU.add))
                pool.tensor_tensor(x[:, t, :], x[:, t, :], yw[:, t % 2, 0, :], ALU.add).then_inc(s_x0, 1)
            pool.wait_ge(s_xn, 2 * T + T)
            pool.tensor_scalar(obo[:, 1, :], row("fcb"), th[:, 1:2], 0.0, ALU.mult, ALU.add).then_inc(s_bo, 1)
            pool.wait_ge(s_bo, 3)
            pool.tensor_tensor(x[:], x[:], obo[:, 1, :].unsqueeze(1).to_broadcast([P, T, D]), ALU.add).then_inc(s_bo, 1)
            for b in range(B):
                ts = slice(TB * b, TB * b + TB)
                pool.wait_ge(s_fq, 2 * b + 2)
                cast(qs1[:, ts, :, 1, :], fq[:, ts]).then_inc(s_qp, 1)
            attention_pool(pool, 1)
            for n in range(HC1 * E1):
                e, c = n // HC1, n % HC1
                pool.wait_ge(s_h1, n + 1)
                if e >= 2 and c == 0:
                    pool.wait_ge(s_y1, e - 1)
                cast(hh1[:, e % 2, c, 0, :], h32[:, n % 2, :]).then_inc(s_h1h, 1)

        @block.scalar
        def _(act):
            links = [0]

            def link(ins):
                links[0] += 1
                ins.then_inc(s_act, 1)
                act.wait_ge(s_act, links[0])

            def rsqrt_first(y, v):
                link(act.activation(y, v, ACT.Ln))
                return act.activation(y, y, ACT.Exp, scale=-0.5)

            act.preload_act_table(ACT.Tanh)
            act.wait_ge(dma["rows"], 16)
            act.activation(th[:], rows[:, ROW["gx"][0]:ROW["gf"][1]], ACT.Tanh).then_inc(s_tanh, 1)
            act.preload_act_table_set("natural_log_exp_and_others")
            act.wait_ge(dma["ctx"], 16)
            act.activation(c16[:, 0, :], ctxT.rearrange("p a b -> p (a b)"), ACT.Copy).then_inc(s_chi, 1)
            act.wait_ge(s_wc, 1)
            act.activation(wsp[:, 1, 0, :], wk, ACT.Copy).then_inc(s_whi, 1)
            act.wait_ge(dma["wv"], 16)
            act.activation(wsp[:, 3, 0, :], wv, ACT.Copy).then_inc(s_whi, 1)
            act.wait_ge(s_wkm, 1)
            act.activation(wsp[:, 2, 0, :], wkm, ACT.Copy).then_inc(s_whi, 1)

            for n in range(NJ + 2):
                if n < NJ:
                    kind, i = JOBS[n]
                    what = "k" if kind == "kv" else "q"
                    act.wait_ge(s_proj, PROJ.index((what, i)) + 1)
                    if n >= 2:
                        act.wait_ge(s_ss, n - 1)
                    act.activation(sq[:, n % 2, :], pair_of(what, i).rearrange("p a b -> p (a b)"),
                                   ACT.Square).then_inc(s_sqr, 1)
                if 0 <= n - 1 < NJ:
                    kind, i = JOBS[n - 1]
                    act.wait_ge(s_ss, n)
                    st_ = ssk if kind == "kv" else ssq
                    rsqrt_first(st_[:, 1, i, :], st_[:, 0, i, :]).then_inc(s_ry, 1)
                if n < NJ and JOBS[n][0] == "kv":
                    c = JOBS[n][1]
                    act.wait_ge(s_proj, PROJ.index(("v", c)) + 1)
                    v = vc if c % 2 else va
                    pv = pair_of("v", c).rearrange("p a (h d) -> p (a h) d", d=HD)
                    act.activation(v[:, 0, c // 2, :, 0:HD], pv, ACT.Copy).then_inc(s_vh, 1)
                if n == 0:
                    act.wait_ge(s_wc, 2)
                    act.activation(wsp[:, 0, 0, :], wq, ACT.Copy).then_inc(s_whi, 1)
                    act.wait_ge(s_lv, 1)
                    rsqrt_first(lnv[:, 1, :], lnv[:, 0, :]).then_inc(s_ly, 1)
                if n == 1:
                    act.wait_ge(s_xt, T)
                    act.activation(xh[:, 0, :], x_ps, ACT.Copy).then_inc(s_xhi, 1)
                if 0 <= n - 2 < NJ and JOBS[n - 2][0] == "q":
                    t = JOBS[n - 2][1]
                    act.wait_ge(s_qn, t + 1)
                    act.activation(qs[:, t, :, 0, 0:HD - 1], qn[:, t % 2, :, 0:HD - 1], ACT.Copy).then_inc(s_qh, 1)
                if n in KTJOB:
                    g = KTJOB.index(n)
                    act.wait_ge(s_coc, 1)
                    act.wait_ge(s_kt, g + 1)
                    if g >= 2:
                        act.wait_ge(s_kl, g - 1)
                    act.activation(kf[:, g % 2, :, :].rearrange("p (a h) k -> p a (h k)", a=2),
                                   ps[:, 6:8, 0:2 * KW], ACT.Identity, bias=coc[:]).then_inc(s_kf, 1)
                    act.wait_ge(s_kf, g + 1)
                    b, h = g // NG, G * (g % NG)
                    act.activation(kT[:, 0, b, h:h + G, :], kf[:, g % 2, :, :], ACT.Copy).then_inc(s_kh, 1)
                if n == NJ - 2:
                    act.wait_ge(dma["wo"], 16)
                    act.activation(wsp[:, 4, 0, :], wo, ACT.Copy).then_inc(s_whi, 1)
            attention_act(act, 0)
            project_out_act(act, 0)

            def layernorm(k):
                act.wait_ge(s_lv, k + 1)
                rsqrt_first(lnv[:, 1, :], lnv[:, 0, :]).then_inc(s_ly, 1)
                ln_act(act, k)

            layernorm(1)
            gates_act(act, 0)
            act.preload_act_table(ACT.Silu)
            for c in range(2):
                act.wait_ge(s_hp, c + 1)
                act.activation(hs[:, c, :], ps[:, 2 * c:2 * c + 2, :].rearrange("p a b -> p (a b)"), ACT.Silu,
                               scale=1.0 / WS).then_inc(s_hs, 1)
                act.wait_ge(s_hs, c + 1)
                act.activation(hh0[:, c, 0, :], hs[:, c, :], ACT.Copy).then_inc(s_h0, 1)
            act.preload_act_table_set("natural_log_exp_and_others")
            act.wait_ge(s_zb, 1)
            act.activation(fk[:, :, :, 0:8], zk, ACT.Exp).then_inc(s_fk, 1)
            act.activation(fk[:, :, :, 8:16], zk, ACT.Exp, scale=-1.0).then_inc(s_fk, 1)
            act.wait_ge(s_fk, 2)
            for slot in (0, 2, 5):
                act.activation(ks[:, :, :, slot, :], fk, ACT.Copy).then_inc(s_ka, 1)
            act.wait_ge(s_kd, 1)
            for slot in (1, 3):
                act.activation(ks[:, :, :, slot, :], rk, ACT.Copy).then_inc(s_ka, 1)
            for g in range(GT):
                act.wait_ge(s_k1, g + 1)
                b, h = g // NG, G * (g % NG)
                act.activation(kT1[0:6 * FD, 0, b, h:h + G, :],
                               ps[:, 6 + g % 2, :].bitcast(BF16)[0:6 * FD, 0:G * KW].rearrange("p (h k) -> p h k", h=G),
                               ACT.Copy).then_inc(s_k1e, 1)
            layernorm(2)
            act.wait_ge(s_zqb, 1)
            for b in range(B):
                ts = slice(TB * b, TB * b + TB)
                act.activation(fq[:, ts, :, 0:8], zq[:, ts], ACT.Exp).then_inc(s_fq, 1)
                act.activation(fq[:, ts, :, 8:16], zq[:, ts], ACT.Exp, scale=-1.0).then_inc(s_fq, 1)
                act.wait_ge(s_fq, 2 * b + 2)
                act.activation(qs1[:, ts, :, 0, :], fq[:, ts], ACT.Copy).then_inc(s_qa, 1)
                act.activation(qs1[:, ts, :, 4, :], fq[:, ts], ACT.Copy).then_inc(s_qa, 1)
            attention_act(act, 1)
            project_out_act(act, 1)
            layernorm(3)
            gates_act(act, 1)
            act.preload_act_table(ACT.Gelu)

            def weights_hi(e):
                act.wait_ge(dma_e[e % 2], 32 * (e // 2 + 1))
                if e >= 4:
                    act.wait_ge(s_y1, e - 3)
                for w in range(2):
                    act.activation(w1s[:, e % 4, 0, 512 * w:512 * w + 512], w1f[:, e % 2, w, :], ACT.Copy).then_inc(s_wh, 1)

            weights_hi(0)
            weights_hi(1)
            for n in range(HC1 * E1):
                e, c = n // HC1, n % HC1
                act.wait_ge(s_h1p, n + 1)
                if n >= 2:
                    act.wait_ge(s_h1l, n - 1)
                act.activation(h32[:, n % 2, :], ps[:, 2 * (n % 2):2 * (n % 2) + 2, :].rearrange("p a b -> p (a b)"),
                               ACT.Gelu, bias=b1c[:, e, c:c + 1]).then_inc(s_h1, 1)
                if c == 2 and e + 2 < E1:
                    weights_hi(e + 2)

        @block.tensor
        def _(pe):
            pe.wait_ge(dma["ident"], 16)
            pe.wait_ge(s_beta, 1)
            pe.transpose(ps[:, 6, 0:P], co[:, 3:5, :].rearrange("p a d -> p (a d)"), ident[:]).then_inc(s_betaT, 1)

            def project(n, xs, k):
                for half in range(2):
                    for i, (a, w) in enumerate(((0, 0), (0, 1), (1, 0))):
                        last = pe.matmul(pair(n)[:, half, :], xs[a], wsp[:, k, w, half * 512:half * 512 + 512],
                                         start=(i == 0), stop=(i == 2))
                last.then_inc(s_proj, 1)

            def keys_transposed(g):
                b, h0 = g // NG, G * (g % NG)
                if g == 0:
                    pe.wait_ge(s_ones, 7)
                    pe.wait_ge(s_xlo, 1)
                else:
                    pe.wait_ge(s_kf, g)
                pe.wait_ge(s_km2, 2 * b + 2)
                for j in range(G):
                    for c, (w, at) in enumerate(((KA, 0), (KCP, KA))):
                        o = (j % 2) * KW + at
                        last = pe.transpose(ps[:, 6 + j // 2, o:o + w],
                                            km[0:w, c, h0 + j].rearrange("p a d -> p (a d)"), ident[0:w, 0:w])
                last.then_inc(s_kt, 1)

            def banks_free(n):
                if n < 0:
                    return
                what, i = PROJ[n]
                if what == "k":
                    pe.wait_ge(s_sqr, job_of(what, i) + 1)
                elif what == "km":
                    pe.wait_ge(s_km, i + 1)
                elif what == "v":
                    pe.wait_ge(s_vl, i + 1)
                else:
                    pe.wait_ge(s_qn, i + 1)

            pe.wait_ge(s_chi, 1)
            for n, (what, i) in enumerate(PROJ):
                banks_free(n - 3)
                if n == 0:
                    pe.wait_ge(s_wlo, 1)
                    pe.wait_ge(s_clo, 1)
                if (what, i) == ("km", 0):
                    pe.wait_ge(s_wlo, 2)
                if (what, i) == ("v", 0):
                    pe.wait_ge(s_clo, 2)
                if (what, i) == ("q", 0):
                    pe.wait_ge(s_xlo, 1)
                    pe.wait_ge(s_clo, 3)
                if what == "q":
                    project(n, [xh[:, j, i * P:i * P + P] for j in range(2)], 0)
                else:
                    project(n, [c16[:, j, i * P:i * P + P] for j in range(2)], {"k": 1, "km": 2, "v": 3}[what])
                if (what, i) == ("v", 1):
                    pe.wait_ge(s_coc, 1)
                    ln_pe(pe, 0)
                if what in "qv" and job_of(what, i) in KTJOB:
                    keys_transposed(KTJOB.index(job_of(what, i)))
            keys_transposed(GT - 1)
            pe.wait_ge(s_qn, T)
            pe.wait_ge(s_ql, T)
            pe.wait_ge(s_kl, GT)
            pe.wait_ge(s_kf, GT)
            pe.wait_ge(s_ones, 6)
            pe.wait_ge(s_cst, 2)
            attention_pe(pe, 0)
            pe.wait_ge(s_clo, 4)
            project_out_pe(pe, 0, lambda w, c: wsp[:, 4, w, c * P:(c + 1) * P])

            HILO = ((0, 0), (0, 1), (1, 0))

            ln_pe(pe, 1)
            router_pe(pe, 0)
            pe.wait_ge(s_xlo, 2)
            pe.wait_ge(s_wg, 1)
            for c in range(2):
                for u in range(2):
                    for i, (w, a) in enumerate(HILO):
                        last = pe.matmul(ps[:, 2 * c + u, :], wgs[:, w, c * P:(c + 1) * P],
                                         xh[:, a, u * 512:u * 512 + 512], start=(i == 0), stop=(i == 2))
                last.then_inc(s_hp, 1)
            pe.wait_ge(s_mk[0], 1)
            for t in range(T):
                for u in range(t + 1):
                    last = pe.matmul(ps[:, 4, t * 8:t * 8 + 8], trib[:] if u == t else onesb[:], maskb[:, u, :],
                                     start=(u == 0), stop=(u == t))
            last.then_inc(s_cum, 1)
            pe.wait_ge(s_fms, 1)
            for c in range(2 * B):
                for i, (a, w) in enumerate(HILO):
                    last = pe.matmul(ps[:, 5, c * P:(c + 1) * P], c16[:, a, c * P:(c + 1) * P], fms[:, w, :],
                                     start=(i == 0), stop=(i == 2))
            last.then_inc(s_zk, 1)
            pe.wait_ge(s_l0, 2)
            pe.wait_ge(s_wg, 2)
            for t in range(T):
                if t >= 2:
                    pe.wait_ge(s_yw, t - 1)
                for u in range(2):
                    n = 0
                    for c in range(2):
                        for a, w in HILO:
                            last = pe.matmul(ps[:, 2 * (t % 2) + u, :], hh0[:, c, a, t * P:(t + 1) * P],
                                             wds[:, w, c, u * 512:u * 512 + 512], start=(n == 0), stop=(n == 5))
                            n += 1
                last.then_inc(s_y0, 1)
            for g in range(GT):
                if g == 0:
                    pe.wait_ge(s_ka, 5)
                    pe.wait_ge(s_kd, 2)
                if g >= 2:
                    pe.wait_ge(s_k1e, g - 1)
                o = ps[:, 6 + g % 2, :].bitcast(BF16)
                for j in range(G):
                    for c, (w, at) in enumerate(((KA, 0), (KCP, KA))):
                        last = pe.transpose(o[0:6 * FD, j * KW + at:j * KW + at + w],
                                            ks[0:w, 2 * (g // NG) + c, G * (g % NG) + j].rearrange("p a d -> p (a d)"),
                                            identb[0:w, 0:w])
                last.then_inc(s_k1, 1)
            pe.wait_ge(s_k1e, GT)
            ln_pe(pe, 2)
            pe.wait_ge(s_xlo, 3)
            for t in range(T):
                for i, (a, w) in enumerate(HILO):
                    last = pe.matmul(ps[:, t // 4, (t % 4) * P:(t % 4 + 1) * P], xh[:, a, t * P:(t + 1) * P], fms[:, w, :],
                                     start=(i == 0), stop=(i == 2))
            last.then_inc(s_zq, 1)
            pe.wait_ge(s_qd, 6)
            pe.wait_ge(s_qa, 4)
            pe.wait_ge(s_qp, 2)
            pe.wait_ge(s_m1, 1)
            attention_pe(pe, 1)
            project_out_pe(pe, 1, lambda w, c: fcs[:, w, c * P:(c + 1) * P])
            ln_pe(pe, 3)
            pe.wait_ge(dma["wr2"], 16)
            router_pe(pe, 1)
            pe.wait_ge(s_xlo, 4)
            pe.wait_ge(s_mk[1], 1)
            for t in range(T):
                pe.transpose(ps[0:E1, 6 + t // 4, (t % 4) * P:(t % 4 + 1) * P], gt[:, MA, t, :], ident[:]).then_inc(s_mT, 1)
            pe.wait_ge(s_mTe, 2)
            pe.wait_ge(dma["b2"], 16)
            for t in range(T):
                last = pe.matmul(ps[:, 4 + t // 4, (t % 4) * P:(t % 4 + 1) * P], maskT[:, t * P:(t + 1) * P], b2s[:],
                                 start=True, stop=True)
            last.then_inc(s_b2, 1)
            pe.wait_ge(dma["b1"], 16)
            for n in range(HC1 * (E1 + 1)):
                e, c = n // HC1, n % HC1
                if e < E1:
                    if c == 0:
                        pe.wait_ge(s_wl, 2 * (e + 1))
                    if n >= 2:
                        pe.wait_ge(s_h1, n - 1)
                    for u in range(2):
                        for i, (w, a) in enumerate(HILO):
                            last = pe.matmul(ps[:, 2 * (n % 2) + u, :], w1s[:, e % 4, w, c * P:(c + 1) * P],
                                             xh[:, a, u * 512:u * 512 + 512], start=(i == 0), stop=(i == 2))
                    last.then_inc(s_h1p, 1)
                if e >= 1:
                    f = e - 1
                    if c == 0:
                        pe.wait_ge(s_h1l, HC1 * e)
                        pe.wait_ge(s_ac, max(1, f))
                    for t in (2 * c, 2 * c + 1):
                        m = 0
                        for q in range(HC1):
                            for a, w in HILO:
                                last = pe.matmul(ps[:, 4 + 2 * (f % 2) + t // 4, (t % 4) * P:(t % 4 + 1) * P],
                                                 hh1[:, f % 2, q, a, t * P:(t + 1) * P],
                                                 w1s[:, f % 4, w, 512 + q * P:512 + (q + 1) * P],
                                                 start=(m == 0), stop=(m == 3 * HC1 - 1))
                                m += 1
                    if c == HC1 - 1:
                        last.then_inc(s_y1, 1)


NAMES = ("rows", "ident", "tri", "ctx", "wq", "wk", "wv", "wo", "fm", "wgate", "wdown", "wrouter",
         "fcw", "wr", "w1", "b1", "w2", "b2")


def laid_out(i):
    f = {k: np.asarray(v) for k, v in i.items()}
    row = np.zeros((1, ROWS), np.float32)
    for name, v in (("bo", f["L0_xattn_bo"]), ("gq", f["L0_xattn_q_gamma"]), ("bq", f["L0_xattn_q_beta"]),
                    ("gk", f["L0_xattn_k_gamma"]), ("bk", f["L0_xattn_k_beta"]), ("gx", f["g_xattn"]),
                    ("gf", f["g_ffn"]), ("fmb", np.tile(f["L1_xattn_fm_b"], NH)), ("fcb", f["L1_xattn_fc_b"]),
                    ("br", f["L1_ffn_br"]), ("iota", np.arange(8, dtype=np.float32))):
        row[0, ROW[name][0]:ROW[name][1]] = v
    c = f["ctx_1024"]
    tiles = []
    for b in range(B):
        tiles.append(c[b, :KA])
        tiles += [np.concatenate([c[b, KA:M], c[b, :KCP - KC]])] * G
    fm = np.zeros((NH, 8, NH, 8), np.float32)
    for h in range(NH):
        fm[h, :, h, :] = f["L1_xattn_fm_w"].T
    return {
        "x": f["x"].reshape(B * N, D), "rows": row, "ident": np.eye(P, dtype=np.float32),
        "tri": np.triu(np.ones((P, P), np.float32)),
        "ctx": np.concatenate(tiles).T.reshape(D, 2 * B, P),
        "wq": f["L0_xattn_Wq"], "wk": f["L0_xattn_Wk"], "wv": f["L0_xattn_Wv"], "wo": f["L0_xattn_Wo"],
        "fm": fm.reshape(P, P), "wgate": f["L0_ffn_w_gate"].T,
        "wdown": f["L0_ffn_w_down"].transpose(2, 0, 1).reshape(2, P, E0 * D).transpose(1, 0, 2),
        "wrouter": f["L0_ffn_w_router"].T, "fcw": f["L1_xattn_fc_w"].T.reshape(2, P, D).transpose(1, 0, 2),
        "wr": f["L1_ffn_Wr"], "w1": f["L1_ffn_W1"], "b1": f["L1_ffn_b1"].reshape(E1, HC1, P).transpose(2, 0, 1),
        "w2": f["L1_ffn_W2"].reshape(E1, HC1, P, D).transpose(0, 2, 1, 3), "b2": f["L1_ffn_b2"],
    }


def kernel(**inputs):
    from concourse import bacc
    from concourse.bass_utils import run_bass_kernel_spmd

    nc = bacc.Bacc("TRN2", target_bir_lowering=False, num_devices=1)
    arrays = {k: np.ascontiguousarray(v) for k, v in laid_out(inputs).items()}
    aps = {k: nc.dram_tensor(k + "_in", v.shape, mybir.dt.from_np(v.dtype), kind="ExternalInput").ap()
           for k, v in arrays.items()}
    out = nc.dram_tensor("out", (B * N, D), F32, kind="ExternalOutput").ap()
    build(nc, aps["x"], out, *[aps[k] for k in NAMES])
    r = run_bass_kernel_spmd(nc, [{k + "_in": v for k, v in arrays.items()}], core_ids=[0])
    return r.results[0]["out"].reshape(B, N, D)
```

```python
from contextlib import ExitStack

import numpy as np

import concourse.bass as bass
from concourse import mybir

ALU = mybir.AluOpType
ACT = mybir.ActivationFunctionType
AX = mybir.AxisListType
F32 = mybir.dt.float32
F16 = mybir.dt.float16
BF16 = mybir.dt.bfloat16
U32 = mybir.dt.uint32

P = 128
B, N, D = 2, 512, 128
M = 154
KA, KC, KCP = 128, 26, 32
KW = KA + KCP
TB = N // P
T = B * TB
NH, HD = 16, 64
G = 4
NG = NH // G
GT = B * NG
EPS = 1e-5
E0, F0, CAP = 8, 256, 160
E1, F1 = 8, 512
HC1 = F1 // P
FD = 16
NB = (N * B + E1 * (P - 1)) // P
WS = 64.0

ROW = {}
_at = 0
for _n, _w in (("bo", D), ("gq", HD), ("bq", HD), ("gk", HD), ("bk", HD), ("gx", 2), ("gf", 2),
               ("fmb", D), ("fcb", D), ("br", E1), ("iota", 8), ("k128", 8), ("before", 64), ("block", NB)):
    ROW[_n] = (_at, _at + _w)
    _at += _w
ROWS = _at


def build(nc, x_d, out_d, rows_d, ident_d, tri_d, ctx_d, wq_d, wk_d, wv_d, wo_d, fm_d,
          wgate_d, wdown_d, wrouter_d, fcw_d, wr_d, w1_d, b1_d, w2_d, b2_d):
    with ExitStack() as ctx:
        def sb(name, shape, dt=F32):
            return ctx.enter_context(nc.sbuf_tensor(name, shape, dt))

        def sem(name):
            return ctx.enter_context(nc.semaphore(name))

        x = sb("x", [P, T, D])
        rows = sb("rows", [P, ROWS])
        ident = sb("ident", [P, P])
        e32 = sb("e32", [P, G + 1, N])
        eh = sb("eh", [P, 2, G + 1, N], F16)
        el = sb("el", [P, 2, G + 1, N], F16)
        e_flat = e32[:].rearrange("p a b -> p (a b)")
        eh_flat = eh[:].rearrange("p z a b -> p (z a b)").bitcast(F32)
        xn = e_flat[:, 0:T * D].rearrange("p (t d) -> p t d", t=T)
        xnT = e_flat[:, T * D:2 * T * D]
        xh = el[:].rearrange("p z a b -> p (z a b)")[:, 0:2 * T * P].rearrange("p (z n) -> p z n", z=2)
        ctxT = eh_flat[:, 0:2 * B * P].rearrange("p (c k) -> p c k", k=P)
        tri = eh_flat[:, 1024:1152]
        stage = sb("stage", [P, 5120])
        wq, wk, wv, wo = (stage[:, 1024 * i:1024 * i + 1024] for i in range(4))
        wkm = stage[:, 4096:5120]
        fm = sb("fm", [P, D])

        def row(name):
            a, b = ROW[name]
            return rows[:, a:b]

        ident16 = sb("ident16", [P, P], F16)
        identb = sb("identb", [P, P], BF16)
        big = sb("big", [P, 5 * 2048 + T * NH * P], F16)
        wsp = big[:, 0:5 * 2048].rearrange("p (i v n) -> p i v n", i=5, v=2)
        c16 = sb("c16", [P, 2, 2 * B * P], F16)
        th = sb("th", [P, 4])
        hmean = sb("hmean", [P, 2, NH])
        co = sb("co", [P, 5, HD])
        coc = sb("coc", [P, 1])
        st = sb("st", [P, T, 6])
        mv = sb("mv", [P, T, 2])
        lnv = sb("lnv", [P, 3, T])
        work = sb("work", [P, T * NH * (HD + 1)])
        sq = work[:, 4096:6144].rearrange("p (z n) -> p z n", z=2)
        ssk = sb("ssk", [P, 3, 2 * B, NH])
        ssq = eh_flat[:, 1152:1152 + 3 * T * NH].rearrange("p (i t h) -> p i t h", i=3, t=T)
        km = work[:, 0:4096].rearrange("p (c h a d) -> p c h a d", c=2, h=NH, a=2)
        kT = sb("kT", [P, 2, B, NH, KW], F16)
        qn = work[:, 6144:8192].rearrange("p (z h d) -> p z h d", z=2, h=NH)
        qs = big[:, 5 * 2048:].rearrange("p (t h a d) -> p t h a d", t=T, h=NH, a=2)
        qT = sb("qT", [P, 3, G, N], F16)
        va = sb("va", [P, 2, B, NH, HD + 1], F16)
        vc = sb("vc", [P, 2, B, NH, HD + 1], F16)
        mx = sb("mx", [P, 2, TB, G])
        m12 = sb("m12", [P, 2, TB, 2, G], BF16)
        mT = sb("mT", [2 * G, 2, N], BF16)
        kf = e_flat[:, 0:2 * G * KW].rearrange("p (z h k) -> p z h k", z=2, h=G)
        osum = work[:].rearrange("p (t h d) -> p t h d", t=T, h=NH)
        rsum = sb("rsum", [P, T, NH])
        obo = sb("obo", [P, 2, D])
        wrt = sb("wrt", [P, 2, 8])
        b1c = sb("b1c", [P, E1, HC1])
        b2s = sb("b2s", [E1, D])
        trib = sb("trib", [P, P], BF16)
        onesb = sb("onesb", [P, P], BF16)
        wgs = sb("wgs", [P, 2, F0], F16)
        fcs = sb("fcs", [P, 2, 2 * D], F16)
        gt = sb("gt", [P, 8, T, 8])
        g1 = sb("g1", [P, 4, T])
        g8 = sb("g8", [P, 2, T, 8])
        gi = sb("gi", [P, T, 8], U32)
        maskb = sb("maskb", [P, T, 8], BF16)
        maskT = work[0:E1, 5120:6144]
        qs_flat = big[:, 5 * 2048:]
        wdf, wgf, fcf = stage[:, 0:2048], stage[:, 2048:2304], stage[:, 2304:2560]
        wds = qs_flat[:, 4096:8192].rearrange("p (v c n) -> p v c n", v=2, c=2)
        hs = work[:, 0:2048].rearrange("p (c n) -> p c n", c=2)
        hh0 = work[:, 2048:4096].bitcast(F16).rearrange("p (c v n) -> p c v n", c=2, v=2)
        yw = work[:, 4096:6144].rearrange("p (z e d) -> p z e d", z=2, e=E0)
        fk = stage[:, 4096:5120].rearrange("p (c h d) -> p c h d", c=2 * B, h=NH)
        rk = work[:, 6144:7168].rearrange("p (c h d) -> p c h d", c=2 * B, h=NH)
        zk = work[:, 7168:7680].rearrange("p (c h d) -> p c h d", c=2 * B, h=NH)
        ks = qT[:].bitcast(BF16).rearrange("p z j n -> p (z j n)")\
            .rearrange("p (c h a d) -> p c h a d", c=2 * B, h=NH, a=6)
        fq = stage[:, 0:2048].rearrange("p (t h d) -> p t h d", t=T, h=NH)
        rq = stage[:, 2048:4096].rearrange("p (t h d) -> p t h d", t=T, h=NH)
        zq = stage[:, 4096:5120].rearrange("p (t h d) -> p t h d", t=T, h=NH)
        qs1 = qs_flat[:, 4096:4096 + T * NH * 6 * FD].bitcast(BF16).rearrange("p (t h a d) -> p t h a d", t=T, h=NH, a=6)
        V1 = FD + 1
        va1, vc1 = (v[:].rearrange("p v b h d -> p (v b h d)")[:, 0:B * NH * 3 * V1].bitcast(BF16)
                    .rearrange("p (b h a d) -> p b h a d", b=B, h=NH, a=3) for v in (va, vc))
        fms = sb("fms", [P, 2, D], F16)
        osum1 = work[:, 0:T * NH * 3 * V1].rearrange("p (t h d) -> p t h d", t=T, h=NH)
        os1 = stage[:, 0:T * NH * V1].rearrange("p (t h d) -> p t h d", t=T, h=NH)
        w1f = stage[:, 3072:5120].rearrange("p (z v n) -> p z v n", z=2, v=2)
        w1s = big[:, 0:E1 * 2048].rearrange("p (e v n) -> p e v n", e=E1, v=2)
        kT_flat = kT[:].rearrange("p w b h k -> p (w b h k)")
        zeros = kT_flat[:, 0:2 * NB * P].bitcast(F32)
        xs_rows = work[:, 0:NB * P].rearrange("p (b d) -> p b d", b=NB)
        ys_rows = work[:, NB * P:2 * NB * P].rearrange("p (b d) -> p b d", b=NB)
        xsT = kT_flat[:, 0:2 * NB * P].rearrange("p (v n) -> p v n", v=2)
        hT = kT_flat[:, 2 * NB * P:2 * NB * P + 4 * 2 * F1].rearrange("p (z v n) -> p z v n", z=4, v=2)
        h32 = stage[:, 1024:3072].rearrange("p (z n) -> p z n", z=4)
        y_tok = stage[:, 0:1024].rearrange("p (t d) -> p t d", t=T)
        e8 = sb("e8", [P, 6, 8])
        e88 = sb("e88", [P, 8, 8])
        slots = sb("slots", [P, T])
        slots_i = sb("slots_i", [P, T], U32)
        bexp = sb("bexp", [P, 2, NB])
        bexp_i = sb("bexp_i", [1, NB], U32)
        boh = sb("boh", [P, NB, E1])
        b1w = e_flat[:, 2 * T * D:2 * T * D + NB * HC1 * E1].rearrange("p (b c e) -> p b c e", b=NB, c=HC1)
        b1s = sb("b1s", [P, NB, HC1])

        xs_d = nc.dram_tensor("sorted_tokens", (NB * P, D), F32, kind="Internal").ap()
        ys_d = nc.dram_tensor("sorted_outputs", (NB * P, D), F32, kind="Internal").ap()
        ps = ctx.enter_context(nc.psum_tensor("ps", [P, 8, 512], F32))

        dma = {n: sem("ld_" + n) for n in ("x", "rows", "ident", "tri", "ctx", "wq", "wk", "wv",
                                           "wo", "small", "wdown", "wgate", "fcw")}
        dma_e = [sem(f"ld_expert{r}") for r in range(2)]
        s_fms = sem("feature_weights_split")
        s_wg = sem("ffn0_weights_split")
        s_xf = sem("ln_f32")
        s_rt = sem("router_logits")
        s_gm = sem("gate_shifted")
        s_ge = sem("gate_exps")
        s_mk = sem("masks")
        s_cum = sem("mask_cumulated")
        s_hp = sem("hidden0_in_psum")
        s_hs = sem("hidden0_silu")
        s_h0 = sem("hidden0_hi")
        s_l0 = sem("hidden0_lo")
        s_y0 = sem("experts0_in_psum")
        s_yw = sem("experts0_weighted")
        s_x0 = sem("ffn0_added")
        s_zk = sem("key_features_in_psum")
        s_zb = sem("key_features_biased")
        s_fk = sem("key_features")
        s_ka = sem("key_parts_act")
        s_kd = sem("key_parts_dve")
        s_v1 = sem("value_ones")
        s_m1 = sem("minus_ones")
        s_k1 = sem("key_stacks_transposed")
        s_k1e = sem("key_stacks_out")
        s_zq = sem("query_features_in_psum")
        s_zqb = sem("query_features_biased")
        s_fq = sem("query_features")
        s_qa = sem("query_parts_act")
        s_qp = sem("query_parts_pool")
        s_qd = sem("query_parts_dve")
        s_os = sem("parts_summed")
        s_mT = sem("mask_transposed")
        s_mTe = sem("mask_rows")
        s_b2 = sem("selected_b2")
        s_zr = sem("zeros")
        s_zs = sem("scratch_zeroed")
        s_sl = sem("slots")
        s_be = sem("block_experts")
        s_b1 = sem("block_biases")
        s_sc = sem("tokens_scattered")
        s_xl = [sem(f"blocks_loaded{r}") for r in range(4)]
        s_bt = sem("blocks_transposed")
        s_bh = sem("blocks_hi")
        s_bl = sem("blocks_lo")
        s_ye = sem("block_outputs_out")
        s_ys = sem("block_outputs_stored")
        s_yg = [sem(f"outputs_gathered{r}") for r in range(2)]
        s_wh = sem("expert_weights_hi")
        s_wl = sem("expert_weights_lo")
        s_h1p = sem("hidden1_in_psum")
        s_h1 = sem("hidden1_gelu")
        s_h1h = sem("hidden1_hi")
        s_h1l = sem("hidden1_lo")
        s_y1 = sem("experts1_in_psum")
        s_dve = sem("dve_chain")
        s_act = sem("act_chain")
        s_pool = sem("pool_chain")
        s_cst = sem("constants_cast")
        s_tanh = sem("gates_ready")
        s_wc = sem("weights_centred")
        s_wkm = sem("wk_mapped")
        s_whi = sem("weights_hi")
        s_wlo = sem("weights_lo")
        s_chi = sem("ctx_hi")
        s_clo = sem("ctx_lo")
        s_beta = sem("beta_row")
        s_betaT = sem("beta_transposed")
        s_coc = sem("beta_column")
        s_lv = sem("ln_var")
        s_ly = sem("ln_rsqrt")
        s_xn = sem("ln_out")
        s_xt = sem("ln_transposed")
        s_xhi = sem("ln_hi")
        s_xlo = sem("ln_lo")
        s_proj = sem("projection_in_psum")
        s_sqr = sem("squares")
        s_ss = sem("square_sums")
        s_ry = sem("head_rsqrt")
        s_km = sem("keys_normalised")
        s_km2 = sem("keys_doubled")
        s_vh = sem("values_hi")
        s_vl = sem("values_lo")
        s_kt = sem("keys_transposed")
        s_kf = sem("keys_f32")
        s_kh = sem("keys_hi")
        s_kl = sem("keys_lo")
        s_qn = sem("queries_normalised")
        s_qh = sem("queries_hi")
        s_ql = sem("queries_lo")
        s_ones = sem("constant_columns")
        s_fin = sem("out_stored")

        def per_layer(name):
            return [sem(f"{name}{k}") for k in range(2)]

        s_qt = per_layer("queries_transposed")
        s_qea = per_layer("queries_out_act")
        s_qed = per_layer("queries_out_dve")
        s_s1 = per_layer("scores_for_max")
        s_mx = per_layer("maxima")
        s_ms = per_layer("maxima_split")
        s_mt = per_layer("maxima_transposed")
        s_md = per_layer("maxima_in_stacks")
        s_me = per_layer("maxima_out")
        s_s2 = per_layer("scores_a")
        s_s2c = per_layer("scores_c")
        s_e = per_layer("exps_a")
        s_ec = per_layer("exps_c")
        s_eha = per_layer("exps_hi_act")
        s_ehp = per_layer("exps_hi_pool")
        s_el = per_layer("exps_lo")
        s_pv = per_layer("weighted_values")
        s_pve = per_layer("weighted_values_out")
        s_on = sem("heads_normalised")
        s_ot = sem("heads_transposed")
        s_oh = sem("heads_hi")
        s_ol = sem("heads_lo")
        s_wo = sem("attention_projected")
        s_mv = sem("ln_statistics")
        s_onp = sem("odd_heads_normalised")
        s_rs = sem("reciprocal_sums")
        s_bo = sem("bias_added")
        s_x = sem("residual_updated")

        JOBS = (("kv", 0), ("kv", 1), ("q", 0), ("q", 1), ("q", 2), ("q", 3), ("kv", 2), ("kv", 3),
                ("q", 4), ("q", 5), ("q", 6), ("q", 7))
        NJ = len(JOBS)
        KTJOB = (3, 4, 5, 6, 9, 10, 11, 12)
        PROJ = []
        for _n in range(NJ):
            kind, i = JOBS[_n]
            PROJ.append(("k" if kind == "kv" else "q", i))
            if _n and JOBS[_n - 1][0] == "kv":
                PROJ.append(("km", JOBS[_n - 1][1]))
            if kind == "kv":
                PROJ.append(("v", i))

        def job_of(what, i):
            return JOBS.index(("q" if what == "q" else "kv", i))

        def pair(n):
            b = 2 * (n % 3)
            return ps[:, b:b + 2, :]

        def pair_of(what, i):
            return pair(PROJ.index((what, i)))

        kT1 = kT[:].bitcast(BF16)
        q_stack = (qs.rearrange("p t h a d -> p t h (a d)"), qs1.rearrange("p t h a d -> p t h (a d)"))
        q_T = (qT[:], qT[:].bitcast(BF16))
        ident_q = (ident16, identb)
        QK = (P, 6 * FD)
        SCALE = (1.0, D ** -0.5)
        KPARTS = ((kT[:, 0], kT[:, 1]), (kT1[:, 0],))
        QM = (P - 1, 6 * FD)
        SK = (P, P)
        VW = (HD + 1, 3 * (FD + 1))
        osums = (osum, osum1)

        def pv_parts(k, b, h, c):
            if k == 0:
                v = vc if c else va
                return ((0, v[:, 0, b, h, :]), (0, v[:, 1, b, h, :]), (1, v[:, 0, b, h, :]))
            v = (vc1 if c else va1)[:, b, h].rearrange("p a d -> p (a d)")
            return ((0, v), (1, v[:, 0:2 * V1]))

        def groups():
            return range(-2, GT + 1)

        def where(g, j):
            return G * g + j, g // NG, G * (g % NG) + j

        MROWS = (1, 2)
        m_T = (mT[:].bitcast(F16), mT[:])
        m_1 = (m12[:].bitcast(F16), m12[:])
        m_ps = tuple(ps[0:MROWS[k] * G, 7, :].bitcast(dt)[:, 0:N] for k, dt in enumerate((F16, BF16)))

        def q_bank(g, half):
            return 4 if g == 0 and half else 5

        def attention_pe(pe, k):
            qTk = q_T[k]

            def scores_for_max(g, j):
                i, b, h = where(g, j)
                if j == 0:
                    pe.wait_ge(s_qea[k], g + 1)
                if j == 2:
                    pe.wait_ge(s_qed[k], g + 1)
                for half in range(2):
                    if i:
                        pe.wait_ge(s_mx[k], 2 * (i - 1) + half + 1)
                    for u in range(2):
                        t = 2 * half + u
                        last = pe.matmul(ps[:, half, u * M:u * M + M], qTk[0:QK[k], g % 3, j, t * P:t * P + P],
                                         KPARTS[k][0][0:QK[k], b, h, 0:M], start=True, stop=True)
                    last.then_inc(s_s1[k], 1)

            def scores(g, j):
                i, b, h = where(g, j)
                if j == 0:
                    pe.wait_ge(s_md[k], 16 * MROWS[k] * (g + 1))
                if i >= 2:
                    pe.wait_ge(s_e[k], i - 1)
                n = len(KPARTS[k])
                for q, kk in enumerate(KPARTS[k]):
                    last = pe.matmul(ps[:, 2 + i % 2, :], kk[0:SK[k], b, h, 0:KA], qTk[0:SK[k], g % 3, j, :],
                                     start=(q == 0), stop=(q == n - 1))
                last.then_inc(s_s2[k], 1)

            def scores_c(g):
                if g:
                    pe.wait_ge(s_ec[k], g)
                n = len(KPARTS[k])
                for q, kk in enumerate(KPARTS[k]):
                    for j in range(G):
                        i, b, h = where(g, j)
                        last = pe.matmul(ps[KCP * j:KCP * j + KCP, 4, :], kk[0:SK[k], b, h, KA:KW],
                                         qTk[0:SK[k], g % 3, j, :], start=(q == 0), stop=(q == n - 1),
                                         tile_position=(0, KCP * j))
                last.then_inc(s_s2c[k], 1)

            def stacks_ready(b):
                if k == 0:
                    pe.wait_ge(s_ql, TB * (b + 1))
                    pe.wait_ge(s_kl, NG * (b + 1))
                else:
                    pe.wait_ge(s_qd, 3 * (b + 1))
                    pe.wait_ge(s_qa, 2 * (b + 1))
                    pe.wait_ge(s_qp, b + 1)

            def queries_in(g, half):
                if g % NG == 0 and half == 0:
                    stacks_ready(g // NG)
                if g and half:
                    pe.wait_ge(s_qea[k], g + 1)
                elif g:
                    pe.wait_ge(s_qed[k], g)
                o = ps[:, q_bank(g, half), :].bitcast(BF16 if k else F16)
                for u in range(2):
                    h = G * (g % NG) + 2 * half + u
                    for t in range(TB):
                        last = pe.transpose(o[0:QK[k], u * N + t * P:u * N + t * P + P],
                                            q_stack[k][:, TB * (g // NG) + t, h, :], ident_q[k][:])
                last.then_inc(s_qt[k], 1)

            def times_values(g, j):
                i, b, h = where(g, j)
                if j == 0:
                    pe.wait_ge(s_el[k], (G + 1) * (g + 1))
                if i >= 2:
                    pe.wait_ge(s_pve[k], i - 1)
                if j == 1:
                    pe.wait_ge(s_me[k], min(g + 3, GT))
                for t in range(TB):
                    out = ps[:, 6 + i % 2, t * VW[k]:(t + 1) * VW[k]]
                    prods = []
                    for c, (slot, lo, hi) in enumerate(((j, 0, KA), (G, KCP * j, KCP * j + KC))):
                        for part, v in pv_parts(k, b, h, c):
                            prods.append(((eh, el)[part][lo:hi, g % 2, slot, t * P:t * P + P], v[lo:hi]))
                    for n, (w, v) in enumerate(prods):
                        last = pe.matmul(out[:, 0:v.shape[1]], w, v, start=(n == 0), stop=(n == len(prods) - 1))
                last.then_inc(s_pv[k], 1)

            def maxima_in(g):
                pe.wait_ge(s_ms[k], g + 1)
                if g >= 3:
                    pe.wait_ge(s_pve[k], G * (g - 2))
                for t in range(TB):
                    last = pe.transpose(m_ps[k][:, t * P:t * P + P],
                                        m_1[k][:, g % 2, t, 0:MROWS[k]].rearrange("p a j -> p (a j)"), ident_q[k][:])
                last.then_inc(s_mt[k], 1)

            for it in groups():
                ahead, now, behind = 0 <= it + 1 < GT, 0 <= it < GT, 0 <= it - 1 < GT
                if now:
                    scores(it, 0)
                if ahead:
                    scores_for_max(it + 1, 1)
                if now:
                    scores(it, 1)
                if ahead:
                    scores_for_max(it + 1, 2)
                if now:
                    scores(it, 2)
                if ahead:
                    scores_for_max(it + 1, 3)
                if now:
                    scores_c(it)
                if behind:
                    times_values(it - 1, 0)
                if ahead:
                    maxima_in(it + 1)
                if now:
                    scores(it, 3)
                if it + 2 < GT:
                    queries_in(it + 2, 0)
                if behind:
                    times_values(it - 1, 1)
                    times_values(it - 1, 2)
                if it + 2 < GT:
                    queries_in(it + 2, 1)
                    scores_for_max(it + 2, 0)
                if behind:
                    times_values(it - 1, 3)

        def queries_out(eng, k, g, half):
            o = ps[:, q_bank(g, half), :].bitcast(BF16 if k else F16)[0:QK[k], :].rearrange("p (u n) -> p u n", u=2)
            dst = q_T[k][0:QK[k], g % 3, 2 * half:2 * half + 2, :]
            eng.wait_ge(s_qt[k], 2 * g + half + 1)
            if half == 0:
                eng.activation(dst, o, ACT.Copy).then_inc(s_qea[k], 1)
            else:
                eng.tensor_copy(dst, o).then_inc(s_qed[k], 1)

        def maxima_to_stacks(sp, k, g):
            sp.wait_ge(s_me[k], g + 1)
            for a in range(MROWS[k]):
                sp.dma_start(q_T[k][QM[k] + a:QM[k] + a + 1, g % 3, :, :],
                             m_T[k][G * a:G * a + G, g % 2, :]).then_inc(s_md[k], 16)

        ORDER = (0, 1, 2, G, 3)

        def e32_free(eng, k, g, j):
            if g:
                eng.wait_ge(s_el[k], (G + 1) * (g - 1) + ORDER.index(j) + 1)

        def attention_act(act, k, beside=None):
            def exps(g, j):
                if k == 0 and g == 0 and j == 0:
                    act.wait_ge(s_kl, GT)
                i = G * g + j
                act.wait_ge(s_s2[k], i + 1)
                e32_free(act, k, g, j)
                act.activation(e32[:, j, :], ps[:, 2 + i % 2, :], ACT.Exp, scale=SCALE[k]).then_inc(s_e[k], 1)

            def exps_c(g):
                act.wait_ge(s_s2c[k], g + 1)
                e32_free(act, k, g, G)
                act.activation(e32[:, G, :], ps[:, 4, :], ACT.Exp, scale=SCALE[k]).then_inc(s_ec[k], 1)

            def values_out(g, j):
                i, b, h = where(g, j)
                act.wait_ge(s_pv[k], i + 1)
                act.activation(osums[k][:, TB * b:TB * b + TB, h, :],
                               ps[:, 6 + i % 2, 0:TB * VW[k]].rearrange("p (t d) -> p t d", t=TB),
                               ACT.Copy).then_inc(s_pve[k], 1)

            for it in groups():
                ahead, now, behind = 0 <= it + 1 < GT, 0 <= it < GT, 0 <= it - 1 < GT
                if now:
                    exps(it, 0)
                    exps(it, 1)
                    act.wait_ge(s_e[k], G * it + 1)
                    if it >= 2:
                        act.wait_ge(s_pv[k], G * (it - 1))
                    act.activation(eh[:, it % 2, 0, :], e32[:, 0, :], ACT.Copy).then_inc(s_eha[k], 1)
                    exps(it, 2)
                    exps_c(it)
                if behind:
                    values_out(it - 1, 0)
                if ahead:
                    act.wait_ge(s_mt[k], it + 2)
                    if it >= 1:
                        act.wait_ge(s_md[k], 16 * MROWS[k] * it)
                    act.activation(m_T[k][0:MROWS[k] * G, (it + 1) % 2, :], m_ps[k], ACT.Copy).then_inc(s_me[k], 1)
                if now:
                    exps(it, 3)
                if it + 2 < GT:
                    queries_out(act, k, it + 2, 0)
                if now and beside:
                    beside(it)
                if behind:
                    values_out(it - 1, 1)
                    values_out(it - 1, 2)
                    values_out(it - 1, 3)

        def attention_pool(pool, k, beside=None):
            for g in range(GT):
                for j in ORDER[1:]:
                    if j == G:
                        pool.wait_ge(s_ec[k], g + 1)
                    else:
                        pool.wait_ge(s_e[k], G * g + j + 1)
                    if g >= 2:
                        pool.wait_ge(s_pv[k], G * (g - 1))
                    pool.tensor_scalar(eh[:, g % 2, j, :], e32[:, j, :], 1.0, 0.0, ALU.mult, ALU.add)\
                        .then_inc(s_ehp[k], 1)
                if beside:
                    beside(g)

        def attention_dve(dve, k, link, beside=None):
            def lo(g):
                for n, j in enumerate(ORDER):
                    if n == 0:
                        dve.wait_ge(s_eha[k], g + 1)
                        if g >= 2:
                            dve.wait_ge(s_pv[k], G * (g - 1))
                    else:
                        dve.wait_ge(s_ehp[k], G * g + n)
                    dve.tensor_tensor(el[:, g % 2, j, :], e32[:, j, :], eh[:, g % 2, j, :], ALU.subtract)\
                       .then_inc(s_el[k], 1)

            def maxima(g, heads):
                for j in heads:
                    i = G * g + j
                    for half in range(2):
                        dve.wait_ge(s_s1[k], 2 * i + half + 1)
                        dve.tensor_reduce(mx[:, g % 2, 2 * half:2 * half + 2, j],
                                          ps[:, half, 0:2 * M].rearrange("p (u m) -> p u m", u=2),
                                          AX.X, ALU.max).then_inc(s_mx[k], 1)

            def maxima_split(g):
                dve.wait_ge(s_mx[k], 2 * G * (g + 1))
                if g >= 2:
                    dve.wait_ge(s_mt[k], g - 1)
                hi = m_1[k][:, g % 2, :, 0, :]
                if k == 0:
                    dve.tensor_copy(hi, mx[:, g % 2]).then_inc(s_ms[k], 1)
                else:
                    link(dve.tensor_copy(hi, mx[:, g % 2]))
                    dve.tensor_tensor(m_1[k][:, g % 2, :, 1, :], mx[:, g % 2], hi, ALU.subtract).then_inc(s_ms[k], 1)

            for it in groups():
                if 0 <= it + 1 < GT:
                    maxima(it + 1, range(1, G))
                    maxima_split(it + 1)
                if 0 <= it < GT:
                    lo(it)
                    if beside:
                        beside(it)
                if it + 2 < GT:
                    maxima(it + 2, (0,))
                    queries_out(dve, k, it + 2, 1)

        on = qs_flat[:, 8192:12288].bitcast(F32)\
            .rearrange("p (z n) -> p z n", z=2)
        HCH = (NH * HD // P, NH * FD // P)
        oT = qs_flat[:, 12288:16384].rearrange("p (z l n) -> p z l n", z=2, l=2)

        def project_out_pe(pe, k, weights):
            C = HCH[k]
            for t in range(T + 1):
                if t < T:
                    if t % 2:
                        pe.wait_ge(s_onp, 4 * k + t // 2 + 1)
                    else:
                        pe.wait_ge(s_on, 4 * k + t // 2 + 1)
                    if t >= 2:
                        pe.wait_ge(s_ol, T * k + t - 1)
                    for c in range(C):
                        last = pe.transpose(ps[:, 2 * (t % 2) + c // 4, (c % 4) * P:(c % 4 + 1) * P],
                                            on[:, t % 2, c * P:(c + 1) * P], ident[:])
                    last.then_inc(s_ot, 1)
                if t:
                    u = t - 1
                    pe.wait_ge(s_ol, T * k + u + 1)
                    n = 0
                    for c in range(C):
                        for a, w in ((0, 0), (0, 1), (1, 0)):
                            last = pe.matmul(ps[:, 4 + u // 4, (u % 4) * P:(u % 4 + 1) * P],
                                             oT[:, u % 2, a, c * P:(c + 1) * P], weights(w, c),
                                             start=(n == 0), stop=(n == 3 * C - 1))
                            n += 1
                    last.then_inc(s_wo, 1)

        def project_out_act(act, k):
            C = HCH[k]
            for t in range(T):
                act.wait_ge(s_ot, T * k + t + 1)
                if t >= 2:
                    act.wait_ge(s_wo, T * k + t - 1)
                act.activation(oT[:, t % 2, 0, 0:C * P], ps[:, 2 * (t % 2):2 * (t % 2) + 2, :]
                               .rearrange("p a b -> p (a b)")[:, 0:C * P], ACT.Copy).then_inc(s_oh, 1)

        def normalised(eng, k, o, r, t):
            C, W = HCH[k], o.shape[3]
            if t >= 2:
                eng.wait_ge(s_ot, T * k + t - 1)
            return eng.tensor_tensor(on[:, t % 2, 0:C * P].rearrange("p (h d) -> p h d", d=W), o[:, t],
                                     r[:, t, :].unsqueeze(2).to_broadcast([P, NH, W]), ALU.mult)

        def project_out_pool(pool, k, o, r, first):
            pool.wait_ge(s_rs, k + 2)
            for t in range(first, T, 2):
                normalised(pool, k, o, r, t).then_inc(s_onp, 1)

        def project_out_dve(dve, k, o, r, midway, first):
            C = HCH[k]
            for t in range(0, T + 1):
                if first <= t < T and t % 2 == 0:
                    normalised(dve, k, o, r, t).then_inc(s_on, 1)
                if t == T - 1:
                    midway()
                if t == 0:
                    continue
                t -= 1
                dve.wait_ge(s_oh, T * k + t + 1)
                dve.tensor_tensor(oT[:, t % 2, 1, 0:C * P], ps[:, 2 * (t % 2):2 * (t % 2) + 2, :]
                                  .rearrange("p a b -> p (a b)")[:, 0:C * P], oT[:, t % 2, 0, 0:C * P],
                                  ALU.subtract).then_inc(s_ol, 1)

        x_ps = ps[:, 6:8, :].rearrange("p a b -> p (a b)")

        def ln_pe(pe, k):
            for t in range(T):
                pe.wait_ge(s_xn, T * k + t + 1)
                pe.transpose(ps[:, 6 + t // 4, (t % 4) * P:(t % 4 + 1) * P], xn[:, t, :], ident[:]).then_inc(s_xt, 1)

        def halves(ap):
            return (ap[:, 0:N], ap[:, N:2 * N])

        def ln_act(act, k):
            for u in range(2):
                act.wait_ge(s_xt, T * k + TB * (u + 1))
                if k in (1, 3):
                    act.activation(halves(xnT)[u], ps[:, 6 + u, :], ACT.Copy).then_inc(s_xf, 1)
                if k < 3:
                    act.activation(halves(xh[:, 0, :])[u], ps[:, 6 + u, :], ACT.Copy).then_inc(s_xhi, 1)

        def ln_dve(dve, k):
            for u in range(2):
                dve.wait_ge(s_xhi, 2 * k + u + 1)
                dve.tensor_tensor(halves(xh[:, 1, :])[u], ps[:, 6 + u, :], halves(xh[:, 0, :])[u],
                                  ALU.subtract).then_inc(s_xlo, 1)

        def router_pe(pe, k):
            pe.wait_ge(dma["small"], 5 * 16)
            for t in range(T):
                if t % TB == 0:
                    pe.wait_ge(s_xf, 2 * k + t // TB + 1)
                last = pe.matmul(ps[:, 5, t * 8:t * 8 + 8], xnT[:, t * P:t * P + P], wrt[:, k, :], start=True, stop=True)
            last.then_inc(s_rt, 1)

        DVE_TILES = (1, 3, 5, 7)

        def x0_count(t):
            return sum(u not in DVE_TILES for u in range(t + 1))

        LG, EX, GA, MA, MB, KM, CO, TM = range(8)

        def wide(ap):
            return ap.unsqueeze(2).to_broadcast([P, T, 8])

        def iota():
            return rows[:, ROW["iota"][0]:ROW["iota"][1]].unsqueeze(1).to_broadcast([P, T, 8])

        def gates_dve(dve, k, link, meanwhile=None):
            dve.wait_ge(s_rt, k + 1)
            lp = ps[:, 5, 0:T * 8].rearrange("p (t e) -> p t e", t=T)
            if k:
                br = rows[:, ROW["br"][0]:ROW["br"][1]].unsqueeze(1).to_broadcast([P, T, 8])
                link(dve.tensor_tensor(gt[:, LG], lp, br, ALU.add))
                lp = gt[:, LG]
            link(dve.tensor_reduce(g1[:, 0, :], lp, AX.X, ALU.max))
            dve.tensor_tensor(gt[:, LG], lp, wide(g1[:, 0, :]), ALU.subtract).then_inc(s_gm, 1)
            if meanwhile:
                meanwhile()
            dve.wait_ge(s_ge, k + 1)
            link(dve.tensor_reduce(g1[:, 1, :], gt[:, EX], AX.X, ALU.add))
            link(dve.reciprocal(g1[:, 2, :], g1[:, 1, :]))
            link(dve.tensor_tensor(gt[:, GA], gt[:, EX], wide(g1[:, 2, :]), ALU.mult))
            for t in range(T):
                last = dve.max(g8[:, 0, t, :], gt[:, GA, t, :])
            link(last)
            for t in range(T):
                last = dve.max_index(gi[:, t, :], g8[:, 0, t, :], gt[:, GA, t, :])
            link(last)
            link(dve.tensor_copy(g8[:, 1], gi[:]))
            link(dve.tensor_tensor(gt[:, MA], iota(), wide(g8[:, 1, :, 0]), ALU.is_equal))
            if k == 0:
                link(dve.tensor_tensor(gt[:, MB], iota(), wide(g8[:, 1, :, 1]), ALU.is_equal))
                link(dve.tensor_tensor(gt[:, MA], gt[:, MA], gt[:, MB], ALU.add))
            dve.tensor_copy(maskb[:], gt[:, MA]).then_inc(s_mk, 1)

        def gates_act(act, k):
            act.wait_ge(s_gm, k + 1)
            act.activation(gt[:, EX], gt[:, LG], ACT.Exp).then_inc(s_ge, 1)

        block = ctx.enter_context(nc.Block())

        @block.sync
        def _(sp):
            for name, dst, src in (
                ("wk", wk, wk_d), ("rows", rows[:], rows_d.partition_broadcast(P)), ("ctx", ctxT, ctx_d),
                ("ident", ident[:], ident_d), ("x", x[:], x_d.rearrange("(t p) d -> p t d", p=P)), ("wv", wv, wv_d), ("wq", wq, wq_d),
                ("tri", tri, tri_d),
                ("wo", wo.rearrange("p (c d) -> p c d", d=D), wo_d.rearrange("(c p) d -> p c d", p=P)),
            ):
                sp.dma_start(dst, src).then_inc(dma[name], 16)
            for dst, src in ((fm[:], fm_d), (wrt[:, 0, :], wrouter_d), (wrt[:, 1, :], wr_d), (b1c[:], b1_d), (b2s[:], b2_d)):
                sp.dma_start(dst, src).then_inc(dma["small"], 16)
            sp.wait_ge(s_zr, 1)
            sp.dma_start(xs_d.rearrange("(b p) d -> p b d", p=P), zeros.rearrange("p (b d) -> p b d", b=NB)).then_inc(s_zs, 16)
            sp.wait_ge(s_clo, 2)
            sp.wait_ge(s_wlo, 3)
            sp.dma_start(wdf, wdown_d.rearrange("p c n -> p (c n)")).then_inc(dma["wdown"], 16)
            sp.dma_start(wgf, wgate_d).then_inc(dma["wgate"], 16)
            sp.dma_start(fcf.rearrange("p (c d) -> p c d", d=D), fcw_d).then_inc(dma["fcw"], 16)
            for g in range(GT):
                maxima_to_stacks(sp, 0, g)
            sp.wait_ge(s_zqb, B)
            sp.wait_ge(s_fq, 4)
            sp.wait_ge(s_qd, 6)
            sp.wait_ge(s_qa, 4)
            for e in range(E1):
                if e >= 2:
                    for g in range(3) if e == 2 else (e,):
                        maxima_to_stacks(sp, 1, g)
                    sp.wait_ge(s_wl, 2 * (e - 1))
                sp.dma_start(w1f[:, e % 2, 0, :], w1_d[e]).then_inc(dma_e[e % 2], 16)
                sp.dma_start(w1f[:, e % 2, 1, :].rearrange("p (c d) -> p c d", c=HC1), w2_d[e]).then_inc(dma_e[e % 2], 16)
            sp.wait_ge(s_sc, 16 * T)
            for q in range(4):
                b0, b1 = 4 * q, min(4 * q + 4, NB)
                sp.dma_start(xs_rows[:, b0:b1, :], xs_d[b0 * P:b1 * P].rearrange("(b p) d -> p b d", p=P))\
                  .then_inc(s_xl[q], 16)
            for q in range(4):
                b0, b1 = 4 * q, min(4 * q + 4, NB)
                sp.wait_ge(s_ye, b1)
                sp.dma_start(ys_d[b0 * P:b1 * P].rearrange("(b p) d -> p b d", p=P), ys_rows[:, b0:b1, :])\
                  .then_inc(s_ys, 16)
            for u in range(2):
                sp.wait_ge(s_x, 6 + u)
                sp.dma_start(out_d.rearrange("(t p) d -> p t d", p=P)[:, TB * u:TB * u + TB],
                             x[:, TB * u:TB * u + TB]).then_inc(s_fin, 16)
            sp.wait_ge(s_fin, 32)

        def heads(ap):
            return ap.rearrange("p (h d) -> p h d", d=HD)

        def bc(ap, shape, axis):
            return ap.unsqueeze(axis).to_broadcast(shape)

        @block.vector
        def _(dve):
            links = [0]

            reciprocals = [0]

            def link(ins, to=None):
                if to is not None:
                    reciprocals[0] += 1
                    ins.then_inc(to, 1)
                    dve.wait_ge(to, reciprocals[0])
                    return
                links[0] += 1
                ins.then_inc(s_dve, 1)
                dve.wait_ge(s_dve, links[0])

            def rsqrt_newton(y, v, t):
                link(dve.tensor_tensor(t, y, y, ALU.mult))
                link(dve.scalar_tensor_tensor(out=t, in0=t, scalar=-0.5, in1=v, op0=ALU.mult, op1=ALU.mult))
                return dve.scalar_tensor_tensor(out=y, in0=t, scalar=1.5, in1=y, op0=ALU.add, op1=ALU.mult)

            def residual(k, u):
                dve.wait_ge(s_wo, T * k + TB * (u + 1))
                dve.wait_ge(s_bo, 2 * k + 2)
                xs = x[:, TB * u:TB * u + TB, :]
                dve.scalar_tensor_tensor(out=xs, in0=ps[:, 4 + u, :].rearrange("p (t d) -> p t d", t=TB),
                                         scalar=th[:, k:k + 1], in1=xs, op0=ALU.mult, op1=ALU.add).then_inc(s_x, 1)
                dve.wait_ge(s_x, 2 * k + u + 1)
                statistics_of(range(TB * u, TB * u + TB))

            def statistics_of(tiles, by_tile=False):
                for t in tiles:
                    if by_tile and t not in DVE_TILES:
                        dve.wait_ge(s_x0, x0_count(t))
                    i = dve.bn_stats(st[:, t, :], x[:, t, :])
                link(i)
                for t in tiles:
                    i = dve.bn_aggr(mv[:, t, :], st[:, t, :])
                if tiles[-1] == T - 1:
                    i.then_inc(s_mv, 1)

            def layernorm(k):
                dve.wait_ge(s_mv, k + 1)
                dve.tensor_scalar(lnv[:, 0, :], mv[:, :, 1], 1.0, EPS, ALU.mult, ALU.add).then_inc(s_lv, 1)
                dve.wait_ge(s_ly, k + 1)
                link(rsqrt_newton(lnv[:, 1, :], lnv[:, 0, :], lnv[:, 2, :]))
                for t in range(T):
                    dve.tensor_scalar(xn[:, t, :], x[:, t, :], mv[:, t, 0:1], lnv[:, 1, t:t + 1],
                                      ALU.subtract, ALU.mult).then_inc(s_xn, 1)

            def minus_means(w, i):
                link(dve.tensor_reduce(hmean[:, i, :], heads(w), AX.X, ALU.add, negate=True))
                return dve.tensor_scalar(hmean[:, i, :], hmean[:, i, :], 1.0 / HD, None, ALU.mult)

            def split_lo(w, k):
                dve.tensor_tensor(wsp[:, k, 1, :], w, wsp[:, k, 0, :], ALU.subtract).then_inc(s_wlo, 1)

            dve.wait_ge(dma["wk"], 16)
            link(minus_means(wk, 0))
            dve.tensor_tensor(heads(wk), heads(wk), bc(hmean[:, 0, :], [P, NH, HD], 2), ALU.add).then_inc(s_wc, 1)
            dve.wait_ge(dma["rows"], 16)
            s = HD ** -0.5
            a, c, tmp, beta, beta2 = (co[:, i, :] for i in range(5))
            L = HD - 1
            dve.scalar_tensor_tensor(out=a, in0=row("gk"), scalar=s, in1=row("gq"), op0=ALU.mult, op1=ALU.mult)
            dve.scalar_tensor_tensor(out=c, in0=row("gk"), scalar=s, in1=row("bq"), op0=ALU.mult, op1=ALU.mult)
            dve.scalar_tensor_tensor(out=beta, in0=row("bk"), scalar=s, in1=row("gq"), op0=ALU.mult, op1=ALU.mult)
            link(dve.scalar_tensor_tensor(out=tmp, in0=row("bk"), scalar=s, in1=row("bq"), op0=ALU.mult, op1=ALU.mult))
            link(dve.tensor_scalar(beta[:, 0:L], beta[:, 0:L], beta[:, L:HD], None, ALU.subtract))
            link(dve.tensor_reduce(beta[:, L:HD], tmp, AX.X, ALU.add))
            dve.tensor_copy(beta2[:, 0:L], beta[:, 0:L])
            dve.memset(beta2[:, L:HD], -1.0).then_inc(s_beta, 1)
            dve.wait_ge(s_whi, 1)
            split_lo(wk, 1)
            dve.wait_ge(s_wc, 1)
            wkc = heads(sq[:, 1, :])
            link(dve.tensor_tensor(wkc, heads(wk), bc(c, [P, NH, HD], 1), ALU.mult))
            link(dve.tensor_reduce(hmean[:, 0, :], wkc, AX.X, ALU.add))
            dve.wait_ge(s_betaT, 1)
            dve.tensor_copy(coc[:], ps[:, 6, 0:1]).then_inc(s_coc, 1)
            dve.wait_ge(s_whi, 2)
            split_lo(wv, 3)
            dve.wait_ge(s_wkm, 2)
            dve.tensor_copy(heads(wkm)[:, :, L], hmean[:, 0, :]).then_inc(s_wkm, 1)
            dve.wait_ge(s_wkm, 3)
            dve.wait_ge(s_whi, 3)
            split_lo(wkm, 2)

            def counted(ins):
                links[0] += 1
                ins.then_inc(s_dve, 1)
                return links[0]

            def statistics(n):
                now, behind = n < NJ, 0 <= n - 1 < NJ
                if now:
                    kind, i = JOBS[n]
                    dst = ssk[:, 0, i, :] if kind == "kv" else ssq[:, 0, i, :]
                if behind:
                    kind, i = JOBS[n - 1]
                    v, y, t = ((ssk if kind == "kv" else ssq)[:, slot, i, :] for slot in range(3))

                def summed(half):
                    dve.wait_ge(s_sqr, 2 * n + half + 1)
                    hs = slice(half * NH // 2, (half + 1) * NH // 2)
                    return dve.tensor_reduce(dst[:, hs], heads(sq[:, n % 2, :])[:, hs, :], AX.X, ALU.add)

                if now:
                    summed(0)
                if behind:
                    dve.wait_ge(s_ry, n)
                    squared = counted(dve.tensor_tensor(t, y, y, ALU.mult))
                if now:
                    sums = counted(summed(1))
                if behind:
                    dve.wait_ge(s_dve, squared)
                    scaled = counted(dve.scalar_tensor_tensor(out=t, in0=t, scalar=-0.5, in1=v, op0=ALU.mult,
                                                              op1=ALU.mult))
                if now:
                    dve.wait_ge(s_dve, sums)
                    dve.tensor_scalar(dst, dst, 1.0 / HD, EPS, ALU.mult, ALU.add).then_inc(s_ss, 1)
                if behind:
                    dve.wait_ge(s_dve, scaled)
                    link(dve.scalar_tensor_tensor(out=y, in0=t, scalar=1.5, in1=y, op0=ALU.add, op1=ALU.mult))

            def normalised(n):
                kind, i = JOBS[n]
                if kind == "kv":
                    if i == 2:
                        dve.wait_ge(s_kt, NG)
                    for half in range(2):
                        hs = slice(half * NH // 2, (half + 1) * NH // 2)
                        dve.wait_ge(s_proj, 2 * PROJ.index(("km", i)) + half + 1)
                        dve.tensor_tensor(km[:, i % 2, hs, 0, :], heads(pair_of("km", i)[:, half, :]),
                                          bc(ssk[:, 1, i, hs], [P, NH // 2, HD], 2), ALU.mult).then_inc(s_km, 1)
                else:
                    if i >= 2:
                        dve.wait_ge(s_qh, i - 1)
                        dve.wait_ge(s_ql, i - 1)
                    for half in range(2):
                        hs = slice(half * NH // 2, (half + 1) * NH // 2)
                        dve.tensor_tensor(qn[:, i % 2, hs, :], heads(pair_of("q", i)[:, half, :]),
                                          bc(ssq[:, 1, i, hs], [P, NH // 2, HD], 2), ALU.mult).then_inc(s_qn, 1)

            for n in range(NJ + 2):
                statistics(n)
                if n == 0:
                    dve.wait_ge(dma["wq"], 16)
                    minus_means(wq, 1).then_inc(s_wc, 1)
                if n == 1:
                    ln_dve(dve, 0)
                if 0 <= n - 1 < NJ:
                    normalised(n - 1)
                if n < NJ and JOBS[n][0] == "kv":
                    c = JOBS[n][1]
                    dve.wait_ge(s_vh, c + 1)
                    v = vc if c % 2 else va
                    pv = pair_of("v", c).rearrange("p a (h d) -> p (a h) d", d=HD)
                    dve.tensor_tensor(v[:, 1, c // 2, :, 0:HD], pv, v[:, 0, c // 2, :, 0:HD],
                                      ALU.subtract).then_inc(s_vl, 1)
                if n == 0:
                    dve.wait_ge(dma["x"], 16)
                    statistics_of(range(T))
                    layernorm(0)
            def batch_reciprocals(b):
                dve.wait_ge(s_pve[0], NH * (b + 1))
                link(dve.reciprocal(rsum[:, TB * b:TB * b + TB], osum[:, TB * b:TB * b + TB, :, HD]), s_rs)

            attention_dve(dve, 0, link, lambda it: batch_reciprocals(0) if it == GT - 3 else None)
            batch_reciprocals(1)
            project_out_dve(dve, 0, osum[:, :, :, 0:HD], rsum, lambda: residual(0, 0), 2)
            residual(0, 1)

            layernorm(1)
            ln_dve(dve, 1)

            def hidden_lo(c):
                dve.wait_ge(s_h0, c + 1)
                dve.tensor_tensor(hh0[:, c, 1, :], hs[:, c, :], hh0[:, c, 0, :], ALU.subtract).then_inc(s_l0, 1)

            hidden_lo(0)
            gates_dve(dve, 0, link, lambda: hidden_lo(1))
            dve.wait_ge(s_cum, 1)
            cum = ps[:, 4, 0:T * 8].rearrange("p (t e) -> p t e", t=T)
            link(dve.scalar_tensor_tensor(out=gt[:, KM], in0=cum, scalar=float(CAP), in1=gt[:, MA],
                                          op0=ALU.is_le, op1=ALU.mult))
            link(dve.tensor_tensor(gt[:, KM], gt[:, KM], gt[:, GA], ALU.mult))
            link(dve.tensor_reduce(g1[:, 0, :], gt[:, KM], AX.X, ALU.add))
            link(dve.tensor_scalar(g1[:, 0, :], g1[:, 0, :], 1.0, 1e-6, ALU.mult, ALU.add))
            link(dve.reciprocal(g1[:, 1, :], g1[:, 0, :]))
            link(dve.tensor_scalar(g1[:, 1, :], g1[:, 1, :], th[:, 2:3], 1.0 / WS, ALU.mult, ALU.mult))
            link(dve.tensor_tensor(gt[:, CO], gt[:, KM], wide(g1[:, 1, :]), ALU.mult))
            for t in range(T):
                dve.wait_ge(s_y0, t + 1)
                if t >= 2 and t - 2 not in DVE_TILES:
                    dve.wait_ge(s_x0, x0_count(t - 2))
                dve.tensor_tensor(yw[:, t % 2], ps[:, 2 * (t % 2):2 * (t % 2) + 2, :].rearrange("p a (e d) -> p (a e) d", d=D),
                                  bc(gt[:, CO, t, :], [P, E0, D], 2), ALU.mult).then_inc(s_yw, 1)
                if t == 4:
                    dve.wait_ge(s_ka, 5)
                    dve.tensor_tensor(ks[:, :, :, 4, :], rk, ks[:, :, :, 1, :], ALU.subtract).then_inc(s_kd, 1)
                if t in DVE_TILES:
                    dve.wait_ge(s_yw, t + 1)
                    link(dve.tensor_reduce(obo[:, 1, :], yw[:, t % 2].rearrange("p e d -> p d e"), AX.X, ALU.add))
                    link(dve.tensor_tensor(x[:, t, :], x[:, t, :], obo[:, 1, :], ALU.add))
                if t == 0:
                    dve.wait_ge(s_zk, 1)
                    fmb = row("fmb").unsqueeze(1).to_broadcast([P, 2 * B, D])
                    dve.tensor_tensor(zk.rearrange("p c h d -> p c (h d)"), ps[:, 5, :].rearrange("p (c n) -> p c n", n=D),
                                      fmb, ALU.add).then_inc(s_zb, 1)
                if t == 2:
                    dve.wait_ge(s_ka, 1)
                    dve.tensor_tensor(rk, fk, ks[:, :, :, 0, :], ALU.subtract).then_inc(s_kd, 1)
                if t == T - 2:
                    dve.wait_ge(s_kd, 2)
                    dve.wait_ge(s_v1, 4)
                    for c in range(2 * B):
                        v = (vc1 if c % 2 else va1)[:, c // 2]
                        for part, slot in enumerate((0, 1, 4)):
                            last = dve.tensor_copy(v[:, :, part, 0:FD], ks[:, c, :, slot, :])
                    last.then_inc(s_kd, 1)

            statistics_of(range(T), True)
            layernorm(2)
            ln_dve(dve, 2)
            dve.wait_ge(s_zq, 1)
            fmb = row("fmb").unsqueeze(1).to_broadcast([P, TB, D])
            for b in range(B):
                dve.tensor_tensor(zq[:, TB * b:TB * b + TB].rearrange("p t h d -> p t (h d)"),
                                  ps[:, b, :].rearrange("p (t n) -> p t n", n=D), fmb, ALU.add).then_inc(s_zqb, 1)
            for b in range(B):
                ts = slice(TB * b, TB * b + TB)
                dve.wait_ge(s_qa, 2 * b + 1)
                link(dve.tensor_tensor(rq[:, ts], fq[:, ts], qs1[:, ts, :, 0, :], ALU.subtract))
                dve.tensor_copy(qs1[:, ts, :, 2, :], rq[:, ts]).then_inc(s_qd, 1)
                dve.wait_ge(s_qd, 3 * b + 1)
                dve.tensor_tensor(qs1[:, ts, :, 5, :], rq[:, ts], qs1[:, ts, :, 2, :], ALU.subtract).then_inc(s_qd, 1)
                dve.tensor_copy(qs1[:, ts, :, 3, :], qs1[:, ts, :, 2, :]).then_inc(s_qd, 1)
            attention_dve(dve, 1, link)
            dve.wait_ge(s_os, GT - 2)
            for g in (GT - 2, GT - 1):
                i, b, h = where(g, 0)
                dve.wait_ge(s_pve[1], G * (g + 1))
                for t in range(TB * b, TB * b + TB):
                    last = dve.tensor_reduce(os1[:, t, h:h + G], osum1[:, t, h:h + G].rearrange("p h (a d) -> p h d a", a=3),
                                             AX.X, ALU.add)
            link(last)
            link(dve.reciprocal(rsum[:], os1[:, :, :, FD]), s_rs)
            project_out_dve(dve, 1, os1[:, :, :, 0:FD], rsum, lambda: residual(1, 0), 0)
            residual(1, 1)

            layernorm(3)
            gates_dve(dve, 1, link)
            dve.wait_ge(s_cum, 2)
            cum = ps[:, 4, 0:T * 8].rearrange("p (t e) -> p t e", t=T)
            total = ps[:, 4, T * 8:T * 8 + 8]
            NBL, FIRST, BASE, END = range(4)

            def w8(ap, axis):
                return ap.unsqueeze(axis).to_broadcast([P, 8, 8])

            link(dve.tensor_tensor(e88[:], w8(total, 2), w8(row("k128"), 1), ALU.is_gt))
            link(dve.tensor_reduce(e8[:, NBL], e88[:], AX.X, ALU.add))
            link(dve.tensor_tensor(e88[:], w8(e8[:, NBL], 1), row("before").rearrange("p (a b) -> p a b", a=8), ALU.mult))
            link(dve.tensor_reduce(e8[:, FIRST], e88[:], AX.X, ALU.add))
            dve.tensor_tensor(e8[:, END], e8[:, FIRST], e8[:, NBL], ALU.add)
            link(dve.tensor_scalar(e8[:, BASE], e8[:, FIRST], float(P), -1.0, ALU.mult, ALU.add))
            link(dve.tensor_tensor(gt[:, TM], cum, e8[:, BASE].unsqueeze(1).to_broadcast([P, T, 8]), ALU.add))
            link(dve.tensor_tensor(gt[:, TM], gt[:, TM], gt[:, MA], ALU.mult))
            link(dve.tensor_reduce(slots[:], gt[:, TM], AX.X, ALU.add))
            dve.tensor_copy(slots_i[:], slots[:]).then_inc(s_sl, 1)
            link(dve.tensor_tensor(boh[:], row("block").unsqueeze(2).to_broadcast([P, NB, E1]),
                                   e8[:, END].unsqueeze(1).to_broadcast([P, NB, E1]), ALU.is_ge))
            link(dve.tensor_reduce(bexp[:, 0], boh[:], AX.X, ALU.add))
            link(dve.tensor_scalar(bexp[:, 1], bexp[:, 0], float(E1 - 1), None, ALU.min))
            dve.tensor_copy(bexp_i[:], bexp[0:1, 1]).then_inc(s_be, 1)
            link(dve.tensor_tensor(boh[:], row("iota").unsqueeze(1).to_broadcast([P, NB, E1]),
                                   bexp[:, 1].unsqueeze(2).to_broadcast([P, NB, E1]), ALU.is_equal))
            dve.wait_ge(dma["small"], 5 * 16)
            for c in range(HC1):
                last = dve.tensor_tensor(b1w[:, :, c, :], boh[:], b1c[:, :, c].unsqueeze(1).to_broadcast([P, NB, E1]), ALU.mult)
            link(last)
            dve.tensor_reduce(b1s[:].rearrange("p b c -> p (b c)"), b1w.rearrange("p b c e -> p (b c) e"),
                              AX.X, ALU.add).then_inc(s_b1, 1)
            for u in range(2):
                dve.wait_ge(s_mT, T)
                dve.tensor_copy(maskT[:, u * 512:u * 512 + 512], ps[0:E1, 6 + u, :]).then_inc(s_mTe, 1)
            def tokens_lo(q):
                b0, b1 = 4 * q, min(4 * q + 4, NB)
                dve.wait_ge(s_bh, q + 1)
                dve.tensor_tensor(xsT[:, 1, b0 * P:b1 * P], ps[:, 6 + q % 2, 0:(b1 - b0) * P], xsT[:, 0, b0 * P:b1 * P],
                                  ALU.subtract).then_inc(s_bl, 1)

            for q in range(3):
                tokens_lo(q)
            for b in range(NB + 2):
                if b == 1:
                    tokens_lo(3)
                if b < NB:
                    dve.wait_ge(s_h1h, b + 1)
                    if b >= 4:
                        dve.wait_ge(s_y1, b - 3)
                    dve.tensor_tensor(hT[:, b % 4, 1, :], h32[:, b % 4, :], hT[:, b % 4, 0, :], ALU.subtract)\
                       .then_inc(s_h1l, 1)
                if b >= 2:
                    dve.wait_ge(s_y1, b - 1)
                    y = ps[:, 2 + b % 2, 0:2 * D].rearrange("p (v n) -> p n v", v=2)
                    dve.tensor_reduce(ys_rows[:, b - 2, :], y, AX.X, ALU.add).then_inc(s_ye, 1)
            dve.wait_ge(s_b2, 1)
            dve.scalar_tensor_tensor(out=x[:], in0=ps[:, 4:6, :].rearrange("p a (t d) -> p (a t) d", d=D),
                                     scalar=th[:, 3:4], in1=x[:], op0=ALU.mult, op1=ALU.add).then_inc(s_x, 1)
            for u in range(2):
                dve.wait_ge(s_yg[u], 16 * TB)
                dve.wait_ge(s_x, 5)
                xu = x[:, TB * u:TB * u + TB, :]
                dve.scalar_tensor_tensor(out=xu, in0=y_tok[:, TB * u:TB * u + TB, :], scalar=th[:, 3:4], in1=xu,
                                         op0=ALU.mult, op1=ALU.add).then_inc(s_x, 1)

        @block.gpsimd
        def _(pool):
            pool.memset(qs[:, :, :, 0, HD - 1:HD], 1.0).then_inc(s_ones, 1)
            pool.memset(qs[:, :, :, 1, HD - 1:HD], 0.0).then_inc(s_ones, 1)
            for v in (va, vc):
                pool.memset(v[:, 0, :, :, HD:HD + 1], 1.0).then_inc(s_ones, 1)
                pool.memset(v[:, 1, :, :, HD:HD + 1], 0.0).then_inc(s_ones, 1)

            pool.memset(zeros, 0.0).then_inc(s_zr, 1)

            def cast(dst, src):
                return pool.tensor_scalar(dst, src, 1.0, 0.0, ALU.mult, ALU.add)

            pool.wait_ge(dma["ident"], 16)
            cast(ident16[:], ident[:]).then_inc(s_cst, 1)
            cast(identb[:], ident[:]).then_inc(s_cst, 1)
            pool.wait_ge(s_chi, 1)
            pool.tensor_tensor(c16[:, 1, :], ctxT.rearrange("p a b -> p (a b)"), c16[:, 0, :],
                               ALU.subtract).then_inc(s_clo, 1)
            pool.wait_ge(s_wc, 1)
            pool.wait_ge(s_beta, 1)
            pool.tensor_tensor(heads(wkm), heads(wk), bc(co[:, 0, :], [P, NH, HD], 1), ALU.mult).then_inc(s_wkm, 1)
            pool.wait_ge(s_wkm, 1)
            pool.tensor_tensor(heads(wkm)[:, :, 0:HD - 1], heads(wkm)[:, :, 0:HD - 1],
                               heads(wkm)[:, :, HD - 1:HD].to_broadcast([P, NH, HD - 1]),
                               ALU.subtract).then_inc(s_wkm, 1)
            pool.wait_ge(dma["tri"], 16)
            cast(trib[:], tri).then_inc(s_cst, 1)
            pool.memset(onesb[:], 1.0).then_inc(s_cst, 1)
            pool.wait_ge(s_wc, 2)
            pool.tensor_tensor(heads(wq), heads(wq), bc(hmean[:, 1, :], [P, NH, HD], 2), ALU.add).then_inc(s_wc, 1)
            pool.wait_ge(s_wc, 3)
            pool.wait_ge(s_whi, 4)
            pool.tensor_tensor(wsp[:, 0, 1, :], wq, wsp[:, 0, 0, :], ALU.subtract).then_inc(s_clo, 1)
            pool.memset(km[:, :, :, 1, HD - 1:HD], 0.0).then_inc(s_ones, 1)
            for n in range(NJ + 2):
                if 0 <= n - 1 < NJ and JOBS[n - 1][0] == "kv":
                    c = JOBS[n - 1][1]
                    pool.wait_ge(s_km, 2 * (c + 1))
                    if c == 2:
                        pool.wait_ge(s_kt, NG)
                    cast(km[:, c % 2, :, 1, 0:HD - 1], km[:, c % 2, :, 0, 0:HD - 1]).then_inc(s_km2, 1)
                if 0 <= n - 2 < NJ and JOBS[n - 2][0] == "q":
                    t = JOBS[n - 2][1]
                    pool.wait_ge(s_qh, t + 1)
                    pool.tensor_tensor(qs[:, t, :, 1, 0:HD - 1], qn[:, t % 2, :, 0:HD - 1],
                                       qs[:, t, :, 0, 0:HD - 1], ALU.subtract).then_inc(s_ql, 1)
                if n in KTJOB:
                    g = KTJOB.index(n)
                    pool.wait_ge(s_kf, g + 1)
                    b, h = g // NG, G * (g % NG)
                    pool.wait_ge(s_kh, g + 1)
                    pool.tensor_tensor(kT[:, 1, b, h:h + G, :], kf[:, g % 2, :, :], kT[:, 0, b, h:h + G, :],
                                       ALU.subtract).then_inc(s_kl, 1)
            def beside0(g):
                if g == 2:
                    pool.wait_ge(s_whi, 5)
                    pool.tensor_tensor(wsp[:, 4, 1, :], wo, wsp[:, 4, 0, :], ALU.subtract).then_inc(s_clo, 1)
                if g == 3:
                    pool.wait_ge(s_tanh, 1)
                    pool.wait_ge(s_xn, T)
                    pool.tensor_scalar(obo[:, 0, :], row("bo"), th[:, 0:1], 0.0, ALU.mult, ALU.add).then_inc(s_bo, 1)
                    pool.wait_ge(s_bo, 1)
                    pool.tensor_tensor(x[:], x[:], obo[:, 0, :].unsqueeze(1).to_broadcast([P, T, D]),
                                       ALU.add).then_inc(s_bo, 1)
                if g == GT - 2:
                    pool.wait_ge(s_rs, 1)
                    pool.wait_ge(s_qt[0], 2 * GT)
                    normalised(pool, 0, osum[:, :, :, 0:HD], rsum, 0).then_inc(s_on, 1)
                    normalised(pool, 0, osum[:, :, :, 0:HD], rsum, 1).then_inc(s_onp, 1)

            attention_pool(pool, 0, beside0)
            project_out_pool(pool, 0, osum[:, :, :, 0:HD], rsum, 3)
            links = [0]

            def link(ins):
                links[0] += 1
                ins.then_inc(s_pool, 1)
                pool.wait_ge(s_pool, links[0])

            pool.wait_ge(dma["wgate"], 16)
            pool.wait_ge(dma["wdown"], 16)
            pool.wait_ge(s_qt[0], 2 * GT)
            wd_hi, wd_lo = (wds[:, w].rearrange("p c n -> p (c n)") for w in range(2))
            for w, hi, lo in ((wgf, wgs[:, 0, :], wgs[:, 1, :]), (wdf, wd_hi, wd_lo)):
                pool.tensor_scalar(hi, w, WS, 0.0, ALU.mult, ALU.add)
                link(pool.tensor_scalar(w, w, WS, 0.0, ALU.mult, ALU.add))
                pool.tensor_tensor(lo, w, hi, ALU.subtract).then_inc(s_wg, 1)
            pool.wait_ge(dma["fcw"], 16)
            pool.wait_ge(dma["small"], 5 * 16)
            cast(fms[:, 0, :], fm[:])
            link(cast(fcs[:, 0, :], fcf))
            pool.tensor_tensor(fms[:, 1, :], fm[:], fms[:, 0, :], ALU.subtract).then_inc(s_fms, 1)
            pool.tensor_tensor(fcs[:, 1, :], fcf, fcs[:, 0, :], ALU.subtract).then_inc(s_fms, 1)
            pool.wait_ge(s_pv[0], B * NH)
            for v in (va1, vc1):
                pool.memset(v[:, :, :, 0, FD:V1], 1.0).then_inc(s_v1, 1)
                pool.memset(v[:, :, :, 1:3, FD:V1], 0.0).then_inc(s_v1, 1)
            below = kT1[QM[1]:P, 0].bitcast(F32)
            pool.wait_ge(s_v1, 4)
            link(pool.memset(below, 0.0))
            pair_of_minus_ones = float(np.array([0xBF80BF80], np.uint32).view(np.float32)[0])
            pool.memset(below[0:2], pair_of_minus_ones).then_inc(s_m1, 1)
            pool.wait_ge(s_m1, 1)
            for t in range(T):
                if t in DVE_TILES:
                    continue
                pool.wait_ge(s_yw, t + 1)
                for half in (4, 2, 1):
                    link(pool.tensor_tensor(yw[:, t % 2, 0:half, :], yw[:, t % 2, 0:half, :],
                                            yw[:, t % 2, half:2 * half, :], ALU.add))
                pool.tensor_tensor(x[:, t, :], x[:, t, :], yw[:, t % 2, 0, :], ALU.add).then_inc(s_x0, 1)
            pool.wait_ge(s_xn, 2 * T + T)
            pool.tensor_scalar(obo[:, 1, :], row("fcb"), th[:, 1:2], 0.0, ALU.mult, ALU.add).then_inc(s_bo, 1)
            pool.wait_ge(s_bo, 3)
            pool.tensor_tensor(x[:], x[:], obo[:, 1, :].unsqueeze(1).to_broadcast([P, T, D]), ALU.add).then_inc(s_bo, 1)
            for b in range(B):
                ts = slice(TB * b, TB * b + TB)
                pool.wait_ge(s_fq, 2 * b + 2)
                cast(qs1[:, ts, :, 1, :], fq[:, ts]).then_inc(s_qp, 1)

            def weights_lo(e):
                pool.wait_ge(s_wh, e + 1)
                for v in range(2):
                    pool.tensor_tensor(w1s[:, e, 1, 512 * v:512 * v + 512], w1f[:, e % 2, v, :],
                                       w1s[:, e, 0, 512 * v:512 * v + 512], ALU.subtract).then_inc(s_wl, 1)

            def parts_summed(g):
                i, b, h = where(g, 0)
                pool.wait_ge(s_pve[1], G * (g + 1))
                o3 = osum1[:, TB * b:TB * b + TB, h:h + G]
                o1 = os1[:, TB * b:TB * b + TB, h:h + G]
                link(pool.tensor_tensor(o1, o3[:, :, :, 0:V1], o3[:, :, :, V1:2 * V1], ALU.add))
                pool.tensor_tensor(o1, o1, o3[:, :, :, 2 * V1:3 * V1], ALU.add).then_inc(s_os, 1)

            def beside(g):
                if g >= 2:
                    parts_summed(g - 2)
                if g < GT - 1:
                    weights_lo(g)

            attention_pool(pool, 1, beside)
            project_out_pool(pool, 1, os1[:, :, :, 0:FD], rsum, 1)
            weights_lo(E1 - 1)
            pool.wait_ge(s_sl, 1)
            pool.wait_ge(s_zs, 16)
            for t in range(T):
                pool.indirect_dma_start(out=xs_d, out_offset=bass.IndirectOffsetOnAxis(ap=slots_i[:, t:t + 1], axis=0),
                                        in_=xn[:, t, :], in_offset=None).then_inc(s_sc, 16)
            for b in range(NB):
                pool.wait_ge(s_h1, HC1 * (b + 1))
                if b >= 4:
                    pool.wait_ge(s_y1, b - 3)
                cast(hT[:, b % 4, 0, :], h32[:, b % 4, :]).then_inc(s_h1h, 1)
            pool.wait_ge(s_ys, 64)
            for t in range(T):
                pool.indirect_dma_start(out=y_tok[:, t, :], out_offset=None, in_=ys_d,
                                        in_offset=bass.IndirectOffsetOnAxis(ap=slots_i[:, t:t + 1], axis=0))\
                    .then_inc(s_yg[t // TB], 16)

        @block.scalar
        def _(act):
            links = [0]

            def link(ins):
                links[0] += 1
                ins.then_inc(s_act, 1)
                act.wait_ge(s_act, links[0])

            def rsqrt_first(y, v):
                link(act.activation(y, v, ACT.Ln))
                return act.activation(y, y, ACT.Exp, scale=-0.5)

            act.preload_act_table(ACT.Tanh)
            act.wait_ge(dma["rows"], 16)
            act.activation(th[:], rows[:, ROW["gx"][0]:ROW["gf"][1]], ACT.Tanh).then_inc(s_tanh, 1)
            act.preload_act_table_set("natural_log_exp_and_others")
            act.wait_ge(dma["ctx"], 16)
            act.activation(c16[:, 0, :], ctxT.rearrange("p a b -> p (a b)"), ACT.Copy).then_inc(s_chi, 1)
            act.wait_ge(s_wc, 1)
            act.activation(wsp[:, 1, 0, :], wk, ACT.Copy).then_inc(s_whi, 1)
            act.wait_ge(dma["wv"], 16)
            act.activation(wsp[:, 3, 0, :], wv, ACT.Copy).then_inc(s_whi, 1)
            act.wait_ge(s_wkm, 3)
            act.activation(wsp[:, 2, 0, :], wkm, ACT.Copy).then_inc(s_whi, 1)

            for n in range(NJ + 2):
                if n < NJ:
                    kind, i = JOBS[n]
                    what = "k" if kind == "kv" else "q"
                    if n >= 2:
                        act.wait_ge(s_ss, n - 1)
                    for half in range(2):
                        act.wait_ge(s_proj, 2 * PROJ.index((what, i)) + half + 1)
                        act.activation(sq[:, n % 2, half * 512:half * 512 + 512], pair_of(what, i)[:, half, :],
                                       ACT.Square).then_inc(s_sqr, 1)
                if 0 <= n - 1 < NJ:
                    kind, i = JOBS[n - 1]
                    act.wait_ge(s_ss, n)
                    st_ = ssk if kind == "kv" else ssq
                    rsqrt_first(st_[:, 1, i, :], st_[:, 0, i, :]).then_inc(s_ry, 1)
                if n < NJ and JOBS[n][0] == "kv":
                    c = JOBS[n][1]
                    act.wait_ge(s_proj, 2 * (PROJ.index(("v", c)) + 1))
                    v = vc if c % 2 else va
                    pv = pair_of("v", c).rearrange("p a (h d) -> p (a h) d", d=HD)
                    act.activation(v[:, 0, c // 2, :, 0:HD], pv, ACT.Copy).then_inc(s_vh, 1)
                if n == 0:
                    act.wait_ge(s_wc, 3)
                    act.activation(wsp[:, 0, 0, :], wq, ACT.Copy).then_inc(s_whi, 1)
                    act.wait_ge(s_lv, 1)
                    rsqrt_first(lnv[:, 1, :], lnv[:, 0, :]).then_inc(s_ly, 1)
                if n == 1:
                    ln_act(act, 0)
                if 0 <= n - 2 < NJ and JOBS[n - 2][0] == "q":
                    t = JOBS[n - 2][1]
                    act.wait_ge(s_qn, 2 * (t + 1))
                    act.activation(qs[:, t, :, 0, 0:HD - 1], qn[:, t % 2, :, 0:HD - 1], ACT.Copy).then_inc(s_qh, 1)
                if n in KTJOB:
                    g = KTJOB.index(n)
                    act.wait_ge(s_coc, 1)
                    act.wait_ge(s_kt, g + 1)
                    if g >= 2:
                        act.wait_ge(s_kl, g - 1)
                    act.activation(kf[:, g % 2, :, :].rearrange("p (a h) k -> p a (h k)", a=2),
                                   ps[:, 6:8, 0:2 * KW], ACT.Identity, bias=coc[:]).then_inc(s_kf, 1)
                    act.wait_ge(s_kf, g + 1)
                    b, h = g // NG, G * (g % NG)
                    if g == 0:
                        act.wait_ge(s_zs, 16)
                    act.activation(kT[:, 0, b, h:h + G, :], kf[:, g % 2, :, :], ACT.Copy).then_inc(s_kh, 1)
                if n == NJ - 2:
                    act.wait_ge(dma["wo"], 16)
                    act.activation(wsp[:, 4, 0, :], wo, ACT.Copy).then_inc(s_whi, 1)
            attention_act(act, 0)
            project_out_act(act, 0)

            def layernorm(k):
                act.wait_ge(s_lv, k + 1)
                rsqrt_first(lnv[:, 1, :], lnv[:, 0, :]).then_inc(s_ly, 1)
                ln_act(act, k)

            layernorm(1)
            act.preload_act_table(ACT.Silu)
            for c in range(2):
                act.wait_ge(s_hp, c + 1)
                act.activation(hs[:, c, :], ps[:, 2 * c:2 * c + 2, :].rearrange("p a b -> p (a b)"), ACT.Silu,
                               scale=1.0 / WS).then_inc(s_hs, 1)
                act.wait_ge(s_hs, c + 1)
                act.activation(hh0[:, c, 0, :], hs[:, c, :], ACT.Copy).then_inc(s_h0, 1)
            act.preload_act_table_set("natural_log_exp_and_others")
            gates_act(act, 0)
            act.wait_ge(s_zb, 1)
            act.activation(fk[:, :, :, 0:8], zk, ACT.Exp).then_inc(s_fk, 1)
            act.activation(fk[:, :, :, 8:16], zk, ACT.Exp, scale=-1.0).then_inc(s_fk, 1)
            act.wait_ge(s_fk, 2)
            for slot in (0, 2, 5):
                act.activation(ks[:, :, :, slot, :], fk, ACT.Copy).then_inc(s_ka, 1)
            act.wait_ge(s_kd, 1)
            for slot in (1, 3):
                act.activation(ks[:, :, :, slot, :], rk, ACT.Copy).then_inc(s_ka, 1)
            for g in range(GT):
                act.wait_ge(s_k1, g + 1)
                b, h = g // NG, G * (g % NG)
                act.activation(kT1[0:6 * FD, 0, b, h:h + G, :],
                               ps[:, 6 + g % 2, :].bitcast(BF16)[0:6 * FD, 0:G * KW].rearrange("p (h k) -> p h k", h=G),
                               ACT.Copy).then_inc(s_k1e, 1)
            layernorm(2)
            act.wait_ge(s_k1, GT)
            act.activation(qT[QM[1]:P].bitcast(F32).rearrange("p z j n -> p (z j n)").rearrange("p (a n) -> p a n", n=P),
                           ident[QM[1]:P].unsqueeze(1).to_broadcast([P - QM[1], 3 * G * N // 2 // P, P]),
                           ACT.Copy, scale=0.0).then_inc(s_m1, 1)
            for b in range(B):
                ts = slice(TB * b, TB * b + TB)
                act.wait_ge(s_zqb, b + 1)
                act.activation(fq[:, ts, :, 0:8], zq[:, ts], ACT.Exp).then_inc(s_fq, 1)
                act.activation(fq[:, ts, :, 8:16], zq[:, ts], ACT.Exp, scale=-1.0).then_inc(s_fq, 1)
                act.wait_ge(s_fq, 2 * b + 2)
                act.activation(qs1[:, ts, :, 0, :], fq[:, ts], ACT.Copy).then_inc(s_qa, 1)
                act.activation(qs1[:, ts, :, 4, :], fq[:, ts], ACT.Copy).then_inc(s_qa, 1)

            def weights_hi(e):
                act.wait_ge(dma_e[e % 2], 32 * (e // 2 + 1))
                act.activation(w1s[:, e, 0, :], w1f[:, e % 2].rearrange("p v n -> p (v n)"), ACT.Copy).then_inc(s_wh, 1)

            attention_act(act, 1, weights_hi)
            project_out_act(act, 1)
            layernorm(3)
            gates_act(act, 1)
            act.preload_act_table(ACT.Gelu)
            def tokens_hi(q):
                b0, b1 = 4 * q, min(4 * q + 4, NB)
                act.wait_ge(s_bt, q + 1)
                act.activation(xsT[:, 0, b0 * P:b1 * P], ps[:, 6 + q % 2, 0:(b1 - b0) * P], ACT.Copy).then_inc(s_bh, 1)

            tokens_hi(0)
            tokens_hi(1)
            act.wait_ge(s_b1, 1)
            for b in range(NB):
                act.wait_ge(s_h1p, b + 1)
                if b >= 4:
                    act.wait_ge(s_h1l, b - 3)
                for c in range(HC1):
                    act.activation(h32[:, b % 4, c * P:(c + 1) * P], ps[:, b % 2, c * P:(c + 1) * P], ACT.Gelu,
                                   bias=b1s[:, b, c:c + 1]).then_inc(s_h1, 1)
                if b < 2:
                    tokens_hi(b + 2)

        @block.tensor
        def _(pe):
            pe.wait_ge(dma["ident"], 16)
            pe.wait_ge(s_beta, 1)
            pe.transpose(ps[:, 6, 0:P], co[:, 3:5, :].rearrange("p a d -> p (a d)"), ident[:]).then_inc(s_betaT, 1)

            def project(n, xs, k):
                for half in range(2):
                    banks_free(n - 3, half)
                    for i, (a, w) in enumerate(((0, 0), (0, 1), (1, 0))):
                        last = pe.matmul(pair(n)[:, half, :], xs[a], wsp[:, k, w, half * 512:half * 512 + 512],
                                         start=(i == 0), stop=(i == 2))
                    last.then_inc(s_proj, 1)

            def keys_transposed(g):
                b, h0 = g // NG, G * (g % NG)
                if g == 0:
                    pe.wait_ge(s_ones, 7)
                    pe.wait_ge(s_xlo, 2)
                else:
                    pe.wait_ge(s_kf, g)
                pe.wait_ge(s_km2, 2 * b + 2)
                for j in range(G):
                    for c, (w, at) in enumerate(((KA, 0), (KCP, KA))):
                        o = (j % 2) * KW + at
                        last = pe.transpose(ps[:, 6 + j // 2, o:o + w],
                                            km[0:w, c, h0 + j].rearrange("p a d -> p (a d)"), ident[0:w, 0:w])
                last.then_inc(s_kt, 1)

            def banks_free(n, half):
                if n < 0:
                    return
                what, i = PROJ[n]
                if what == "k":
                    pe.wait_ge(s_sqr, 2 * job_of(what, i) + half + 1)
                elif what == "km":
                    pe.wait_ge(s_km, 2 * i + half + 1)
                elif what == "v":
                    pe.wait_ge(s_vl, i + 1)
                else:
                    pe.wait_ge(s_qn, 2 * i + half + 1)

            pe.wait_ge(s_chi, 1)
            for n, (what, i) in enumerate(PROJ):
                if n == 0:
                    pe.wait_ge(s_wlo, 1)
                    pe.wait_ge(s_clo, 1)
                if (what, i) == ("km", 0):
                    pe.wait_ge(s_wlo, 3)
                if (what, i) == ("v", 0):
                    pe.wait_ge(s_wlo, 2)
                if (what, i) == ("q", 0):
                    pe.wait_ge(s_xlo, 1)
                    pe.wait_ge(s_clo, 2)
                if (what, i) == ("q", TB):
                    pe.wait_ge(s_xlo, 2)
                if what == "q":
                    project(n, [xh[:, j, i * P:i * P + P] for j in range(2)], 0)
                else:
                    project(n, [c16[:, j, i * P:i * P + P] for j in range(2)], {"k": 1, "km": 2, "v": 3}[what])
                if (what, i) == ("v", 1):
                    pe.wait_ge(s_coc, 1)
                    ln_pe(pe, 0)
                if what in "qv" and job_of(what, i) in KTJOB:
                    keys_transposed(KTJOB.index(job_of(what, i)))
            keys_transposed(GT - 1)
            pe.wait_ge(s_qn, 2 * T)
            pe.wait_ge(s_kf, GT)
            pe.wait_ge(s_ones, 6)
            pe.wait_ge(s_cst, 2)
            attention_pe(pe, 0)
            pe.wait_ge(s_clo, 3)
            project_out_pe(pe, 0, lambda w, c: wsp[:, 4, w, c * P:(c + 1) * P])

            HILO = ((0, 0), (0, 1), (1, 0))

            ln_pe(pe, 1)
            pe.wait_ge(s_xlo, 4)
            pe.wait_ge(s_wg, 1)
            for c in range(2):
                for u in range(2):
                    for i, (w, a) in enumerate(HILO):
                        last = pe.matmul(ps[:, 2 * c + u, :], wgs[:, w, c * P:(c + 1) * P],
                                         xh[:, a, u * 512:u * 512 + 512], start=(i == 0), stop=(i == 2))
                last.then_inc(s_hp, 1)
            router_pe(pe, 0)
            def positions():
                pe.wait_ge(s_mk, 1)
                for t in range(T):
                    for u in range(t + 1):
                        last = pe.matmul(ps[:, 4, t * 8:t * 8 + 8], trib[:] if u == t else onesb[:], maskb[:, u, :],
                                         start=(u == 0), stop=(u == t))
                last.then_inc(s_cum, 1)
                pe.wait_ge(s_fms, 1)
                for c in range(2 * B):
                    for i, (a, w) in enumerate(HILO):
                        last = pe.matmul(ps[:, 5, c * P:(c + 1) * P], c16[:, a, c * P:(c + 1) * P], fms[:, w, :],
                                         start=(i == 0), stop=(i == 2))
                last.then_inc(s_zk, 1)

            pe.wait_ge(s_l0, 2)
            pe.wait_ge(s_wg, 2)
            for t in range(T):
                if t >= 2:
                    pe.wait_ge(s_yw, t - 1)
                for u in range(2):
                    n = 0
                    for c in range(2):
                        for a, w in HILO:
                            last = pe.matmul(ps[:, 2 * (t % 2) + u, :], hh0[:, c, a, t * P:(t + 1) * P],
                                             wds[:, w, c, u * 512:u * 512 + 512], start=(n == 0), stop=(n == 5))
                            n += 1
                last.then_inc(s_y0, 1)
                if t == 0:
                    positions()
            for g in range(GT):
                if g == 0:
                    pe.wait_ge(s_ka, 5)
                    pe.wait_ge(s_kd, 2)
                if g >= 2:
                    pe.wait_ge(s_k1e, g - 1)
                o = ps[:, 6 + g % 2, :].bitcast(BF16)
                for j in range(G):
                    for c, (w, at) in enumerate(((KA, 0), (KCP, KA))):
                        last = pe.transpose(o[0:6 * FD, j * KW + at:j * KW + at + w],
                                            ks[0:w, 2 * (g // NG) + c, G * (g % NG) + j].rearrange("p a d -> p (a d)"),
                                            identb[0:w, 0:w])
                last.then_inc(s_k1, 1)
            pe.wait_ge(s_k1e, GT)
            ln_pe(pe, 2)
            pe.wait_ge(s_xlo, 6)
            for t in range(T):
                for i, (a, w) in enumerate(HILO):
                    last = pe.matmul(ps[:, t // 4, (t % 4) * P:(t % 4 + 1) * P], xh[:, a, t * P:(t + 1) * P], fms[:, w, :],
                                     start=(i == 0), stop=(i == 2))
            last.then_inc(s_zq, 1)
            pe.wait_ge(s_zqb, B)
            pe.wait_ge(s_m1, 2)
            pe.wait_ge(s_kd, 3)
            attention_pe(pe, 1)
            project_out_pe(pe, 1, lambda w, c: fcs[:, w, c * P:(c + 1) * P])
            ln_pe(pe, 3)
            pe.wait_ge(dma["small"], 5 * 16)
            router_pe(pe, 1)
            pe.wait_ge(s_mk, 2)
            for t in range(T):
                for u in range(t + 1):
                    last = pe.matmul(ps[:, 4, t * 8:t * 8 + 8], trib[:] if u == t else onesb[:], maskb[:, u, :],
                                     start=(u == 0), stop=(u == t))
            for u in range(T):
                last = pe.matmul(ps[:, 4, T * 8:T * 8 + 8], onesb[:], maskb[:, u, :], start=(u == 0), stop=(u == T - 1))
            last.then_inc(s_cum, 1)
            for t in range(T):
                pe.transpose(ps[0:E1, 6 + t // 4, (t % 4) * P:(t % 4 + 1) * P], gt[:, MA, t, :], ident[:]).then_inc(s_mT, 1)
            pe.wait_ge(s_be, 1)
            expert = [pe.value_load(bexp_i[0:1, b:b + 1], min_val=0, max_val=E1 - 1) for b in range(NB)]

            def block_in(q):
                pe.wait_ge(s_xl[q], 16)
                if q >= 2:
                    pe.wait_ge(s_bl, q - 1)
                for b in range(4 * q, min(4 * q + 4, NB)):
                    last = pe.transpose(ps[:, 6 + q % 2, (b % 4) * P:(b % 4 + 1) * P], xs_rows[:, b, :], ident[:])
                last.then_inc(s_bt, 1)

            def block_hidden(b):
                if b >= 2:
                    pe.wait_ge(s_h1, HC1 * (b - 1))
                for c in range(HC1):
                    for i, (v, a) in enumerate(HILO):
                        w = w1s[:, bass.ds(expert[b], 1), v, c * P:(c + 1) * P].rearrange("p a n -> p (a n)")
                        last = pe.matmul(ps[:, b % 2, c * P:(c + 1) * P], w, xsT[:, a, b * P:(b + 1) * P],
                                         start=(i == 0), stop=(i == 2))
                last.then_inc(s_h1p, 1)

            def block_output(b):
                pe.wait_ge(s_h1l, b + 1)
                if b >= 2:
                    pe.wait_ge(s_ye, b - 1)
                y = ps[:, 2 + b % 2, 0:2 * D].rearrange("p (v n) -> p v n", v=2)
                for c in range(HC1):
                    w = w1s[:, bass.ds(expert[b], 1), :, 512 + c * P:512 + (c + 1) * P].rearrange("p a v n -> p (a v) n")
                    for a in ((0, 1) if c == 0 else (1, 0)):
                        last = pe.matmul(y[:, 0:2 - a, :], hT[:, b % 4, a, c * P:(c + 1) * P], w[:, 0:2 - a, :],
                                         start=(c == 0 and a == 0), stop=(c == HC1 - 1 and a == 0))
                last.then_inc(s_y1, 1)

            pe.wait_ge(s_wl, 2 * E1)
            pe.wait_ge(s_mTe, 2)
            block_in(0)
            block_in(1)
            for b in range(NB + 2):
                if b < NB:
                    if b % 4 == 0:
                        pe.wait_ge(s_bl, b // 4 + 1)
                    block_hidden(b)
                if b < 2:
                    block_in(b + 2)
                if b >= 2:
                    block_output(b - 2)
            pe.wait_ge(s_mTe, 2)
            pe.wait_ge(dma["small"], 5 * 16)
            for t in range(T):
                last = pe.matmul(ps[:, 4 + t // 4, (t % 4) * P:(t % 4 + 1) * P], maskT[:, t * P:(t + 1) * P], b2s[:],
                                 start=True, stop=True)
            last.then_inc(s_b2, 1)


NAMES = ("rows", "ident", "tri", "ctx", "wq", "wk", "wv", "wo", "fm", "wgate", "wdown", "wrouter",
         "fcw", "wr", "w1", "b1", "w2", "b2")


def laid_out(i):
    f = {k: np.asarray(v) for k, v in i.items()}
    row = np.zeros((1, ROWS), np.float32)
    for name, v in (("bo", f["L0_xattn_bo"]), ("gq", f["L0_xattn_q_gamma"]), ("bq", f["L0_xattn_q_beta"]),
                    ("gk", f["L0_xattn_k_gamma"]), ("bk", f["L0_xattn_k_beta"]), ("gx", f["g_xattn"]),
                    ("gf", f["g_ffn"]), ("fmb", np.tile(f["L1_xattn_fm_b"], NH)), ("fcb", f["L1_xattn_fc_b"]),
                    ("br", f["L1_ffn_br"]), ("iota", np.arange(8)), ("k128", P * np.arange(8)),
                    ("before", np.tril(np.ones((8, 8)), -1).reshape(-1)), ("block", np.arange(NB))):
        row[0, ROW[name][0]:ROW[name][1]] = v
    c = f["ctx_1024"]
    tiles = []
    for b in range(B):
        tiles.append(c[b, :KA])
        tiles += [np.concatenate([c[b, KA:M], c[b, :KCP - KC]])] * G
    fm = np.zeros((NH, 8, NH, 8), np.float32)
    for h in range(NH):
        fm[h, :, h, :] = f["L1_xattn_fm_w"].T
    return {
        "x": f["x"].reshape(B * N, D), "rows": row, "ident": np.eye(P, dtype=np.float32),
        "tri": np.triu(np.ones((P, P), np.float32)),
        "ctx": np.concatenate(tiles).T.reshape(D, 2 * B, P),
        "wq": f["L0_xattn_Wq"], "wk": f["L0_xattn_Wk"], "wv": f["L0_xattn_Wv"], "wo": f["L0_xattn_Wo"],
        "fm": fm.reshape(P, P), "wgate": f["L0_ffn_w_gate"].T,
        "wdown": f["L0_ffn_w_down"].transpose(2, 0, 1).reshape(2, P, E0 * D).transpose(1, 0, 2),
        "wrouter": f["L0_ffn_w_router"].T, "fcw": f["L1_xattn_fc_w"].T.reshape(2, P, D).transpose(1, 0, 2),
        "wr": f["L1_ffn_Wr"], "w1": f["L1_ffn_W1"], "b1": f["L1_ffn_b1"].reshape(E1, HC1, P).transpose(2, 0, 1),
        "w2": f["L1_ffn_W2"].reshape(E1, HC1, P, D).transpose(0, 2, 1, 3), "b2": f["L1_ffn_b2"],
    }


def kernel(**inputs):
    from concourse import bacc
    from concourse.bass_utils import run_bass_kernel_spmd

    nc = bacc.Bacc("TRN2", target_bir_lowering=False, num_devices=1)
    arrays = {k: np.ascontiguousarray(v) for k, v in laid_out(inputs).items()}
    aps = {k: nc.dram_tensor(k + "_in", v.shape, mybir.dt.from_np(v.dtype), kind="ExternalInput").ap()
           for k, v in arrays.items()}
    out = nc.dram_tensor("out", (B * N, D), F32, kind="ExternalOutput").ap()
    build(nc, aps["x"], out, *[aps[k] for k in NAMES])
    r = run_bass_kernel_spmd(nc, [{k + "_in": v for k, v in arrays.items()}], core_ids=[0])
    return r.results[0]["out"].reshape(B, N, D)
```
